# Optimizing a Trainium2 kernel written in Bass

```python
import numpy as np
import jax
import jax.numpy as jnp

def _softmax(x, axis=-1):
    return jax.nn.softmax(x, axis=axis)

def _gelu(x):
    return jax.nn.gelu(x, approximate=True)

def _silu(x):
    return jax.nn.silu(x)

def _sigmoid(x):
    return jax.nn.sigmoid(x)

def _layernorm(x, axis=-1, eps=1e-05):
    m = jnp.mean(x, axis=axis, keepdims=True)
    v = jnp.var(x, axis=axis, keepdims=True)
    return (x - m) / jnp.sqrt(v + eps)

def _scatter_add(tgt, idx, src, axis=0):
    return tgt.at[idx].add(src)

def _segment_sum(src, seg, n):
    return jax.ops.segment_sum(src, seg, n)
kernel_name = 'mk_vit_tower_d2_tok_img256_r4_578780'

def setup_inputs(seed: int=0):
    np.random.seed(seed)
    _w = jnp.asarray

    def _rec_inputs():
        import jax
        import jax.numpy as jnp
        _rk = jax.random.key(seed)
        x = 7.22013e-05 + 1.00017 * jax.random.normal(jax.random.fold_in(_rk, 1), (4, 1, 1024, 64), jnp.float32)
        return x
    x = _rec_inputs()

    def _L0_tok_setup():
        import jax, jax.numpy as jnp
        import numpy as np
        T, D_IN, D_INT, D_OUT, B = (1024, 64, 64, 64, 8)
        key = jax.random.key(seed)
        ks = jax.random.split(key, 12)
        s_in = 1.0 / np.sqrt(D_IN)
        s_int = 1.0 / np.sqrt(D_INT)
        return {'x_batched': jax.random.normal(ks[0], (B, 1, T, D_IN), dtype=jnp.float32), 'd_gamma_batched': jax.random.uniform(ks[1], (T, T), dtype=jnp.float32), 'Wq': jax.random.uniform(ks[2], (D_IN, D_INT), jnp.float32, -s_in, s_in), 'bq': jax.random.uniform(ks[3], (D_INT,), jnp.float32, -s_in, s_in), 'Wk': jax.random.uniform(ks[4], (D_IN, D_INT), jnp.float32, -s_in, s_in), 'bk': jax.random.uniform(ks[5], (D_INT,), jnp.float32, -s_in, s_in), 'Wv': jax.random.uniform(ks[6], (D_IN, D_INT), jnp.float32, -s_in, s_in), 'bv': jax.random.uniform(ks[7], (D_INT,), jnp.float32, -s_in, s_in), 'Wo': jax.random.uniform(ks[8], (D_INT, D_OUT), jnp.float32, -s_int, s_int), 'bo': jax.random.uniform(ks[9], (D_OUT,), jnp.float32, -s_int, s_int), 'prelu_a': jnp.float32(0.25)}
    _L0_tok_all = _L0_tok_setup()
    _L0_tok_in = {k: v for k, v in _L0_tok_all.items() if k in ('d_gamma_batched', 'Wq', 'bq', 'Wk', 'bk', 'Wv', 'bv', 'Wo', 'bo', 'prelu_a')}
    del _L0_tok_all

    def _L0_attn_setup():
        import jax, jax.numpy as jnp
        import numpy as np
        NUM_HEADS = 4
        LN_EPS = 1e-05

        def positional_encoding(length, d_model):
            pos = jnp.arange(length, dtype=jnp.float32)[:, None]
            div = jnp.exp(jnp.arange(0, d_model, 2, dtype=jnp.float32) * (-np.log(10000.0) / d_model))
            pe = jnp.zeros((length, d_model), dtype=jnp.float32)
            pe = pe.at[:, 0::2].set(jnp.sin(pos * div))
            pe = pe.at[:, 1::2].set(jnp.cos(pos * div))
            return pe

        def rel_shift(pos_score):
            B, H, S, _ = pos_score.shape
            padded = jnp.pad(pos_score, ((0, 0), (0, 0), (0, 0), (1, 0)))
            padded = padded.reshape(B, H, S + 1, S)
            return padded[:, :, 1:].reshape(B, H, S, S)
        key = jax.random.key(seed)
        ks = jax.random.split(key, 8)
        B, S, D, H = (8, 512, 64, NUM_HEADS)
        dh = D // H
        s = 0.02
        return {'inputs': jax.random.normal(ks[0], (B, S, D), dtype=jnp.float32), 'ln_gamma': jnp.ones((D,), jnp.float32), 'ln_beta': jnp.zeros((D,), jnp.float32), 'Wq': jax.random.normal(ks[1], (D, D), jnp.float32) * s, 'bq': jnp.zeros((D,), jnp.float32), 'Wk': jax.random.normal(ks[2], (D, D), jnp.float32) * s, 'bk': jnp.zeros((D,), jnp.float32), 'Wv': jax.random.normal(ks[3], (D, D), jnp.float32) * s, 'bv': jnp.zeros((D,), jnp.float32), 'Wpos': jax.random.normal(ks[4], (D, D), jnp.float32) * s, 'u_bias': jax.random.normal(ks[5], (H, dh), jnp.float32) * s, 'v_bias': jax.random.normal(ks[6], (H, dh), jnp.float32) * s, 'Wout': jax.random.normal(ks[7], (D, D), jnp.float32) * s, 'bout': jnp.zeros((D,), jnp.float32)}
    _L0_attn_all = _L0_attn_setup()
    _L0_attn_in = {k: v for k, v in _L0_attn_all.items() if k in ('ln_gamma', 'ln_beta', 'Wq', 'bq', 'Wk', 'bk', 'Wv', 'bv', 'Wpos', 'u_bias', 'v_bias', 'Wout', 'bout')}
    del _L0_attn_all

    def _L0_ffn_setup():
        import jax, jax.numpy as jnp
        import numpy as np
        B, T, C = (64, 96, 64)
        NH, NKV = (4, 2)
        HD = C // NH
        NREP = NH // NKV
        NE, TOPK = (8, 2)
        HID = int(8 / 3 * C)
        EPS_RMS = 1e-06

        def _rope_tables(t_len):
            inv_freq = 1.0 / 10000.0 ** (np.arange(0, HD, 2, dtype=np.float32) / HD)
            t = np.arange(t_len, dtype=np.float32)
            freqs = np.outer(t, inv_freq)
            emb = np.concatenate([freqs, freqs], axis=-1)
            return (jnp.asarray(np.cos(emb)), jnp.asarray(np.sin(emb)))

        def _rotate_half(x):
            h = x.shape[-1] // 2
            return jnp.concatenate([-x[..., h:], x[..., :h]], axis=-1)

        def _rmsnorm(v, w):
            return v * jax.lax.rsqrt(jnp.mean(v * v, axis=-1, keepdims=True) + EPS_RMS) * w
        key = jax.random.key(seed)
        ks = jax.random.split(key, 10)
        s = lambda k, shape: jax.random.normal(k, shape, jnp.float32) * 0.02
        return {'x': jax.random.normal(ks[0], (B, T, C), jnp.float32), 'ln1_w': jnp.ones((C,), jnp.float32), 'ln2_w': jnp.ones((C,), jnp.float32), 'wq': s(ks[1], (NH * HD, C)), 'wk': s(ks[2], (NKV * HD, C)), 'wv': s(ks[3], (NKV * HD, C)), 'wo': s(ks[4], (C, C)), 'router_w': s(ks[5], (NE, C)), 'w1': s(ks[6], (NE, HID, C)), 'w2': s(ks[7], (NE, C, HID)), 'w3': s(ks[8], (NE, HID, C))}
    _L0_ffn_all = _L0_ffn_setup()
    _L0_ffn_in = {k: v for k, v in _L0_ffn_all.items() if k in ('ln1_w', 'ln2_w', 'wq', 'wk', 'wv', 'wo', 'router_w', 'w1', 'w2', 'w3')}
    del _L0_ffn_all

    def _L1_attn_setup():
        import jax, jax.numpy as jnp
        import numpy as np
        B, N, D, TOP_K = (4, 1024, 64, 64)
        EPS = 1e-12
        key = jax.random.key(seed)
        kx, kw, kb = jax.random.split(key, 3)
        x = jax.random.normal(kx, (B, N, D), dtype=jnp.float32)
        lim = 1.0 / np.sqrt(D)
        W = jax.random.uniform(kw, (D, D), dtype=jnp.float32, minval=-lim, maxval=lim)
        b = jax.random.uniform(kb, (D,), dtype=jnp.float32, minval=-lim, maxval=lim)
        return {'x': x, 'W': W, 'b': b}
    _L1_attn_all = _L1_attn_setup()
    _L1_attn_in = {k: v for k, v in _L1_attn_all.items() if k in ('W', 'b')}
    del _L1_attn_all

    def _L1_ffn_setup():
        import jax, jax.numpy as jnp
        import numpy as np
        TOP_K = 2
        key = jax.random.key(seed)
        ks = jax.random.split(key, 4)
        B, L, D, H, E = (8, 1024, 64, 256, 8)
        s = 0.02
        return {'x': jax.random.normal(ks[0], (B, L, D), jnp.float32), 'Wg': jax.random.normal(ks[1], (D, E), jnp.float32) * s, 'bg': jnp.zeros((E,), jnp.float32), 'W1': jax.random.normal(ks[2], (E, D, H), jnp.float32) * s, 'b1': jnp.zeros((E, H), jnp.float32), 'W2': jax.random.normal(ks[3], (E, H, D), jnp.float32) * s, 'b2': jnp.zeros((E, D), jnp.float32)}
    _L1_ffn_all = _L1_ffn_setup()
    _L1_ffn_in = {k: v for k, v in _L1_ffn_all.items() if k in ('Wg', 'bg', 'W1', 'b1', 'W2', 'b2')}
    del _L1_ffn_all
    return {'x': x, 'L0_tok_d_gamma_batched': _L0_tok_in['d_gamma_batched'], 'L0_tok_Wq': _L0_tok_in['Wq'], 'L0_tok_bq': _L0_tok_in['bq'], 'L0_tok_Wk': _L0_tok_in['Wk'], 'L0_tok_bk': _L0_tok_in['bk'], 'L0_tok_Wv': _L0_tok_in['Wv'], 'L0_tok_bv': _L0_tok_in['bv'], 'L0_tok_Wo': _L0_tok_in['Wo'], 'L0_tok_bo': _L0_tok_in['bo'], 'L0_tok_prelu_a': _L0_tok_in['prelu_a'], 'L0_attn_ln_gamma': _L0_attn_in['ln_gamma'], 'L0_attn_ln_beta': _L0_attn_in['ln_beta'], 'L0_attn_Wq': _L0_attn_in['Wq'], 'L0_attn_bq': _L0_attn_in['bq'], 'L0_attn_Wk': _L0_attn_in['Wk'], 'L0_attn_bk': _L0_attn_in['bk'], 'L0_attn_Wv': _L0_attn_in['Wv'], 'L0_attn_bv': _L0_attn_in['bv'], 'L0_attn_Wpos': _L0_attn_in['Wpos'], 'L0_attn_u_bias': _L0_attn_in['u_bias'], 'L0_attn_v_bias': _L0_attn_in['v_bias'], 'L0_attn_Wout': _L0_attn_in['Wout'], 'L0_attn_bout': _L0_attn_in['bout'], 'L0_ffn_ln1_w': _L0_ffn_in['ln1_w'], 'L0_ffn_ln2_w': _L0_ffn_in['ln2_w'], 'L0_ffn_wq': _L0_ffn_in['wq'], 'L0_ffn_wk': _L0_ffn_in['wk'], 'L0_ffn_wv': _L0_ffn_in['wv'], 'L0_ffn_wo': _L0_ffn_in['wo'], 'L0_ffn_router_w': _L0_ffn_in['router_w'], 'L0_ffn_w1': _L0_ffn_in['w1'], 'L0_ffn_w2': _L0_ffn_in['w2'], 'L0_ffn_w3': _L0_ffn_in['w3'], 'L1_attn_W': _L1_attn_in['W'], 'L1_attn_b': _L1_attn_in['b'], 'L1_ffn_Wg': _L1_ffn_in['Wg'], 'L1_ffn_bg': _L1_ffn_in['bg'], 'L1_ffn_W1': _L1_ffn_in['W1'], 'L1_ffn_b1': _L1_ffn_in['b1'], 'L1_ffn_W2': _L1_ffn_in['W2'], 'L1_ffn_b2': _L1_ffn_in['b2']}

def reference(x, L0_tok_d_gamma_batched, L0_tok_Wq, L0_tok_bq, L0_tok_Wk, L0_tok_bk, L0_tok_Wv, L0_tok_bv, L0_tok_Wo, L0_tok_bo, L0_tok_prelu_a, L0_attn_ln_gamma, L0_attn_ln_beta, L0_attn_Wq, L0_attn_bq, L0_attn_Wk, L0_attn_bk, L0_attn_Wv, L0_attn_bv, L0_attn_Wpos, L0_attn_u_bias, L0_attn_v_bias, L0_attn_Wout, L0_attn_bout, L0_ffn_ln1_w, L0_ffn_ln2_w, L0_ffn_wq, L0_ffn_wk, L0_ffn_wv, L0_ffn_wo, L0_ffn_router_w, L0_ffn_w1, L0_ffn_w2, L0_ffn_w3, L1_attn_W, L1_attn_b, L1_ffn_Wg, L1_ffn_bg, L1_ffn_W1, L1_ffn_b1, L1_ffn_W2, L1_ffn_b2):
    import jax
    import jax.numpy as jnp

    def _L0_tok_ref(x_batched, d_gamma_batched, Wq, bq, Wk, bk, Wv, bv, Wo, bo, prelu_a):
        import jax, jax.numpy as jnp
        import numpy as np
        T, D_IN, D_INT, D_OUT, B = (1024, 64, 64, 64, 8)
        x = x_batched.reshape(x_batched.shape[0], T, D_IN)
        q = x @ Wq + bq
        k = x @ Wk + bk
        v = x @ Wv + bv
        scores = jnp.einsum('btd,bsd->bts', q, k)
        retained = jnp.einsum('bts,bsd->btd', d_gamma_batched * scores, v)
        y = retained @ Wo + bo
        out = jnp.where(y >= 0, y, prelu_a * y)
        return out

    def _L0_attn_ref(inputs, ln_gamma, ln_beta, Wq, bq, Wk, bk, Wv, bv, Wpos, u_bias, v_bias, Wout, bout):
        import jax, jax.numpy as jnp
        import numpy as np
        NUM_HEADS = 4
        LN_EPS = 1e-05

        def positional_encoding(length, d_model):
            pos = jnp.arange(length, dtype=jnp.float32)[:, None]
            div = jnp.exp(jnp.arange(0, d_model, 2, dtype=jnp.float32) * (-np.log(10000.0) / d_model))
            pe = jnp.zeros((length, d_model), dtype=jnp.float32)
            pe = pe.at[:, 0::2].set(jnp.sin(pos * div))
            pe = pe.at[:, 1::2].set(jnp.cos(pos * div))
            return pe

        def rel_shift(pos_score):
            B, H, S, _ = pos_score.shape
            padded = jnp.pad(pos_score, ((0, 0), (0, 0), (0, 0), (1, 0)))
            padded = padded.reshape(B, H, S + 1, S)
            return padded[:, :, 1:].reshape(B, H, S, S)
        B, S, D = inputs.shape
        H = NUM_HEADS
        dh = D // H
        mu = jnp.mean(inputs, axis=-1, keepdims=True)
        var = jnp.mean(jnp.square(inputs - mu), axis=-1, keepdims=True)
        x = (inputs - mu) / jnp.sqrt(var + LN_EPS) * ln_gamma + ln_beta
        pe = positional_encoding(S, D)
        q = (x @ Wq + bq).reshape(B, S, H, dh)
        k = (x @ Wk + bk).reshape(B, S, H, dh)
        v = (x @ Wv + bv).reshape(B, S, H, dh)
        p = (pe @ Wpos).reshape(S, H, dh)
        content_score = jnp.einsum('bshd,bthd->bhst', q + u_bias, k)
        pos_score = jnp.einsum('bshd,thd->bhst', q + v_bias, p)
        pos_score = rel_shift(pos_score)
        score = (content_score + pos_score) / np.sqrt(D).astype(np.float32)
        attn = jax.nn.softmax(score, axis=-1)
        ctx = jnp.einsum('bhst,bthd->bshd', attn, v).reshape(B, S, D)
        return ctx @ Wout + bout

    def _L0_ffn_ref(x, ln1_w, ln2_w, wq, wk, wv, wo, router_w, w1, w2, w3):
        import jax, jax.numpy as jnp
        import numpy as np
        B, T, C = (64, 96, 64)
        NH, NKV = (4, 2)
        HD = C // NH
        NREP = NH // NKV
        NE, TOPK = (8, 2)
        HID = int(8 / 3 * C)
        EPS_RMS = 1e-06

        def _rope_tables(t_len):
            inv_freq = 1.0 / 10000.0 ** (np.arange(0, HD, 2, dtype=np.float32) / HD)
            t = np.arange(t_len, dtype=np.float32)
            freqs = np.outer(t, inv_freq)
            emb = np.concatenate([freqs, freqs], axis=-1)
            return (jnp.asarray(np.cos(emb)), jnp.asarray(np.sin(emb)))

        def _rotate_half(x):
            h = x.shape[-1] // 2
            return jnp.concatenate([-x[..., h:], x[..., :h]], axis=-1)

        def _rmsnorm(v, w):
            return v * jax.lax.rsqrt(jnp.mean(v * v, axis=-1, keepdims=True) + EPS_RMS) * w
        Bx, Tx, Cx = x.shape
        h = _rmsnorm(x, ln1_w)
        q = (h @ wq.T).reshape(Bx, Tx, NH, HD).transpose(0, 2, 1, 3)
        k = (h @ wk.T).reshape(Bx, Tx, NKV, HD).transpose(0, 2, 1, 3)
        v = (h @ wv.T).reshape(Bx, Tx, NKV, HD).transpose(0, 2, 1, 3)
        cos, sin = _rope_tables(Tx)
        cos, sin = (cos[None, None], sin[None, None])
        q = q * cos + _rotate_half(q) * sin
        k = k * cos + _rotate_half(k) * sin
        k = jnp.repeat(k, NREP, axis=1)
        v = jnp.repeat(v, NREP, axis=1)
        scores = jnp.einsum('bhtd,bhsd->bhts', q, k) / jnp.sqrt(jnp.float32(HD))
        causal = jnp.tril(jnp.ones((Tx, Tx), dtype=bool))
        scores = jnp.where(causal[None, None], scores, jnp.float32(-1e+30))
        att = jax.nn.softmax(scores, axis=-1)
        y = jnp.einsum('bhts,bhsd->bhtd', att, v).transpose(0, 2, 1, 3).reshape(Bx, Tx, Cx)
        x = x + y @ wo.T
        flat = _rmsnorm(x, ln2_w).reshape(-1, Cx)
        probs = jax.nn.softmax(flat @ router_w.T, axis=-1)
        tp, ti = jax.lax.top_k(probs, TOPK)
        tp = tp / (jnp.sum(tp, axis=-1, keepdims=True) + 1e-09)
        weights = jnp.sum(tp[..., None] * jax.nn.one_hot(ti, NE, dtype=flat.dtype), axis=1)
        out = jnp.zeros_like(flat)
        for e in range(NE):
            hh = jax.nn.silu(flat @ w1[e].T) * (flat @ w3[e].T)
            out = out + weights[:, e:e + 1] * (hh @ w2[e].T)
        return x + out.reshape(Bx, Tx, Cx)

    def _L1_attn_ref(x, W, b):
        import jax, jax.numpy as jnp
        import numpy as np
        B, N, D, TOP_K = (4, 1024, 64, 64)
        EPS = 1e-12
        value = jnp.einsum('bnd,ed->bne', x, W) + b
        norm = jnp.linalg.norm(x, axis=-1, keepdims=True)
        normed_x = x / jnp.maximum(norm, EPS)
        cos_sim = jnp.einsum('bnd,bmd->bnm', normed_x, normed_x)
        topk_vals, topk_inds = jax.lax.top_k(cos_sim, TOP_K)
        b_idx = jnp.arange(x.shape[0])[:, None, None]
        n_idx = jnp.arange(x.shape[1])[None, :, None]
        attn_sparse = jnp.zeros_like(cos_sim).at[b_idx, n_idx, topk_inds].set(topk_vals)
        attn = jax.nn.softmax(attn_sparse, axis=-1)
        return jnp.einsum('bnm,bmd->bnd', attn, value)

    def _L1_ffn_ref(x, Wg, bg, W1, b1, W2, b2):
        import jax, jax.numpy as jnp
        import numpy as np
        TOP_K = 2
        B, L, D = x.shape
        E = W1.shape[0]
        xf = x.reshape(-1, D)
        gate_logits = xf @ Wg + bg
        top_w, top_i = jax.lax.top_k(gate_logits, TOP_K)
        top_w = jax.nn.softmax(top_w, axis=-1)
        w_dense = jnp.sum(jax.nn.one_hot(top_i, E, dtype=xf.dtype) * top_w[..., None], axis=1)
        out = jnp.zeros_like(xf)
        for e in range(E):
            h = jax.nn.gelu(xf @ W1[e] + b1[e], approximate=False)
            out = out + w_dense[:, e:e + 1] * (h @ W2[e] + b2[e])
        return out.reshape(B, L, D)
    h = _L0_tok_ref(x, L0_tok_d_gamma_batched, L0_tok_Wq, L0_tok_bq, L0_tok_Wk, L0_tok_bk, L0_tok_Wv, L0_tok_bv, L0_tok_Wo, L0_tok_bo, L0_tok_prelu_a)
    h = h + _L0_attn_ref(_layernorm(h, axis=-1), L0_attn_ln_gamma, L0_attn_ln_beta, L0_attn_Wq, L0_attn_bq, L0_attn_Wk, L0_attn_bk, L0_attn_Wv, L0_attn_bv, L0_attn_Wpos, L0_attn_u_bias, L0_attn_v_bias, L0_attn_Wout, L0_attn_bout)
    h = h + _L0_ffn_ref(_layernorm(h, axis=-1), L0_ffn_ln1_w, L0_ffn_ln2_w, L0_ffn_wq, L0_ffn_wk, L0_ffn_wv, L0_ffn_wo, L0_ffn_router_w, L0_ffn_w1, L0_ffn_w2, L0_ffn_w3)
    h = h + _L1_attn_ref(_layernorm(h, axis=-1), L1_attn_W, L1_attn_b)
    h = h + _L1_ffn_ref(_layernorm(h, axis=-1), L1_ffn_Wg, L1_ffn_bg, L1_ffn_W1, L1_ffn_b1, L1_ffn_W2, L1_ffn_b2)
    return h

_drawn_inputs = setup_inputs


def setup_inputs(seed=0):
    import zlib

    import numpy as np

    out = dict(_drawn_inputs(seed))
    spreads = {'L0_attn_ln_gamma': (1.0, 0.6),
     'L0_attn_ln_beta': (0.0, 0.8),
     'L0_attn_bq': (0.0, 2.0),
     'L0_attn_bk': (0.0, 2.0),
     'L0_attn_bv': (0.0, 0.8),
     'L0_attn_bout': (0.0, 2.0),
     'L0_ffn_ln1_w': (1.0, 0.6),
     'L0_ffn_ln2_w': (1.0, 0.6),
     'L1_ffn_bg': (0.0, 0.8),
     'L1_ffn_b1': (0.0, 2.0),
     'L1_ffn_b2': (0.0, 2.0)}
    factors = {'L0_tok_bo': 33.611,
     'L0_attn_Wq': 8.0,
     'L0_attn_Wk': 8.0,
     'L0_attn_Wv': 8.0,
     'L0_attn_Wpos': 50.292,
     'L0_attn_u_bias': 64.0,
     'L0_attn_v_bias': 64.0,
     'L0_attn_Wout': 8.0,
     'L0_ffn_wq': 8.0,
     'L0_ffn_wk': 8.0,
     'L0_ffn_wv': 8.0,
     'L0_ffn_wo': 8.0,
     'L0_ffn_router_w': 8.0,
     'L0_ffn_w1': 8.0,
     'L0_ffn_w2': 8.0,
     'L0_ffn_w3': 8.0,
     'L1_attn_W': 25.22,
     'L1_attn_b': 33.431,
     'L1_ffn_Wg': 8.0,
     'L1_ffn_W1': 8.0,
     'L1_ffn_W2': 8.0}
    for name, (base, spread) in spreads.items():
        noise = np.random.default_rng([zlib.crc32(name.encode()), seed]).standard_normal(out[name].shape)
        drawn = base * np.exp(spread * noise) if base else spread * noise
        out[name] = jnp.asarray(drawn.astype(out[name].dtype))
    for name, factor in factors.items():
        out[name] = (out[name] * factor).astype(out[name].dtype)
    return out
```

```python
from contextlib import ExitStack

import numpy as np

import concourse.bass as bass
from concourse import mybir
from concourse.alu_op_type import AluOpType as ALU

F32 = mybir.dt.float32
F32R = mybir.dt.float32r
BF16 = mybir.dt.bfloat16
I32 = mybir.dt.int32
U32 = mybir.dt.uint32
ACT = mybir.ActivationFunctionType
X = mybir.AxisListType.X

P = 128
B, T, D = 4, 1024, 64
NC = T // P
HALF = 512
H, DH = 4, 16
E = 8
HID = int(8 / 3 * D)
REST = HID - P
NQ = E + E // 2
GH = 256
NG = E * GH // P
TOPK = 64
DUP = D // DH
PREP = 8
PREP_AT = [0, 2, 4, 5, 6, 7, 8, 8, 8]
SPLIT = 3
TAKEN = -3.0

POWERS = [(1, 0), (3, 0), (1, 0), (3, 0), (3, 0), (1, 0), (3, 1), (1, 0)]

INPUTS = ["xT", "gateT", "tok_Wq", "tok_bq", "tok_Wk", "tok_bk", "tok_Wv", "tok_bv", "tok_Wo", "tok_bo", "prelu_a",
          "ln_gamma", "ln_beta", "Wq", "WqT", "bq", "Wk", "bk", "Wv", "bv", "WposT", "u_bias", "v_bias", "Wout",
          "bout", "ln1_w", "ln2_w", "wqT", "wkT", "wvT", "woT", "routerT", "w1T", "w2T", "w3T",
          "W_D", "b_D", "Wg", "bg", "W1", "b1", "W2", "b2",
          "pe_early", "pe_late", "rot_cos", "rot_sin", "rope_cos", "rope_sin", "identity", "late_mask", "next_mask", "future",
          "parts"]


def attend_steps(groups, last_chunk, fix=False, prep=False):
    steps = [("P", 0, k) for k in range(PREP)] if prep else []
    waiting = []

    def product():
        if len(waiting) == SPLIT:
            steps.append(("AV",) + waiting.pop(0))

    for g in range(groups + 1):
        todo = [(g - 1, j) for j in range(last_chunk(g - 1) + 1)] if g else []
        for a in range(4):
            if g < groups:
                steps.append(("S", 4 * g + a, 0))
                product()
                if fix:
                    steps.append(("F", 4 * g + a, 0))
            for t in todo[len(todo) * a // 4:len(todo) * (a + 1) // 4]:
                product()
                steps.append(("T",) + t)
                waiting.append(t)
            if prep and g // 2 + 1 < groups // 2:
                n = 4 * (g % 2) + a
                steps += [("P", g // 2 + 1, k) for k in range(PREP_AT[n], PREP_AT[n + 1])]
    return steps + [("AV",) + t for t in waiting]


def build(nc, t, out):
    with ExitStack() as ctx:
        def sb(name, shape, dt=F32):
            return ctx.enter_context(nc.sbuf_tensor(name, shape, dt))

        sems = {}

        def sem(name):
            if name not in sems:
                sems[name] = ctx.enter_context(nc.semaphore(name))
            return sems[name]

        rot_cos, rot_sin = sb("rot_cos_sb", [P, T]), sb("rot_sin_sb", [P, T])
        rope_cos, rope_sin = sb("rope_cos_sb", [P, T]), sb("rope_sin_sb", [P, T])
        ident = sb("ident", [P, P])
        ident_bf = sb("ident_bf", [P, P], BF16)
        future = sb("future_sb", [P, P], BF16)
        late_mask, next_mask = sb("late_mask_sb", [P, P + 1], I32), sb("next_mask_sb", [P, P + 1], I32)
        parts = sb("parts_sb", [P, 3])
        tok_w = {n: sb("tok_w" + n, [D + 1, 2 * D if n in "qk" else D]) for n in "qkvo"}
        prelu = sb("prelu", [P, 1])
        affine = sb("affine", [D, 4])
        posw = sb("posw", [D + 1, H, 4 * D])
        qkw = sb("qkw", [D + 1, 2, H, D])
        wv_b, wout_b = sb("wv_b", [D + 1, D]), sb("wout_b", [D + 1, D])
        qk_c = sb("qk_c", [D, 3, 2, P])
        wv_c, wo_c = sb("wv_c", [D, 2 * DH]), sb("wo_c", [D, D])
        router = sb("router", [D, E])
        w13 = sb("w13", [P, NQ, P])
        w1p, w3p = w13[0:D], w13[D:P]
        w2a, w2b = sb("w2a", [P, E, D]), sb("w2b", [P, E // 2, 2 * D])
        w_d, wg_e = sb("w_d", [D + 1, D]), sb("wg_e", [D + 1, E])
        w1e, b1e = sb("w1e", [D + 1, NG * P]), sb("b1e", [P, NG])
        w2e = sb("w2e", [P, NG, D])
        b2e, ones_row = w1e[D:D + 1, 0:E * D], w1e[D:D + 1, E * D:E * D + P]
        exponents = sb("exponents", [P, 2, NC])
        lowest = sb("lowest", [P, NC, E])
        first_key = sb("first_key", [P, E])

        fm = sb("fm", [D + 1, T])
        fm2 = sb("fm2", [D + 1, T])
        pair = sb("pair", [P, T])
        context_sum = pair[0:D, :]
        fm_low = pair[D:P, :]
        v_tok = sb("v_tok", [P, NC, D])
        v_d = sb("v_d", [P, NC, P], F32R)
        v_pad = sb("v_pad", [P, NC, H, P], F32R)
        base = -(-nc.sbuf_base // 32) * 32
        area = sb("area", [P, 6 * T + 8])
        assert nc.sbuf_base == base + 4 * (6 * T + 8)

        def at(name, offset, shape, dt=F32R):
            return nc.alloc_sbuf_tensor_at(name, shape, dt, offset=base + 4 * offset)

        q1 = at("q1", 0, [P, 2, T + 1])
        q2 = at("q2", 2 * T + 8, [P, 2, T])
        q2_late = at("q2_late", 4 * T + 8, [P, 2, T])
        k1, k1_late = sb("k1", [P, T], F32R), sb("k1_late", [P, T], F32R)
        k2, k2_late = sb("k2", [P, 2, T], F32R), sb("k2_late", [P, 2, T], F32R)
        rounded = sb("rounded", [P, 2, HALF], F32R)
        probs = sb("probs", [P, 2, 4, T])
        probsT = sb("probsT", [P, 2, SPLIT, HALF], F32R)
        stack_a = probsT[:].rearrange("p a b t -> p (a b t)")
        big = probs[:].rearrange("p a b t -> p (a b t)")
        wqT_b = big[0:DH, 0:H * (D + 1)].rearrange("d (h m) -> d h m", h=H)
        wpos = big[0:DH, 512:512 + H * 4 * D].rearrange("d (h m) -> d h m", h=H)
        vb16 = big[0:DH, 2048:2048 + H]
        u_row = big[0:D + 1, 2560:2560 + D]
        pe_raw = big[:, 3072:3072 + 2 * T].rearrange("p (a t) -> p a t", a=2)
        qk_raw = big[0:D + 1, 5120 + D:5120 + 3 * D].rearrange("m (a n) -> m a n", a=2)
        wqk_raw = big[0:D, 5632:5632 + D + 2 * DH]
        hid = big.rearrange("p (q t) -> p q t", t=HALF)
        cosb = sb("cosb", [P, 2, T])
        silu = cosb[:, 0, :].rearrange("p (b t) -> p b t", b=2)
        work = sb("work", [P, T])
        top8 = sb("top8", [P, 8])
        nmax = sb("nmax", [P, 32])
        rsum = sb("rsum", [P, 32])
        h = sb("h", [P, NC, D])
        xc = sb("xc", [P, NC, D])
        sq = sb("sq", [P, NC, D])
        f_tok = sb("f_tok", [P, NC, D])
        xn = xc
        mix = sq
        st = sb("st", [P, 8, NC])
        gl = sb("gl", [P, 5, NC, E])
        gates = sb("gates", [P, NC, E])
        gs = sb("gs", [P, 3, NC])

        S = [ctx.enter_context(nc.psum_tensor(f"scores{i}", [P, T], F32)) for i in range(2)]
        R = [ctx.enter_context(nc.psum_tensor(f"ring{i}", [P, HALF], F32)) for i in range(2)]
        C = [ctx.enter_context(nc.psum_tensor(f"context{i}", [P, HALF], F32)) for i in range(2)]

        def f(ap):
            return ap.bitcast(F32)

        gate_a = nc.alloc_sbuf_tensor_at("gate_a", [P, 6, T], F32, offset=base)
        gate = [gate_a[:, c, :] for c in range(6)] + [cosb[:, c, :] for c in range(2)]

        def load_gate(load):
            by_tile = t["gateT"].rearrange("(c p) t -> p c t", p=P)
            load(gate_a[:], by_tile[:, 0:6, :])
            load(cosb[:], by_tile[:, 6:8, :])

        a_q_hi, a_q_lo, a_keys = (stack_a[:, k * T:(k + 1) * T] for k in range(3))
        a_k_hi = rounded[:].rearrange("p a t -> p (a t)")
        c_stack = q2[:, 0, :], q2[:, 1, :], q2_late[:, 0, :]
        d_hi, d_lo, d_stack = q1[:, 0, 0:T], q1[:, 1, 0:T], q2_late[:, 1, :]

        def half(j):
            return slice(j * HALF, (j + 1) * HALF)

        def chunk(c):
            return slice(c * P, (c + 1) * P)

        def toks(ap):
            return ap.rearrange("p c d -> p (c d)")

        def over_features(ap):
            return ap.rearrange("p (c o) -> p c o", o=1).to_broadcast([P, NC, D])

        with nc.Block() as block:
            zeroed, loaded, made = sem("zeroed"), sem("loaded"), sem("made")
            n_loads = [0]

            fills = [(w13[:], 0.0), (w2b[:], 0.0), (f(v_pad[:]), 0.0)]
            fills += [(fm[D:D + 1, :], 1.0), (fm2[D:D + 1, :], 1.0), (ones_row, 1.0)]
            fills += [(exponents[:, 0], -0.5), (exponents[:, 1], 0.5), (lowest[:], -3.0e38)]
            fills += [(first_key[:, e:e + 1], float(E - e)) for e in range(E)]

            @block.gpsimd
            def _(pool):
                for n, (where, value) in enumerate(fills):
                    if n:
                        pool.wait_ge(zeroed, n)
                    nc.gpsimd.memset(where, value).then_inc(zeroed, 1)

            @block.sync
            def _(sp):
                def load(dst, src):
                    n_loads[0] += 1
                    sp.dma_start(dst, src, allow_slow_non_contiguous=True).then_inc(loaded, 16)

                row = lambda ap: ap.rearrange("(o n) -> o n", o=1)
                col = lambda ap: ap.rearrange("(n o) -> n o", o=1)
                load(rot_cos[:], t["rot_cos"])
                load(rot_sin[:], t["rot_sin"])
                load(rope_cos[:], t["rope_cos"])
                load(rope_sin[:], t["rope_sin"])
                load(ident[:], t["identity"])
                load(late_mask[:], t["late_mask"])
                load(next_mask[:], t["next_mask"])
                load(future[:], t["future"])
                load(parts[:], t["parts"])
                for r in range(2):
                    load(pe_raw[r * D:(r + 1) * D, 0, :], t["pe_early"])
                    load(pe_raw[r * D:(r + 1) * D, 1, :], t["pe_late"])
                for n in "qkvo":
                    for r in range(2 if n in "qk" else 1):
                        load(tok_w[n][0:D, r * D:(r + 1) * D], t["tok_W" + n])
                        load(tok_w[n][D:D + 1, r * D:(r + 1) * D], row(t["tok_b" + n]))
                load(prelu[:], t["prelu_a"].to_broadcast([P, 1]))
                for i, n in enumerate(("ln_gamma", "ln_beta", "ln1_w", "ln2_w")):
                    load(affine[:, i:i + 1], col(t[n]))
                load(wqT_b[:, :, 0:D], t["WqT"].rearrange("(h d) m -> d h m", d=DH))
                load(wqT_b[:, :, D:D + 1], t["bq"].rearrange("(h d o) -> d h o", d=DH, o=1))
                load(vb16, t["v_bias"])
                pos = t["WposT"].rearrange("s (h d) m -> d h s m", d=DH)
                for s in range(4):
                    load(wpos[:, :, s * D:(s + 1) * D], pos[:, :, s // 2, :])
                for i, n in enumerate("qk"):
                    load(qk_raw[0:D, i, :], t["W" + n])
                    load(qk_raw[D:D + 1, i, :], row(t["b" + n]))
                load(u_row[D:D + 1, :], t["u_bias"].rearrange("(o h) d -> o (h d)", o=1))
                load(wqk_raw[:, 0:D], t["wqT"])
                load(wqk_raw[:, D:D + 2 * DH], t["wkT"])
                load(wv_b[0:D, :], t["Wv"])
                load(wv_b[D:D + 1, :], row(t["bv"]))
                load(wout_b[0:D, :], t["Wout"])
                load(wout_b[D:D + 1, :], row(t["bout"]))
                load(wv_c[:], t["wvT"])
                load(wo_c[:], t["woT"])
                load(router[:], t["routerT"])
                sp.wait_ge(zeroed, len(fills))
                for rows, src in ((w1p, "w1T"), (w3p, "w3T")):
                    w = t[src].rearrange("e m n -> m e n")
                    load(rows[:, 0:E, :], w[:, :, 0:P])
                    for r in range(2):
                        load(rows[:, E:NQ, 64 * r:64 * r + REST], w[:, r::2, P:HID])
                load(w2a[:], t["w2T"][:, 0:P, :].rearrange("e n m -> n e m"))
                for r in range(2):
                    load(w2b[64 * r:64 * r + REST, :, r * D:(r + 1) * D], t["w2T"][r::2, P:HID, :].rearrange("e n m -> n e m"))
                load(w_d[0:D, :], t["W_D"])
                load(w_d[D:D + 1, :], row(t["b_D"]))
                load(wg_e[0:D, :], t["Wg"])
                load(wg_e[D:D + 1, :], row(t["bg"]))
                load(w1e[0:D, :].rearrange("m (e n) -> m e n", e=E), t["W1"].rearrange("e m n -> m e n"))
                load(b1e[:], t["b1"].rearrange("e (q n) -> n (e q)", n=P))
                load(w2e[:], t["W2"].rearrange("e (q n) m -> n (e q) m", n=P))
                load(b2e, t["b2"].rearrange("(o e) m -> o (e m)", o=1))
                load_gate(load)
                sp.wait_ge(loaded, 16 * n_loads[0])

            @block.vector
            def _(dve):
                dve.wait_ge(loaded, 16 * n_loads[0])
                n = [0]

                def step(ins):
                    ins.then_inc(made, 1)
                    n[0] += 1
                    dve.wait_ge(made, n[0])

                bqv = wqT_b[:, :, D:D + 1].rearrange("d h o -> d (h o)")
                step(nc.vector.tensor_tensor(bqv, bqv, vb16, ALU.add))
                step(nc.vector.tensor_scalar(wqT_b[:], wqT_b[:], 0.125, None, ALU.mult))
                step(nc.vector.tensor_tensor(qk_raw[D:D + 1, 0, :], qk_raw[D:D + 1, 0, :], u_row[D:D + 1, :], ALU.add))
                step(nc.vector.tensor_scalar(qk_raw[:, 0, :], qk_raw[:, 0, :], 0.125, None, ALU.mult))
                for i in range(2):
                    nc.vector.tensor_copy(
                        qkw[:, i, :, :].rearrange("m h (k d) -> m h k d", k=DUP),
                        qk_raw[:, i, :].rearrange("m (h o d) -> m h o d", h=H, o=1).to_broadcast([D + 1, H, DUP, DH]))\
                        .then_inc(made, 1)
                    n[0] += 1
                dve.wait_ge(made, n[0])
                step(nc.vector.tensor_scalar(wqk_raw[:, 0:D], wqk_raw[:, 0:D], 0.25, None, ALU.mult))
                for k in range(3):
                    if k < 2:
                        src = wqk_raw[:, 0:D].rearrange("m (g t d) -> m t g d", g=2, t=2)[:, k]
                    else:
                        src = wqk_raw[:, D:D + 2 * DH].rearrange("m (g d) -> m g d", g=2)
                    src = src.rearrange("m g (o d) -> m g o d", o=1)
                    out_ = qk_c[:, k].rearrange("m x (g k d) -> m x g k d", g=2, k=DUP)
                    for x, d0, s0, w in ((0, 0, 0, DH), (1, 0, DH // 2, DH // 2), (1, DH // 2, 0, DH // 2)):
                        step(nc.vector.tensor_copy(out_[:, x, :, :, d0:d0 + w],
                                                   src[:, :, :, s0:s0 + w].to_broadcast([D, 2, DUP, w])))
                step(nc.vector.tensor_copy(ident_bf[:], ident[:]))
                for i, (hi, low) in enumerate(((k1, k2), (k1_late, k2_late))):
                    step(nc.vector.tensor_copy(hi[:], pe_raw[:, i, :]))
                    for b in range(2):
                        step(nc.vector.tensor_tensor(low[0:D, b, :], pe_raw[0:D, i, :], f(hi[0:D, :]), ALU.subtract))
                for hh in range(H):
                    dve.wait_ge(sem("posw_ready"), hh + 1)
                    nc.vector.tensor_copy(posw[:, hh, :], R[hh % 2][0:D + 1, 0:4 * D]).then_inc(sem("posw_copied"), 1)

            @block.tensor
            def _(pe):
                pe.wait_ge(made, 2)
                for hh in range(H):
                    if hh >= 2:
                        pe.wait_ge(sem("posw_copied"), hh - 1)
                    nc.tensor.matmul(R[hh % 2][0:D + 1, 0:4 * D], wqT_b[:, hh, :], wpos[:, hh, :],
                                     start=True, stop=True).then_inc(sem("posw_ready"), 1)

        class Attend:

            def __init__(self, name, groups, causal=False, prep=False):
                self.name, self.groups, self.causal = name, groups, causal
                self.scores_read = "scores_used" if name == "D" else "probs"
                self.steps = attend_steps(groups, lambda g: 4 * (g % 2) + 3 if causal else NC - 1, name == "B", prep)
                self.t_at = {s[1:]: i for i, s in enumerate(x for x in self.steps if x[0] == "T")}
                self.ring = [s for s in self.steps if s[0] in "TPF"]
                self.slot = {s: k for k, s in enumerate(self.ring)}

            def s(self, what):
                return sem(f"{self.name}_{what}")

            def t_until(self, g):
                return sum(1 for (gg, j) in self.t_at if gg <= g)

            def wait_slot(self, eng, k):
                if k < 2:
                    return
                kind, x, j = self.ring[k - 2]
                if kind == "T":
                    eng.wait_ge(self.s("lo"), self.t_at[(x, j)] + 1)
                elif kind == "F":
                    eng.wait_ge(self.s("fixed"), 2 * x + 2)
                else:
                    eng.wait_ge(self.s("prep_dve"), 12 * x + 6 * (j // 4) + (1, 2, 4, 5)[j % 4])

            def width(self, x, j):
                return max(0, j - 4 * (x % 2)) * P if self.causal else 0

            def tensor(self, pe, scores, values, fix=None, prepare=None):
                for kind, x, j in self.steps:
                    if kind == "P":
                        self.wait_slot(pe, self.slot[(kind, x, j)])
                        prepare(x, j, R[self.slot[(kind, x, j)] % 2]).then_inc(self.s("prep"), 1)
                    elif kind == "S":
                        if x >= 2:
                            pe.wait_ge(self.s(self.scores_read), x - 1)
                        ins = scores(x)
                        if fix is None:
                            ins.then_inc(self.s("scores"), 1)
                    elif kind == "F":
                        self.wait_slot(pe, self.slot[(kind, x, j)])
                        fix(x, R[self.slot[(kind, x, j)] % 2]).then_inc(self.s("scores"), 1)
                    elif kind == "T":
                        k, w = self.slot[(kind, x, j)], self.width(x, j)
                        if j == 0:
                            pe.wait_ge(self.s("probs"), 4 * x + 4)
                        self.wait_slot(pe, k)
                        for a in range(w // P, 4):
                            ins = nc.tensor.transpose(R[k % 2][:, chunk(a)], probs[:, x % 2, a, chunk(j)], ident[:])
                        ins.then_inc(self.s("turned"), 1)
                    else:
                        m, w = self.t_at[(x, j)], self.width(x, j)
                        last = 4 * (x % 2) + 3 if self.causal else NC - 1
                        pe.wait_ge(self.s("hi"), m + 1)
                        nc.tensor.matmul(C[x % 2][:, w:HALF], values(x, j), probsT[:, 0, m % SPLIT, w:HALF],
                                         start=(x < 2 and j == 0), stop=False, skip_group_check=True)
                        pe.wait_ge(self.s("lo"), m + 1)
                        nc.tensor.matmul(C[x % 2][:, w:HALF], values(x, j), probsT[:, 1, m % SPLIT, w:HALF], start=False,
                                         stop=(x >= self.groups - 2 and j == last),
                                         skip_group_check=True).then_inc(self.s("products"), 1)

            def take_hi(self, act, x, j):
                m, k, w = self.t_at[(x, j)], self.slot[("T", x, j)], self.width(x, j)
                act.wait_ge(self.s("turned"), m + 1)
                if m >= SPLIT:
                    act.wait_ge(self.s("products"), m - SPLIT + 1)
                nc.scalar.activation(probsT[:, 0, m % SPLIT, w:HALF], R[k % 2][:, w:HALF], ACT.Copy)\
                    .then_inc(self.s("hi"), 1)

            def take_lo(self, dve, x, j):
                m, k, w = self.t_at[(x, j)], self.slot[("T", x, j)], self.width(x, j)
                dve.wait_ge(self.s("hi"), m + 1)
                nc.vector.tensor_tensor(probsT[:, 1, m % SPLIT, w:HALF], R[k % 2][:, w:HALF],
                                        f(probsT[:, 0, m % SPLIT, w:HALF]), ALU.subtract).then_inc(self.s("lo"), 1)

            def n_products(self):
                return len(self.t_at)

        AB = Attend("B", 2 * H, prep=True)
        AC = Attend("C", 2 * H, causal=True)
        AD = Attend("D", 2)

        setup_sems = set(sems)
        with nc.Fori(0, B) as seq:
            with nc.Block() as block:

                @block.sync
                def _(sp):
                    sp.dma_start(fm[0:D, :], t["xT"][bass.ds(seq, 1)].rearrange("o d t -> (o d) t"))\
                      .then_inc(sem("x_loaded"), 16)
                    for hh in range(H):
                        b = hh % 2
                        sp.wait_ge(sem("B_prep_act"), 8 * (hh + 1))
                        sp.wait_ge(sem("B_prep_dve"), 12 * (hh + 1))
                        for dst, src in ((q2[0:D, b, :], q1[0:D, b, 0:T]),
                                         (q2_late[0:D, b, 0:T - 1], q1[0:D, b, 1:T]),
                                         (q2_late[D:P, b, :], q2[D:P, b, :]), (k2_late[D:P, b, :], k2[D:P, b, :])):
                            sp.dma_start(f(dst), f(src)).then_inc(sem("B_copied"), 16)
                    sp.wait_ge(sem("D_products"), AD.n_products())
                    load_gate(lambda dst, src: sp.dma_start(dst, src).then_inc(sem("gate_loaded"), 16))
                    sp.wait_ge(sem("gate_loaded"), 32)
                    sp.wait_ge(sem("result"), 1)
                    sp.dma_start(out[bass.ds(seq, 1)].rearrange("o (c p) d -> p (o c) d", p=P), h[:])\
                      .then_inc(sem("stored"), 16)
                    sp.wait_ge(sem("stored"), 16)

                @block.gpsimd
                def _(pool):
                    for n, (k, p) in enumerate(POWERS):
                        if n == 1:
                            for i, pad in enumerate((f(q1[:, :, T:T + 1]), f(q2_late[0:D, :, T - 1:T]))):
                                if i:
                                    pool.wait_ge(sem("padded"), i)
                                nc.gpsimd.memset(pad, 0.0).then_inc(sem("padded"), 1)
                        pool.wait_ge(sem("power_base"), n + 1)
                        nc.gpsimd.tensor_tensor(st[:, k], st[:, 4], exponents[:, p], ALU.pow)\
                            .then_inc(sem("powered"), 1)

                @block.tensor
                def _(pe):
                    mm = nc.tensor.matmul

                    def project(dst, w, src, k, done):
                        for j in range(2):
                            ins = mm(dst(j), w, src[0:k, half(j)], start=True, stop=True)
                        ins.then_inc(done, 1)

                    def by_token(dst, src, w, k, n, done):
                        for c in range(NC):
                            ins = mm(dst[:, c * n:(c + 1) * n], src[0:k, chunk(c)], w, start=True, stop=True)
                        ins.then_inc(done, 1)

                    def turn(src, done):
                        for c in range(NC):
                            ins = nc.tensor.transpose(S[0][0:D, chunk(c)], src[:, c, :], ident[:])
                        ins.then_inc(done, 1)

                    def normalise(x):
                        pe.wait_ge(sem(f"{x}_recip"), 1)
                        for i in range(NC):
                            ins = nc.tensor.transpose(S[0][0:D, chunk(i)], work[:, i * D:(i + 1) * D], ident[:])
                        ins.then_inc(sem(f"{x}_spread"), 1)

                    pe.wait_ge(sem("x_loaded"), 16)
                    project(lambda j: S[0][:, half(j)], tok_w["q"][:], fm, D + 1, sem("A_q"))
                    project(lambda j: S[1][:, half(j)], tok_w["k"][:], fm, D + 1, sem("A_k"))
                    by_token(R[0], fm, tok_w["v"][:], D + 1, D, sem("A_v"))
                    pe.wait_ge(sem("A_q_hi"), 1)
                    pe.wait_ge(sem("A_split"), 2)
                    for s in range(NC + 1):
                        if s < NC:
                            if s >= 2:
                                pe.wait_ge(sem("A_gated"), s - 1)
                            for j in range(2):
                                mm(S[s % 2][:, half(j)], a_keys[:, chunk(s)], a_q_hi[:, half(j)],
                                   start=True, stop=False)
                                ins = mm(S[s % 2][:, half(j)], a_keys[:, chunk(s)], a_q_lo[:, half(j)],
                                         start=False, stop=True)
                            ins.then_inc(sem("A_scores"), 1)
                        if s >= 1:
                            pe.wait_ge(sem("A_gated"), s)
                            if s == 1:
                                pe.wait_ge(sem("A_v_copied"), 1)
                            for j in range(2):
                                ins = mm(C[j][0:D, :], v_tok[:, s - 1, :], probs[:, 0, (s - 1) % 2, half(j)],
                                         start=(s == 1), stop=(s == NC))
                            ins.then_inc(sem("A_products"), 1)
                    pe.wait_ge(sem("A_mix_copied"), 2)
                    by_token(R[1], fm2, tok_w["o"][:], D + 1, D, sem("A_out"))

                    pe.wait_ge(sem("B_xn"), 1)
                    turn(xn, sem("B_turned_x"))
                    pe.wait_ge(sem("B_fm"), 1)
                    by_token(C[0], fm, wv_b[:], D + 1, D, sem("B_v"))

                    def prepare_b(hh, k, bank):
                        what, cols = k % 4, half(k // 4)
                        if what < 2:
                            return mm(bank[:], posw[:, hh, what * P:(what + 1) * P], fm[:, cols], start=True, stop=True)
                        return mm(bank[D:P, :], qkw[:, what - 2, hh, :], fm[:, cols], start=True, stop=True)

                    def late_scores(dst, b, i, j0, j1):
                        mm(dst, q1[:, b, i * P + 1:(i + 1) * P + 1], k1_late[:, j0:j1], start=True, stop=False,
                           skip_group_check=True)
                        return mm(dst, q2_late[:, b, chunk(i)], k2_late[:, b, j0:j1], start=False, stop=True,
                                  skip_group_check=True)

                    def scores_b(n):
                        hh, i = n // NC, n % NC
                        b = hh % 2
                        if i == 0:
                            pe.wait_ge(sem("B_prep_dve"), 12 * (hh + 1))
                            pe.wait_ge(sem("B_prep_act"), 8 * (hh + 1))
                            pe.wait_ge(sem("B_copied"), 64 * (hh + 1))
                        if n == 0:
                            pe.wait_ge(sem("padded"), 2)
                        edge = (i + 1) * P
                        for j0, j1 in ((0, min(edge, HALF)), (HALF, edge)):
                            if j1 > j0:
                                mm(S[n % 2][:, j0:j1], q1[:, b, chunk(i)], k1[:, j0:j1], start=True, stop=False,
                                   skip_group_check=True)
                                mm(S[n % 2][:, j0:j1], q2[:, b, chunk(i)], k2[:, b, j0:j1], start=False, stop=True,
                                   skip_group_check=True)
                        for j0, j1 in ((edge, HALF), (max(edge, HALF), T)):
                            if j1 > j0:
                                late_scores(S[n % 2][:, j0:j1], b, i, j0, j1)

                    def fix_b(n, bank):
                        hh, i = n // NC, n % NC
                        b, j1 = hh % 2, min((i + 1) * P + 2, T)
                        late_scores(bank[:, 0:j1 - i * P], b, i, i * P, j1)
                        return mm(bank[:, 256:256 + j1 - i * P], q2[D:P, b, chunk(i)], k2[D:P, b, i * P:j1],
                                  start=True, stop=True, skip_group_check=True)

                    pe.wait_ge(sem("B_v_hi"), 4)
                    pe.wait_ge(sem("B_v_lo"), 4)
                    AB.tensor(pe, scores_b, lambda x, j: v_pad[:, j, x // 2, :], fix_b, prepare_b)
                    normalise("B")
                    pe.wait_ge(sem("B_context"), 2)
                    by_token(R[0], fm2, wout_b[:], D + 1, D, sem("B_out"))

                    pe.wait_ge(sem("C_xn"), 1)
                    turn(xn, sem("C_turned_x"))
                    pe.wait_ge(sem("C_fm"), 1)
                    for k in range(3):
                        if k == 2:
                            pe.wait_ge(sem("C_rope"), 2)
                        project(lambda j: (R[j][:] if k == 1 else S[0][:, half(j)]), qk_c[:, k, 0, :], fm, D,
                                sem("C_proj"))
                        project(lambda j: (C[j][:] if k == 1 else S[1][:, half(j)]), qk_c[:, k, 1, :], fm, D,
                                sem("C_proj"))
                    pe.wait_ge(sem("C_rope"), 8)
                    by_token(C[0], fm, wv_c[:], D, 2 * DH, sem("C_v"))

                    def scores_c(n):
                        hh, i = n // NC, n % NC
                        rows, edge = slice(D * (hh // 2), D * (hh // 2) + D), (i + 1) * P
                        for j0, j1 in ((0, min(edge, HALF)), (HALF, edge)):
                            if j1 > j0:
                                mm(S[n % 2][:, j0:j1], c_stack[hh % 2][rows, chunk(i)], c_stack[2][rows, j0:j1],
                                   start=True, stop=False, skip_group_check=True)
                        return mm(S[n % 2][:, chunk(i)], ident_bf[:], future[:], start=False, stop=True,
                                  skip_group_check=True)

                    pe.wait_ge(sem("C_v_hi"), 4)
                    pe.wait_ge(sem("C_v_lo"), 4)
                    pe.wait_ge(sem("C_rope"), 14)
                    AC.tensor(pe, scores_c, lambda x, j: v_pad[:, j, x // 2, :])
                    normalise("C")
                    pe.wait_ge(sem("C_context"), 2)
                    by_token(R[0], fm2, wo_c[:], D, D, sem("C_out"))

                    pe.wait_ge(sem("M_xn"), 1)
                    turn(xn, sem("M_turned_x"))
                    pe.wait_ge(sem("M_fm"), 2)
                    by_token(R[0], fm, router[:], D, E, sem("M_logits"))
                    pe.wait_ge(sem("M_logits_read"), 1)
                    for j in range(2):
                        for q in range(NQ):
                            n = NQ * j + q
                            if n >= 2:
                                pe.wait_ge(sem("M_hidden"), n - 1)
                            mm(S[n % 2][:, half(0)], w1p[:, q, :], fm[0:D, half(j)], start=True, stop=True)\
                                .then_inc(sem("M_gate"), 1)
                            mm(S[n % 2][:, half(1)], w3p[:, q, :], fm_low[:, half(j)], start=True, stop=True)\
                                .then_inc(sem("M_up"), 1)
                        pe.wait_ge(sem("M_hidden"), NQ * (j + 1))
                        for c in range(4):
                            n = 4 * j + c
                            if n >= 2:
                                pe.wait_ge(sem("M_weighted"), n - 1)
                            for e in range(0, E, 2):
                                for k in (e, e + 1):
                                    mm(R[n % 2][:, k * D:(k + 1) * D], hid[:, k, chunk(c)], w2a[:, k, :],
                                       start=(k == 0), stop=False, skip_group_check=True)
                                ins = mm(R[n % 2][:, e * D:(e + 2) * D], hid[:, E + e // 2, chunk(c)],
                                         w2b[:, e // 2, :], start=False, stop=(e == E - 2), skip_group_check=True)
                            ins.then_inc(sem("M_down"), 1)

                    pe.wait_ge(sem("D_x"), 1)
                    turn(f_tok, sem("D_turned_x"))
                    pe.wait_ge(sem("D_fm"), 1)
                    by_token(R[0], fm, w_d[:], D + 1, D, sem("D_v"))
                    pe.wait_ge(sem("D_unit_x"), 2)
                    for c in range(NC):
                        ins = nc.tensor.transpose(S[0][:, chunk(c)], work[:, chunk(c)], ident[:])
                    ins.then_inc(sem("D_turned_unit"), 1)
                    pe.wait_ge(sem("D_unit_split"), 2)
                    pe.wait_ge(sem("D_unit_hi"), 1)
                    pe.wait_ge(sem("D_v_hi"), 1)
                    pe.wait_ge(sem("D_v_lo"), 1)

                    def scores_d(n):
                        for j in range(2):
                            mm(S[n % 2][:, half(j)], d_stack[:, chunk(n)], d_hi[:, half(j)], start=True, stop=False)
                            ins = mm(S[n % 2][:, half(j)], d_stack[:, chunk(n)], d_lo[:, half(j)],
                                     start=False, stop=True)
                        return ins

                    AD.tensor(pe, scores_d, lambda x, j: v_d[:, j, :])
                    pe.wait_ge(sem("D_context"), 2)
                    for c in range(NC):
                        ins = nc.tensor.transpose(S[0][:, c * D:(c + 1) * D], context_sum[:, chunk(c)], ident[0:D, 0:D])
                    ins.then_inc(sem("D_by_token"), 1)

                    pe.wait_ge(sem("E_x"), 1)
                    turn(f_tok, sem("E_turned_x"))
                    pe.wait_ge(sem("E_fm"), 1)
                    by_token(R[0], fm, wg_e[:], D + 1, E, sem("E_logits"))
                    pe.wait_ge(sem("E_logits_read"), 1)
                    for j in range(2):
                        for q in range(NG):
                            n = NG * j + q
                            if n >= 4:
                                pe.wait_ge(sem("E_hidden"), n - 3)
                            mm(S[n // 2 % 2][:, half(n % 2)], w1e[0:D, chunk(q)], fm[0:D, half(j)],
                               start=True, stop=True).then_inc(sem("E_up"), 1)
                        pe.wait_ge(sem("E_hidden"), NG * (j + 1))
                        for c in range(4):
                            n = 4 * j + c
                            if n >= 2:
                                pe.wait_ge(sem("E_weighted"), n - 1)
                            mm(R[n % 2][:], ones_row, b2e, start=True, stop=False, skip_group_check=True)
                            for q in range(NG):
                                e = q // 2
                                ins = mm(R[n % 2][:, e * D:(e + 1) * D], hid[:, q, chunk(c)], w2e[:, q, :],
                                         start=False, stop=(q == NG - 1), skip_group_check=True)
                            ins.then_inc(sem("E_down"), 1)

                @block.scalar
                def _(act):
                    fn = nc.scalar.activation

                    def copy(dst, src):
                        return fn(dst, src, ACT.Copy)

                    def softmax_of(att, width):
                        scored = []

                        def exponential():
                            if scored:
                                x = scored.pop()
                                g, a = x // 4, x % 4
                                act.wait_ge(att.s("max"), x + 1)
                                if g >= 2:
                                    act.wait_ge(att.s("turned"), att.t_until(g - 2))
                                w = width(x)
                                fn(probs[:, g % 2, a, 0:w], S[x % 2][:, 0:w], ACT.Exp, bias=nmax[:, x:x + 1],
                                   accum_out=rsum[:, x:x + 1])\
                                    .then_inc(att.s("probs"), 1)

                        for kind, x, j in att.steps:
                            if kind == "S":
                                exponential()
                                scored.append(x)
                            elif kind == "T":
                                if x == att.groups - 1:
                                    exponential()
                                att.take_hi(act, x, j)
                            elif kind == "P":
                                exponential()
                                prepare_b(x, j)

                    act.wait_ge(sem("A_q"), 1)
                    copy(a_q_hi, S[0][:]).then_inc(sem("A_q_hi"), 1)
                    act.wait_ge(sem("A_k"), 1)
                    copy(a_k_hi, S[1][:]).then_inc(sem("A_k_hi"), 1)
                    act.wait_ge(sem("A_v"), 1)
                    copy(toks(v_tok[:]), R[0][:]).then_inc(sem("A_v_copied"), 1)
                    act.wait_ge(sem("A_products"), NC)
                    for j in range(2):
                        copy(fm2[0:D, half(j)], C[j][0:D, :]).then_inc(sem("A_mix_copied"), 1)
                    act.wait_ge(sem("B_turned_x"), 1)
                    fn(fm[0:D, :], S[0][0:D, :], ACT.Identity, bias=affine[:, 1:2], scale=affine[:, 0:1])\
                        .then_inc(sem("B_fm"), 1)
                    act.wait_ge(sem("B_v"), 1)

                    def values_hi(x, width, group):
                        for hh in range(H):
                            src = C[0][:, 0:NC * width].rearrange("p (c d) -> p c d", d=width)
                            g = group(hh)
                            copy(v_pad[:, :, hh, hh * DH:(hh + 1) * DH], src[:, :, g * DH:(g + 1) * DH])\
                                .then_inc(sem(f"{x}_v_hi"), 1)

                    def prepare_b(hh, k):
                        b, j, what = hh % 2, k // 4, k % 4
                        at = 12 * hh + 6 * j
                        if what == 1:
                            act.wait_ge(sem("B_prep_dve"), at + 3)
                            copy(q1[0:D, b, half(j)], work[0:D, half(j)]).then_inc(sem("B_prep_act"), 1)
                            copy(rounded[D:P, 0, :], work[D:P, half(j)]).then_inc(sem("B_prep_act"), 1)
                        elif what == 2:
                            act.wait_ge(sem("B_prep"), PREP * hh + k + 1)
                            copy(rounded[D:P, 1, :], R[AB.slot[("P", hh, k)] % 2][D:P, :]).then_inc(sem("B_prep_act"), 1)
                        elif what == 3:
                            act.wait_ge(sem("B_prep"), PREP * hh + k + 1)
                            copy(rounded[0:D, 1, :], R[AB.slot[("P", hh, k)] % 2][D:P, :]).then_inc(sem("B_prep_act"), 1)

                    values_hi("B", D, lambda hh: hh)
                    softmax_of(AB, lambda n: T)
                    def context(x):
                        act.wait_ge(sem(f"{x}_products"), {"B": AB, "C": AC, "D": AD}[x].n_products())
                        for j in range(2):
                            copy(context_sum[:, half(j)], C[j][D:P, :]).then_inc(sem(f"{x}_ctx_copied"), 1)

                    context("B")
                    act.wait_ge(sem("C_turned_x"), 1)
                    fn(fm[0:D, :], S[0][0:D, :], ACT.Identity, scale=affine[:, 2:3]).then_inc(sem("C_fm"), 1)
                    for k in range(3):
                        act.wait_ge(sem("C_rope"), (3, 9, 13)[k])
                        copy(stack_a[:, k * T:(k + 1) * T], work[:]).then_inc(sem("C_rounded"), 1)
                        if k == 1:
                            act.wait_ge(sem("C_v"), 1)
                            values_hi("C", 2 * DH, lambda hh: hh // 2)
                    softmax_of(AC, lambda n: (n % NC + 1) * P)
                    context("C")
                    act.wait_ge(sem("M_turned_x"), 1)
                    fn(fm[0:D, :], S[0][0:D, :], ACT.Identity, scale=affine[:, 3:4]).then_inc(sem("M_fm"), 1)
                    fn(fm_low[:], S[0][0:D, :], ACT.Identity, scale=affine[:, 3:4]).then_inc(sem("M_fm"), 1)
                    act.wait_ge(sem("M_shifted"), 1)
                    fn(gl[:, 1], gl[:, 1], ACT.Exp).then_inc(sem("M_exp"), 1)
                    for n in range(2 * NQ):
                        act.wait_ge(sem("M_gate"), n + 1)
                        if n >= 2:
                            act.wait_ge(sem("M_hidden"), n - 1)
                        fn(silu[:, n % 2, :], S[n % 2][:, half(0)], ACT.Silu).then_inc(sem("M_silu"), 1)
                    act.wait_ge(sem("D_turned_x"), 1)
                    copy(fm[0:D, :], S[0][0:D, :]).then_inc(sem("D_fm"), 1)
                    act.wait_ge(sem("D_v"), 1)
                    copy(v_d[:, :, 0:D], R[0][:].rearrange("p (c d) -> p c d", d=D)).then_inc(sem("D_v_hi"), 1)
                    act.wait_ge(sem("D_turned_unit"), 1)
                    copy(d_hi, S[0][:]).then_inc(sem("D_unit_hi"), 1)

                    def sparse_exp(x):
                        act.wait_ge(AD.s("sparse"), x + 1)
                        row = probs[:, x // 4, x % 4, :]
                        fn(row, row, ACT.Exp, accum_out=rsum[:, x:x + 1]).then_inc(AD.s("probs"), 1)

                    for kind, x, j in AD.steps:
                        if kind == "S":
                            act.wait_ge(AD.s("scores"), x + 1)
                            if x >= 2:
                                act.wait_ge(AD.s("sparse"), x - 1)
                            copy(cosb[:, x % 2, :], S[x % 2][:]).then_inc(AD.s("scores_used"), 1)
                            if x >= 1:
                                sparse_exp(x - 1)
                        elif kind == "T":
                            if (x, j) == (1, 0):
                                sparse_exp(NC - 1)
                            AD.take_hi(act, x, j)
                    context("D")
                    act.wait_ge(sem("E_turned_x"), 1)
                    copy(fm[0:D, :], S[0][0:D, :]).then_inc(sem("E_fm"), 1)
                    act.wait_ge(sem("E_shifted"), 1)
                    fn(gl[:, 1], gl[:, 1], ACT.Exp).then_inc(sem("E_exp"), 1)
                    for n in range(2 * NG):
                        act.wait_ge(sem("E_up"), n + 1)
                        if n == NG:
                            act.wait_ge(sem("E_down"), 4)
                        q = n % NG
                        fn(hid[:, q, :], S[n // 2 % 2][:, half(n % 2)], ACT.Gelu, bias=b1e[:, q:q + 1])\
                            .then_inc(sem("E_hidden"), 1)

                @block.vector
                def _(dve):
                    v = nc.vector
                    own, n_own = sem("dve_own"), [0]

                    def step(ins):
                        ins.then_inc(own, 1)
                        n_own[0] += 1
                        dve.wait_ge(own, n_own[0])

                    n_powers = [0]

                    def power(k, base):
                        assert POWERS[n_powers[0]][0] == k
                        base.then_inc(sem("power_base"), 1)
                        n_powers[0] += 1
                        dve.wait_ge(sem("powered"), n_powers[0])

                    def center(x):
                        step(v.tensor_reduce(st[:, 2], x, X, ALU.add))
                        step(v.tensor_scalar(st[:, 2], st[:, 2], -1.0 / D, None, ALU.mult))
                        step(v.tensor_tensor(xc[:], x, over_features(st[:, 2]), ALU.add))
                        mean_square(xc)
                        power(1, v.tensor_scalar(st[:, 4], st[:, 0], 1e-5, None, ALU.add))
                        step(v.tensor_tensor(st[:, 3], st[:, 1], st[:, 1], ALU.mult))
                        step(v.tensor_tensor(st[:, 3], st[:, 3], st[:, 0], ALU.mult))

                    def mean_square(x):
                        step(v.tensor_tensor(sq[:], x[:], x[:], ALU.mult))
                        step(v.tensor_reduce(st[:, 0], sq[:], X, ALU.add))
                        step(v.tensor_scalar(st[:, 0], st[:, 0], 1.0 / D, None, ALU.mult))

                    def scaled(dst, src, k):
                        return v.tensor_tensor(dst, src, over_features(st[:, k]), ALU.mult)

                    def row_max(att, n, width):
                        v.tensor_reduce(nmax[:, n:n + 1], S[n % 2][:, 0:width], X, ALU.max, negate=True)\
                            .then_inc(att.s("max"), 1)

                    def normalise(x):
                        att = {"B": AB, "C": AC, "D": AD}[x]
                        dve.wait_ge(att.s("probs"), 4 * att.groups)
                        n = 4 * att.groups
                        step(v.reciprocal(rsum[:, 0:n], rsum[:, 0:n]))
                        if x != "D":
                            by_chunk = rsum[:].rearrange("p (h i o) -> p i h o", h=H, o=1)
                            v.tensor_copy(work[:, 0:HALF].rearrange("p (i h d) -> p i h d", i=NC, h=H),
                                          by_chunk.to_broadcast([P, NC, H, DH])).then_inc(sem(f"{x}_recip"), 1)
                        for j in range(2):
                            dve.wait_ge(sem(f"{x}_ctx_copied"), j + 1)
                            both = v.tensor_tensor(context_sum[:, half(j)], C[j][0:D, :], context_sum[:, half(j)],
                                                   ALU.add)
                            if x == "D":
                                both.then_inc(sem("D_context"), 1)
                            else:
                                step(both)
                                dve.wait_ge(sem(f"{x}_spread"), 1)
                                v.tensor_tensor(fm2[0:D, half(j)], context_sum[:, half(j)], S[0][0:D, half(j)],
                                                ALU.mult)\
                                    .then_inc(sem(f"{x}_context"), 1)

                    def values_lo(x, width, group):
                        dve.wait_ge(sem(f"{x}_v_hi"), 4)
                        for hh in range(H):
                            src = C[0][:, 0:NC * width].rearrange("p (c d) -> p c d", d=width)
                            g = group(hh)
                            v.tensor_tensor(v_pad[:, :, hh, D + hh * DH:D + (hh + 1) * DH],
                                            src[:, :, g * DH:(g + 1) * DH],
                                            f(v_pad[:, :, hh, hh * DH:(hh + 1) * DH]), ALU.subtract)\
                                .then_inc(sem(f"{x}_v_lo"), 1)

                    def e_bcast(ap):
                        return ap.rearrange("p (c o) -> p c o", o=1).to_broadcast([P, NC, E])

                    def top_two(score, one, other, mask):
                        rank = first_key[:].rearrange("p (o e) -> p o e", o=1).to_broadcast([P, NC, E])
                        for dst, src in ((mask, score), (one, other)):
                            step(v.tensor_reduce(gs[:, 1], src, X, ALU.max))
                            step(v.tensor_tensor(dst, src, e_bcast(gs[:, 1]), ALU.is_equal))
                            step(v.tensor_tensor(dst, dst, rank, ALU.mult))
                            step(v.tensor_reduce(gs[:, 1], dst, X, ALU.max))
                            step(v.tensor_tensor(dst, dst, e_bcast(gs[:, 1]), ALU.is_equal))
                            if src is score:
                                step(v.tensor_copy(other, score))
                                step(v.copy_predicated(other, mask.bitcast(U32), lowest[:]))
                        step(v.tensor_tensor(mask, mask, one, ALU.add))

                    def weigh(name, j, c):
                        n = 4 * j + c
                        dve.wait_ge(sem(f"{name}_down"), n + 1)
                        g = gates[:, n, :].rearrange("p (e o) -> p e o", o=1).to_broadcast([P, E, D])
                        v.tensor_tensor(work[:, 0:HALF].rearrange("p (e d) -> p e d", d=D),
                                        R[n % 2][:].rearrange("p (e d) -> p e d", d=D), g, ALU.mult)\
                            .then_inc(sem(f"{name}_weighted"), 1)
                        dve.wait_ge(sem(f"{name}_weighted"), n + 1)
                        step(v.tensor_reduce(mix[:, n, :], work[:, 0:HALF].rearrange("p (e d) -> p d e", d=D),
                                             X, ALU.add))

                    dve.wait_ge(sem("A_q_hi"), 1)
                    v.tensor_tensor(a_q_lo, S[0][:], f(a_q_hi), ALU.subtract).then_inc(sem("A_split"), 1)
                    dve.wait_ge(sem("A_k_hi"), 1)
                    v.scalar_tensor_tensor(a_keys, f(a_k_hi), parts[:, 0:1], S[1][:], ALU.mult, ALU.add)\
                        .then_inc(sem("A_split"), 1)
                    for s in range(NC):
                        dve.wait_ge(sem("A_scores"), s + 1)
                        if s >= 2:
                            dve.wait_ge(sem("A_products"), s - 1)
                        v.tensor_tensor(probs[:, 0, s % 2, :], S[s % 2][:], gate[s], ALU.mult)\
                            .then_inc(sem("A_gated"), 1)
                    dve.wait_ge(sem("A_out"), 1)
                    y = R[1][:]
                    step(v.tensor_scalar(toks(sq[:]), y, 0.0, prelu[:, 0:1], ALU.min, ALU.mult))
                    step(v.scalar_tensor_tensor(toks(h[:]), y, 0.0, toks(sq[:]), ALU.max, ALU.add))
                    center(h[:])
                    power(3, v.tensor_scalar(st[:, 4], st[:, 3], 1e-5, None, ALU.add))
                    step(v.tensor_tensor(st[:, 3], st[:, 3], st[:, 1], ALU.mult))
                    scaled(xn[:], xc[:], 3).then_inc(sem("B_xn"), 1)

                    values_lo("B", D, lambda hh: hh)

                    def prepare_b(hh, k):
                        b, j, what = hh % 2, k // 4, k % 4
                        bank, cols, done = R[AB.slot[("P", hh, k)] % 2], half(k // 4), sem("B_prep_dve")
                        at = 12 * hh + 6 * j
                        dve.wait_ge(sem("B_prep"), PREP * hh + k + 1)
                        if what == 0:
                            if at:
                                dve.wait_ge(done, at)
                            v.tensor_tensor(cosb[:, 0, cols], bank[:], rot_cos[:, cols], ALU.mult).then_inc(done, 1)
                        elif what == 1:
                            v.tensor_tensor(cosb[:, 1, cols], bank[:], rot_sin[:, cols], ALU.mult).then_inc(done, 1)
                            dve.wait_ge(done, at + 2)
                            if at >= 12:
                                dve.wait_ge(sem("B_prep_act"), 8 * hh + 4 * j - 6)
                            v.tensor_tensor(work[:, cols], cosb[:, 0, cols], cosb[:, 1, cols], ALU.add).then_inc(done, 1)
                        elif what == 2:
                            dve.wait_ge(sem("B_prep_act"), 8 * hh + 4 * j + 3)
                            v.scalar_tensor_tensor(q2[D:P, b, cols], f(rounded[D:P, 1, :]), parts[D:P, 1:2], bank[D:P, :],
                                                   ALU.mult, ALU.add).then_inc(done, 1)
                        else:
                            dve.wait_ge(sem("B_prep_act"), 8 * hh + 4 * j + 4)
                            v.scalar_tensor_tensor(k2[D:P, b, cols], f(rounded[0:D, 1, :]), parts[0:D, 2:3], bank[D:P, :],
                                                   ALU.mult, ALU.add).then_inc(done, 1)
                            v.tensor_tensor(q1[D:P, b, cols], work[D:P, cols], f(rounded[D:P, 0, :]), ALU.subtract)\
                                .then_inc(done, 1)

                    for kind, x, j in AB.steps:
                        if kind == "P":
                            prepare_b(x, j)
                        elif kind == "F":
                            i, k = x % NC, AB.slot[("F", x, 0)]
                            w = min(P + 1, T - i * P)
                            dve.wait_ge(AB.s("scores"), x + 1)
                            v.copy_predicated(S[x % 2][:, i * P:i * P + w], late_mask[:, 0:w], R[k % 2][:, 0:w])\
                                .then_inc(AB.s("fixed"), 1)
                            dve.wait_ge(AB.s("fixed"), 2 * x + 1)
                            v.copy_predicated(S[x % 2][:, i * P:i * P + w], next_mask[:, 0:w],
                                              R[k % 2][:, 256:256 + w]).then_inc(AB.s("fixed"), 1)
                            dve.wait_ge(AB.s("fixed"), 2 * x + 2)
                            row_max(AB, x, T)
                        elif kind == "T":
                            AB.take_lo(dve, x, j)
                    normalise("B")
                    dve.wait_ge(sem("B_out"), 1)
                    step(v.tensor_tensor(toks(h[:]), R[0][:], toks(h[:]), ALU.add))
                    center(h[:])
                    step(scaled(f_tok[:], xc[:], 1))
                    power(3, v.tensor_scalar(st[:, 4], st[:, 3], 1e-6, None, ALU.add))
                    scaled(xn[:], f_tok[:], 3).then_inc(sem("C_xn"), 1)
                    a, b = cosb[:, 0, :], cosb[:, 1, :]
                    rope, n_rope = sem("C_rope"), 0
                    for k in range(3):
                        for dst, table, banks in ((a, rope_cos, R if k == 1 else S[0]), (b, rope_sin, C if k == 1 else S[1])):
                            dve.wait_ge(sem("C_proj"), 2 * k + (1 if dst is a else 2))
                            if dst is a and k:
                                dve.wait_ge(rope, n_rope)
                            if k == 1:
                                for j in range(2):
                                    v.tensor_tensor(dst[:, half(j)], banks[j][:], table[:, half(j)], ALU.mult)\
                                        .then_inc(rope, 1)
                            else:
                                v.tensor_tensor(dst, banks[:], table[:], ALU.mult).then_inc(rope, 1)
                            n_rope += 2 if k == 1 else 1
                        dve.wait_ge(rope, n_rope)
                        v.tensor_tensor(work[:], a, b, ALU.add).then_inc(rope, 1)
                        dve.wait_ge(sem("C_rounded"), k + 1)
                        v.scalar_tensor_tensor(c_stack[k], f(stack_a[:, k * T:(k + 1) * T]), parts[:, 2 if k == 2 else 1:3 if k == 2 else 2],
                                               work[:], ALU.mult, ALU.add).then_inc(rope, 1)
                        n_rope += 2
                    values_lo("C", 2 * DH, lambda hh: hh // 2)
                    for kind, x, j in AC.steps:
                        if kind == "S":
                            dve.wait_ge(AC.s("scores"), x + 1)
                            row_max(AC, x, (x % NC + 1) * P)
                        elif kind == "T":
                            AC.take_lo(dve, x, j)
                    normalise("C")
                    dve.wait_ge(sem("C_out"), 1)
                    step(v.tensor_tensor(toks(f_tok[:]), R[0][:], toks(f_tok[:]), ALU.add))
                    mean_square(f_tok)
                    power(3, v.tensor_scalar(st[:, 4], st[:, 0], 1e-6, None, ALU.add))
                    scaled(xn[:], f_tok[:], 3).then_inc(sem("M_xn"), 1)
                    dve.wait_ge(sem("M_logits"), 1)
                    v.tensor_copy(gl[:, 0], R[0][:, 0:NC * E].rearrange("p (c e) -> p c e", e=E))\
                        .then_inc(sem("M_logits_read"), 1)
                    dve.wait_ge(sem("M_logits_read"), 1)
                    step(v.tensor_reduce(gs[:, 0], gl[:, 0], X, ALU.max))
                    v.tensor_tensor(gl[:, 1], gl[:, 0], e_bcast(gs[:, 0]), ALU.subtract).then_inc(sem("M_shifted"), 1)
                    dve.wait_ge(sem("M_exp"), 1)
                    step(v.tensor_reduce(gs[:, 0], gl[:, 1], X, ALU.add))
                    step(v.reciprocal(gs[:, 0], gs[:, 0]))
                    step(v.tensor_tensor(gl[:, 0], gl[:, 1], e_bcast(gs[:, 0]), ALU.mult))
                    top_two(gl[:, 0], gl[:, 2], gl[:, 3], gl[:, 4])
                    step(v.tensor_tensor(gates[:], gl[:, 0], gl[:, 4], ALU.mult))
                    step(v.tensor_reduce(gs[:, 0], gates[:], X, ALU.add))
                    step(v.tensor_scalar(gs[:, 0], gs[:, 0], 1e-9, None, ALU.add))
                    step(v.reciprocal(gs[:, 0], gs[:, 0]))
                    step(v.tensor_tensor(gates[:], gates[:], e_bcast(gs[:, 0]), ALU.mult))
                    for j in range(2):
                        for q in range(NQ):
                            n = NQ * j + q
                            dve.wait_ge(sem("M_silu"), n + 1)
                            dve.wait_ge(sem("M_up"), n + 1)
                            if n == NQ:
                                dve.wait_ge(sem("M_down"), 4)
                            v.tensor_tensor(hid[:, q, :], S[n % 2][:, half(1)], silu[:, n % 2, :], ALU.mult)\
                                .then_inc(sem("M_hidden"), 1)
                        for c in range(4):
                            weigh("M", j, c)
                    step(v.tensor_tensor(h[:], h[:], f_tok[:], ALU.add))
                    step(v.tensor_tensor(h[:], h[:], mix[:], ALU.add))
                    center(h[:])
                    scaled(f_tok[:], xc[:], 1).then_inc(sem("D_x"), 1)
                    dve.wait_ge(sem("D_x"), 1)
                    power(3, v.tensor_scalar(st[:, 4], st[:, 3], float(D), None, ALU.mult))
                    step(v.tensor_scalar(st[:, 3], st[:, 3], 1e-12, None, ALU.max))
                    step(v.reciprocal(st[:, 3], st[:, 3]))
                    twice = work[:].rearrange("p (c r d) -> p c r d", c=NC, r=2)
                    for r in range(2):
                        scaled(twice[:, :, r, :], f_tok[:], 3).then_inc(sem("D_unit_x"), 1)
                    dve.wait_ge(sem("D_v_hi"), 1)
                    v.tensor_tensor(v_d[:, :, D:P], R[0][:].rearrange("p (c d) -> p c d", d=D), f(v_d[:, :, 0:D]),
                                    ALU.subtract).then_inc(sem("D_v_lo"), 1)
                    dve.wait_ge(sem("D_unit_hi"), 1)
                    v.tensor_tensor(d_lo, S[0][:], f(d_hi), ALU.subtract).then_inc(sem("D_unit_split"), 1)
                    v.scalar_tensor_tensor(d_stack, f(d_hi), parts[:, 0:1], S[0][:], ALU.mult, ALU.add)\
                        .then_inc(sem("D_unit_split"), 1)
                    pending = list(AD.steps)

                    def until_scores(n):
                        while pending and pending[0] != ("S", n, 0):
                            kind, x, j = pending.pop(0)
                            if kind == "T":
                                AD.take_lo(dve, x, j)
                        if pending:
                            pending.pop(0)

                    for n in range(NC):
                        until_scores(n)
                        dve.wait_ge(AD.s("scores_used"), n + 1)
                        src = cosb[:, n % 2, :]
                        for r in range(TOPK // 8):
                            step(v.max(top8[:], src if r == 0 else work[:]))
                            step(v.match_replace(work[:], top8[:], src if r == 0 else work[:], TAKEN))
                        v.scalar_tensor_tensor(probs[:, n // 4, n % 4, :], work[:], TAKEN, src,
                                               ALU.is_equal, ALU.mult).then_inc(AD.s("sparse"), 1)
                    until_scores(None)
                    normalise("D")
                    dve.wait_ge(sem("D_by_token"), 1)
                    step(v.tensor_tensor(sq[:], S[0][:, 0:HALF].rearrange("p (c d) -> p c d", d=D),
                                         over_features(rsum[:, 0:NC]), ALU.mult))
                    step(v.tensor_tensor(h[:], h[:], sq[:], ALU.add))
                    center(h[:])
                    scaled(f_tok[:], xc[:], 1).then_inc(sem("E_x"), 1)
                    dve.wait_ge(sem("E_logits"), 1)
                    v.tensor_copy(gl[:, 0], R[0][:, 0:NC * E].rearrange("p (c e) -> p c e", e=E))\
                        .then_inc(sem("E_logits_read"), 1)
                    dve.wait_ge(sem("E_logits_read"), 1)
                    step(v.tensor_reduce(gs[:, 0], gl[:, 0], X, ALU.max))
                    v.tensor_tensor(gl[:, 1], gl[:, 0], e_bcast(gs[:, 0]), ALU.subtract).then_inc(sem("E_shifted"), 1)
                    top_two(gl[:, 0], gl[:, 2], gl[:, 3], gl[:, 4])
                    dve.wait_ge(sem("E_exp"), 1)
                    step(v.tensor_tensor(gates[:], gl[:, 1], gl[:, 4], ALU.mult))
                    step(v.tensor_reduce(gs[:, 0], gates[:], X, ALU.add))
                    step(v.reciprocal(gs[:, 0], gs[:, 0]))
                    step(v.tensor_tensor(gates[:], gates[:], e_bcast(gs[:, 0]), ALU.mult))
                    for j in range(2):
                        for c in range(4):
                            weigh("E", j, c)
                    v.tensor_tensor(h[:], h[:], mix[:], ALU.add).then_inc(sem("result"), 1)

            for name in sems:
                if name not in setup_sems:
                    nc.gpsimd.sem_clear(sems[name])
            nc.all_engine_barrier()


def tables():
    div = np.exp(np.arange(0, D, 2, dtype=np.float32) * np.float32(-np.log(10000.0) / D)).astype(np.float64)
    pos = np.arange(T, dtype=np.float64)
    angle = div[:, None] * pos
    pe_early, pe_late = (np.concatenate([np.sin(a), np.cos(a)]) for a in (angle, div[:, None] * (pos - T)))
    turn = div[:, None] * (T - 1 - pos)
    rot_cos = np.concatenate([np.cos(turn)] * 4)
    rot_sin = np.concatenate([-np.sin(turn), np.sin(turn)] * 2)
    inv = 1.0 / 10000.0 ** (np.arange(0, DH, 2, dtype=np.float32) / DH)
    freqs = np.outer(np.arange(T, dtype=np.float32), inv)
    c, s = np.cos(freqs).T, np.sin(freqs).T
    rope_cos, rope_sin = np.concatenate([c, c] * 2 * DUP), np.concatenate([-s, s] * 2 * DUP)
    i, j = np.arange(P)[:, None], np.arange(P + 1)
    bf16 = mybir.dt.np(BF16)
    copy = np.arange(P) % D // DH
    parts = -np.stack([np.arange(P) >= D, copy % 2 == 1, copy >= 2], axis=1).astype(np.float32)
    f32 = lambda a: np.ascontiguousarray(a, dtype=np.float32)
    return {"pe_early": f32(pe_early), "pe_late": f32(pe_late), "rot_cos": f32(rot_cos), "rot_sin": f32(rot_sin), "rope_cos": f32(rope_cos),
            "rope_sin": f32(rope_sin), "identity": np.eye(P, dtype=np.float32),
            "late_mask": (j >= i + 2).astype(np.int32), "next_mask": (j == i + 1).astype(np.int32),
            "future": np.where(j[:P] > i, -1e30, 0.0).astype(bf16), "parts": f32(parts)}


def laid_out(inp):
    a = {k: np.asarray(v) for k, v in inp.items()}
    L = "L0_attn_"
    pos_t = a[L + "Wpos"].T
    sin_rows, cos_rows = pos_t[:, 0::2], pos_t[:, 1::2]
    r = {"xT": a["x"].reshape(B, T, D).transpose(0, 2, 1), "gateT": a["L0_tok_d_gamma_batched"].T,
         "prelu_a": a["L0_tok_prelu_a"].reshape(1, 1),
         "WqT": a[L + "Wq"].T, "WposT": np.stack([np.concatenate([sin_rows, cos_rows], 1),
                                                 np.concatenate([cos_rows, sin_rows], 1)]),
         "v_bias": a[L + "v_bias"].T,
         "W_D": a["L1_attn_W"].T, "b_D": a["L1_attn_b"]}
    for n in ("Wq", "bq", "Wk", "bk", "Wv", "bv", "Wo", "bo"):
        r["tok_" + n] = a["L0_tok_" + n]
    for n in ("ln_gamma", "ln_beta", "Wq", "bq", "Wk", "bk", "Wv", "bv", "u_bias", "Wout", "bout"):
        r[n] = a[L + n]
    for n in ("wq", "wk", "wv", "wo"):
        r[n + "T"] = a["L0_ffn_" + n].T
    r["routerT"] = a["L0_ffn_router_w"].T
    for n in ("w1", "w2", "w3"):
        r[n + "T"] = a["L0_ffn_" + n].transpose(0, 2, 1)
    for n in ("ln1_w", "ln2_w"):
        r[n] = a["L0_ffn_" + n]
    for n in ("Wg", "bg", "W1", "b1", "W2", "b2"):
        r[n] = a["L1_ffn_" + n]
    r.update(tables())
    return {n: np.ascontiguousarray(r[n]) for n in INPUTS}


def kernel(**inputs):
    from concourse import bacc, bass_utils

    nc = bacc.Bacc("TRN2", target_bir_lowering=False, num_devices=1)
    arrays, aps = {}, {}
    for name, a in laid_out(inputs).items():
        arrays[f"in_{name}"] = a
        aps[name] = nc.dram_tensor(f"in_{name}", a.shape, mybir.dt.from_np(a.dtype), kind="ExternalInput").ap()
    out = nc.dram_tensor("out", (B, T, D), F32, kind="ExternalOutput").ap()
    build(nc, aps, out)
    r = bass_utils.run_bass_kernel_spmd(nc, [arrays], core_ids=[0])
    return r.results[0]["out"]
```

```python
from contextlib import ExitStack

import numpy as np

import concourse.bass as bass
from concourse import mybir
from concourse.alu_op_type import AluOpType as ALU

F32 = mybir.dt.float32
F32R = mybir.dt.float32r
BF16 = mybir.dt.bfloat16
F16 = mybir.dt.float16
I32 = mybir.dt.int32
U32 = mybir.dt.uint32
ACT = mybir.ActivationFunctionType
X = mybir.AxisListType.X

P = 128
B, T, D = 4, 1024, 64
NC = T // P
HALF = 512
H, DH = 4, 16
E = 8
HID = int(8 / 3 * D)
REST = HID - P
NQ = E + E // 2
GH = 256
NG = E * GH // P
TOPK = 64
DUP = D // DH
PREP = 3
PREP_AFTER = [0, 1, 4]
SPLIT = 3
COUNTS = 6
WANTED, SLACK = 60, 3
FIRST_CUT = 1.55
SLOPE = 130.0
BY_VECTOR = 5
TOP_ORDER = [0, 1, 5, 2, 6, 3, 7, 4]
TAKEN = -3.0

SWIGLU_POWER, SEARCH_POWER = 4, 7
POWERS = [(1, 0), (3, 0), (1, 0), (3, 0), (3, 0), (1, 0), (3, 1), (5, 1), (1, 0)]

INPUTS = ["xT", "gateT", "tok_Wq", "tok_bq", "tok_Wk", "tok_bk", "tok_Wv", "tok_bv", "tok_Wo", "tok_bo", "prelu_a",
          "ln_gamma", "ln_beta", "Wq", "WqT", "bq", "Wk", "bk", "Wv", "bv", "WposT", "u_bias", "v_bias", "Wout",
          "bout", "ln1_w", "ln2_w", "wqT", "wkT", "wvT", "woT", "routerT", "w1T", "w2T", "w3T",
          "W_D", "b_D", "Wg", "bg", "W1", "b1", "W2", "b2",
          "pe_early", "pe_late", "rot_cos", "rot_sin", "rope_cos", "rope_sin", "identity", "late_mask", "next_mask", "future",
          "parts", "gate_rows"]


def attend_steps(groups, last_chunk, fix=False, prep=False):
    steps = [("P", 0, k) for k in range(PREP)] if prep else []
    waiting = []

    def product():
        if len(waiting) == SPLIT:
            steps.append(("AV",) + waiting.pop(0))

    for g in range(groups + 1):
        todo = [(g - 1, j) for j in range(last_chunk(g - 1) + 1)] if g else []
        for a in range(4):
            if g < groups:
                steps.append(("S", 4 * g + a, 0))
                product()
                if fix:
                    steps.append(("F", 4 * g + a, 0))
            for t in todo[len(todo) * a // 4:len(todo) * (a + 1) // 4]:
                product()
                steps.append(("T",) + t)
                waiting.append(t)
            if prep and g // 2 + 1 < groups // 2 and 4 * (g % 2) + a in PREP_AFTER:
                steps.append(("P", g // 2 + 1, PREP_AFTER.index(4 * (g % 2) + a)))
    return steps + [("AV",) + t for t in waiting]


def build(nc, t, out):
    with ExitStack() as ctx:
        def sb(name, shape, dt=F32):
            return ctx.enter_context(nc.sbuf_tensor(name, shape, dt))

        sems = {}

        def sem(name):
            if name not in sems:
                sems[name] = ctx.enter_context(nc.semaphore(name))
            return sems[name]

        turn_cos, turn_sin = sb("turn_cos", [P, T]), sb("turn_sin", [P, T])
        ident = sb("ident", [P, P])
        ident_bf = sb("ident_bf", [P, P], BF16)
        future = sb("future_sb", [P, P], BF16)
        late_mask, next_mask = sb("late_mask_sb", [P, P + 1], I32), sb("next_mask_sb", [P, P + 1], I32)
        parts = sb("parts_sb", [P, 3])
        tok_w = {n: sb("tok_w" + n, [D + 1, 2 * D if n in "qk" else D]) for n in "qkvo"}
        prelu = sb("prelu", [P, 1])
        affine = sb("affine", [D, 4])
        posw = sb("posw", [D + 1, H, 4 * D])
        qkw = sb("qkw", [D + 1, H, 2, D])
        wv_b, wout_b = sb("wv_b", [D + 1, D]), sb("wout_b", [D + 1, D])
        qk_c = sb("qk_c", [D, 3, 2, P])
        wv_c, wo_c = sb("wv_c", [D, 2 * DH]), sb("wo_c", [D, D])
        router = sb("router", [D, E])
        w_d, wg_e = sb("w_d", [D + 1, D]), sb("wg_e", [D + 1, E])
        b1e, b2e = sb("b1e", [P, NG]), sb("b2e", [E, D])
        region = sb("region", [P, 2 * NQ * P + 3 * NQ * P], F32R)
        LO, HI = slice(0, 2 * NQ * P), slice(2 * NQ * P, 5 * NQ * P)
        m_lo = region[0:D, LO].rearrange("p (w q n) -> p w q n", w=2, q=NQ)
        m_hi = region[:, HI][:, 0:2 * NQ * P].rearrange("p (w q n) -> p w q n", w=2, q=NQ)
        m_down = region[:, HI][:, 2 * NQ * P:3 * NQ * P].rearrange("p (q n) -> p q n", q=NQ)
        e_lo = region[0:D, 0:NG * P].rearrange("p (q n) -> p q n", q=NG)
        e_hi = region[:, HI][:, 0:NG * P].rearrange("p (q n) -> p q n", q=NG)
        e_down = region[:, HI][:, NG * P:2 * NG * P].rearrange("p (q n) -> p q n", q=NG)
        gate_rows = region[D:P, 0:NQ * P].rearrange("p (q n) -> p q n", q=NQ)
        kept = {n: nc.dram_tensor(f"kept_{n}", shape, F32, kind="Internal").ap() for n, shape in
                (("m_lo", (D, 2 * NQ * P)), ("m_hi", (P, 3 * NQ * P)), ("e_lo", (D, NG * P)), ("e_hi", (P, 2 * NG * P)))}
        exponents = sb("exponents", [P, 2, NC])
        lowest = sb("lowest", [P, NC, E])
        first_key = sb("first_key", [P, E])

        fm = sb("fm", [D + 1, T])
        fm2 = sb("fm2", [D + 1, T])
        context_sum = sb("context_sum", [D, T])
        v_tok = sb("v_tok", [P, NC, D])
        v_d = sb("v_d", [P, NC, P], F32R)
        v_pad = sb("v_pad", [P, NC, H, P], F32R)
        base = -(-nc.sbuf_base // 32) * 32
        area = sb("area", [P, 6 * T + 8])
        assert nc.sbuf_base == base + 4 * (6 * T + 8)

        def at(name, offset, shape, dt=F32R):
            return nc.alloc_sbuf_tensor_at(name, shape, dt, offset=base + 4 * offset)

        q1 = at("q1", 0, [P, 2, T + 1])
        q2 = at("q2", 2 * T + 8, [P, 2, T])
        q2_late = at("q2_late", 4 * T + 8, [P, 2, T])
        k1, k1_late = sb("k1", [P, T], F32R), sb("k1_late", [P, T], F32R)
        k2, k2_late = sb("k2", [P, 2, T], F32R), sb("k2_late", [P, 2, T], F32R)
        rounded_at = -(-nc.sbuf_base // 32) * 32
        rounded = sb("rounded", [P, 2, HALF], F32R)
        assert nc.sbuf_base == rounded_at + 8 * HALF
        probs = sb("probs", [P, 2, 4, T])
        probsT_at = -(-nc.sbuf_base // 32) * 32
        probsT = sb("probsT", [P, 2, SPLIT, HALF], F32R)
        assert nc.sbuf_base == probsT_at + 8 * SPLIT * HALF
        stack_a = probsT[:].rearrange("p a b t -> p (a b t)")
        big = probs[:].rearrange("p a b t -> p (a b t)")
        wqT_b = big[0:DH, 0:H * (D + 1)].rearrange("d (h m) -> d h m", h=H)
        wpos = big[0:DH, 512:512 + H * 4 * D].rearrange("d (h m) -> d h m", h=H)
        vb16 = big[0:DH, 2048:2048 + H]
        u_row = big[0:D + 1, 2560:2560 + D]
        pe_raw = big[:, 3072:3072 + 2 * T].rearrange("p (a t) -> p a t", a=2)
        qk_raw = big[0:D + 1, 5120 + D:5120 + 3 * D].rearrange("m (a n) -> m a n", a=2)
        wqk_raw = big[0:D, 5632:5632 + D + 2 * DH]
        activated, gated, hidden = (big[:, 3 * i * HALF:3 * (i + 1) * HALF].rearrange("p (b t) -> p b t", b=3)
                                    for i in range(3))
        cosb = sb("cosb", [P, 2, T])
        work = sb("work", [P, T])
        top8 = sb("top8", [P, NC, 8])
        cut = sb("cut", [P, 21, NC])
        repeat = sb("repeat", [1, 1], I32)
        nmax = sb("nmax", [P, 32])
        rsum = sb("rsum", [P, 32])
        h = sb("h", [P, NC, D])
        xc_at = -(-nc.sbuf_base // 32) * 32
        xc = sb("xc", [P, NC, D])
        sq = sb("sq", [P, NC, D])
        assert nc.sbuf_base == xc_at + 4 * 2 * NC * D
        f_tok = sb("f_tok", [P, NC, D])
        xn = xc
        st = sb("st", [P, 8, NC])
        gl = sb("gl", [P, 5, NC, E])
        gates = sb("gates", [P, NC, E])
        gs = sb("gs", [P, 3, NC])

        S = [ctx.enter_context(nc.psum_tensor(f"scores{i}", [P, T], F32)) for i in range(2)]
        R = [ctx.enter_context(nc.psum_tensor(f"ring{i}", [P, HALF], F32)) for i in range(2)]
        C = [ctx.enter_context(nc.psum_tensor(f"context{i}", [P, HALF], F32)) for i in range(2)]

        def f(ap):
            return ap.bitcast(F32)

        gate_a = nc.alloc_sbuf_tensor_at("gate_a", [P, 6, T], F32, offset=base)
        gate_raw = nc.alloc_sbuf_tensor_at("gate_raw", [P, 6 * T], F32, offset=base)
        gate = [gate_a[:, c, :] for c in range(6)] + [cosb[:, c, :] for c in range(2)]

        def load_gate(load):
            by_tile = t["gateT"].rearrange("(c p) t -> p c t", p=P)
            load(gate_a[:], by_tile[:, 0:6, :])
            load(cosb[:], by_tile[:, 6:8, :])

        a_q_hi, a_q_lo, a_keys = (stack_a[:, k * T:(k + 1) * T] for k in range(3))
        rounded_wide = rounded[:].rearrange("p a t -> p (a t)")
        a_k_hi = rounded_wide
        c_stack = q2[:, 0, :], q2[:, 1, :], q2_late[:, 0, :]
        d_hi, d_lo, d_stack = q1[:, 0, 0:T], q1[:, 1, 0:T], q2_late[:, 1, :]

        x_stack = rounded[:].rearrange("p a t -> p (a t)")
        gate_stack = v_d[D:P].rearrange("p c d -> p (c d)")
        raw = gate_raw[:]
        raw_up = raw[:, 0:2 * NQ * P]
        raw_down = raw[:, 2 * NQ * P:2 * NQ * P + NQ * D]
        raw_e = raw[:, 2 * NQ * P + NQ * D:2 * NQ * P + NQ * D + NG * P]
        raw_e_down = work[:]
        e_hi_made = big[:, 6 * T:6 * T + NG * P].bitcast(F32R)
        e_lo_made = stack_a[0:D, 0:NG * P]
        e_down_made = cosb[:].rearrange("p a t -> p (a t)").bitcast(F32R)

        halved_a = nc.alloc_sbuf_tensor_at("halved_a", [P, 4, T], F16, offset=base + 4 * (2 * T + 8))
        halved = [halved_a[:, n, :] for n in range(4)]
        halved += [cosb[:, n // 2, :].bitcast(F16)[:, n % 2 * T:(n % 2 + 1) * T] for n in range(4)]
        unread = nc.alloc_sbuf_tensor_at("unread", [P, 2 * SPLIT, T], F16, offset=probsT_at)
        below = [work[:], nc.alloc_sbuf_tensor_at("below", [P, T], F32, offset=rounded_at)[:]]
        spare = nc.alloc_sbuf_tensor_at("spare", [P, T], F32, offset=xc_at)
        sums, squares, count, seen, low, high, above, missed, edge_low, edge_high, slope, most, least = (
            cut[:, k, :] for k in range(13))
        threshold, inverse = ([cut[:, k + i, :] for i in range(2)] for k in (14, 16))
        chosen, beyond = cut[:, 18, :], cut[:, 19, :]
        all_rows = cut[:, 20, 0:1]

        def half(j):
            return slice(j * HALF, (j + 1) * HALF)

        def chunk(c):
            return slice(c * P, (c + 1) * P)

        def toks(ap):
            return ap.rearrange("p c d -> p (c d)")

        def over_features(ap):
            return ap.rearrange("p (c o) -> p c o", o=1).to_broadcast([P, NC, D])

        with nc.Block() as block:
            zeroed, loaded, made = sem("zeroed"), sem("loaded"), sem("made")
            fills = [(raw[:, 0:2 * NQ * P + NQ * D], 0.0), (f(v_pad[:]), 0.0)]
            fills += [(fm[D:D + 1, :], 1.0), (fm2[D:D + 1, :], 1.0)]
            fills += [(exponents[:, 0], -0.5), (exponents[:, 1], 0.5), (lowest[:], -3.0e38)]
            fills += [(first_key[:, e:e + 1], float(E - e)) for e in range(E)]

            @block.gpsimd
            def _(pool):
                for n, (where, value) in enumerate(fills):
                    if n:
                        pool.wait_ge(zeroed, n)
                    nc.gpsimd.memset(where, value).then_inc(zeroed, 1)

            up_parts = ((region[:, HI][:, 0:2 * NQ * P], raw_up, region[0:D, LO]), (e_hi_made, raw_e, e_lo_made))
            down_parts = ((region[:, HI][:, 2 * NQ * P:3 * NQ * P], raw_down), (e_down_made, raw_e_down))

            def both_halves(dst):
                b = dst.rearrange("p (q n) -> p q n", n=2 * D)
                return b[:, :, 0:D], b[:, :, D:2 * D]

            row = lambda ap: ap.rearrange("(o n) -> o n", o=1)
            col = lambda ap: ap.rearrange("(n o) -> n o", o=1)
            n_loads, n_weights = [0], [0]

            def loader(engine, signal, count):
                def load(dst, src):
                    count[0] += 1
                    engine.dma_start(dst, src, allow_slow_non_contiguous=True).then_inc(signal, 16)
                return load

            @block.sync
            def _(sp):
                load = loader(sp, sem("weights_loaded"), n_weights)
                for r in range(2):
                    load(raw_e[r * D:(r + 1) * D, :].rearrange("m (e n) -> m e n", e=E), t["W1"].rearrange("e m n -> m e n"))
                load(raw_e_down.rearrange("n (q m) -> n q m", q=NG), t["W2"].rearrange("e (q n) m -> n (e q) m", n=P))
                sp.wait_ge(zeroed, 1)
                for i, src in enumerate(("w1T", "w3T")):
                    w = t[src].rearrange("e m n -> m e n")
                    for r in range(2):
                        rows = raw_up[r * D:(r + 1) * D, i * NQ * P:(i + 1) * NQ * P].rearrange("m (q n) -> m q n", q=NQ)
                        load(rows[:, 0:E, :], w[:, :, 0:P])
                        for k in range(2):
                            load(rows[:, E:NQ, D * k:D * k + REST], w[:, k::2, P:HID])
                down = raw_down.rearrange("n (q m) -> n q m", q=NQ)
                load(down[:, 0:E, :], t["w2T"][:, 0:P, :].rearrange("e n m -> n e m"))
                for k in range(2):
                    load(down[D * k:D * k + REST, E:NQ, :], t["w2T"][k::2, P:HID, :].rearrange("e n m -> n e m"))
                load = loader(sp, loaded, n_loads)
                for i, n in enumerate(("ln_gamma", "ln_beta", "ln1_w", "ln2_w")):
                    load(affine[:, i:i + 1], col(t[n]))
                load(prelu[:], t["prelu_a"].to_broadcast([P, 1]))
                load(wv_b[0:D, :], t["Wv"])
                load(wv_b[D:D + 1, :], row(t["bv"]))
                load(wout_b[0:D, :], t["Wout"])
                load(wout_b[D:D + 1, :], row(t["bout"]))
                load(wv_c[:], t["wvT"])
                load(wo_c[:], t["woT"])
                load(router[:], t["routerT"])
                load(w_d[0:D, :], t["W_D"])
                load(w_d[D:D + 1, :], row(t["b_D"]))
                load(wg_e[0:D, :], t["Wg"])
                load(wg_e[D:D + 1, :], row(t["bg"]))
                load(b1e[:], t["b1"].rearrange("e (q n) -> n (e q)", n=P))
                load(b2e[:], t["b2"])
                sp.wait_ge(sem("weights_hi"), 4)
                sp.wait_ge(sem("weights_lo"), 4)
                for dst, src in ((kept["e_hi"][:, NG * P:2 * NG * P], e_down_made), (kept["m_lo"], region[0:D, LO]),
                                 (kept["m_hi"], region[:, HI]), (kept["e_lo"], e_lo_made), (kept["e_hi"][:, 0:NG * P], e_hi_made)):
                    sp.dma_start(dst, f(src)).then_inc(sem("kept"), 16)
                by_tile = t["gateT"].rearrange("(c p) t -> p c t", p=P)
                sp.dma_start(gate_a[:], by_tile[:, 0:6, :]).then_inc(sem("first_gate"), 16)
                sp.wait_ge(sem("kept"), 80)
                sp.dma_start(cosb[:], by_tile[:, 6:8, :]).then_inc(sem("first_gate"), 16)
                sp.wait_ge(sem("first_gate"), 32)

            @block.scalar
            def _(act):
                load = loader(act, loaded, n_loads)
                load(wqT_b[:, :, 0:D], t["WqT"].rearrange("(h d) m -> d h m", d=DH))
                load(wqT_b[:, :, D:D + 1], t["bq"].rearrange("(h d o) -> d h o", d=DH, o=1))
                load(vb16, t["v_bias"])
                pos = t["WposT"].rearrange("s (h d) m -> d h s m", d=DH)
                for s in range(4):
                    load(wpos[:, :, s * D:(s + 1) * D], pos[:, :, s // 2, :])
                for i, n in enumerate("qk"):
                    load(qk_raw[0:D, i, :], t["W" + n])
                    load(qk_raw[D:D + 1, i, :], row(t["b" + n]))
                load(u_row[D:D + 1, :], t["u_bias"].rearrange("(o h) d -> o (h d)", o=1))
                load(wqk_raw[:, 0:D], t["wqT"])
                load(wqk_raw[:, D:D + 2 * DH], t["wkT"])
                load(ident[:], t["identity"])
                load(late_mask[:], t["late_mask"])
                load(next_mask[:], t["next_mask"])
                load(future[:], t["future"])
                load(parts[:], t["parts"])
                load(big[D:P, 0:NQ * P], t["gate_rows"])
                for r in range(2):
                    load(pe_raw[r * D:(r + 1) * D, 0, :], t["pe_early"])
                    load(pe_raw[r * D:(r + 1) * D, 1, :], t["pe_late"])
                for n in "qkvo":
                    for r in range(2 if n in "qk" else 1):
                        load(tok_w[n][0:D, r * D:(r + 1) * D], t["tok_W" + n])
                        load(tok_w[n][D:D + 1, r * D:(r + 1) * D], row(t["tok_b" + n]))
                load(fm[0:D, :], t["xT"][0])
                act.wait_ge(sem("weights_loaded"), 16 * n_weights[0])
                for dst, src, _ in up_parts:
                    nc.scalar.activation(dst, src, ACT.Copy).then_inc(sem("weights_hi"), 1)
                for dst, src in down_parts:
                    nc.scalar.activation(both_halves(dst)[0], src.rearrange("p (q n) -> p q n", n=D), ACT.Copy)\
                        .then_inc(sem("weights_hi"), 1)
                act.dma_start(h[0:1, 0, 0:1], t["xT"][0, 0:1, 0:1]).then_inc(sem("stored"), 16)
                act.wait_ge(loaded, 16 * n_loads[0])

            @block.vector
            def _(dve):
                for i, (hi, src, lo) in enumerate(up_parts):
                    dve.wait_ge(sem("weights_hi"), i + 1)
                    nc.vector.tensor_tensor(lo, src[0:D, :], f(hi[0:D, :]), ALU.subtract).then_inc(sem("weights_lo"), 1)
                for i, (dst, src) in enumerate(down_parts):
                    hi, lo = both_halves(dst)
                    dve.wait_ge(sem("weights_hi"), i + 3)
                    nc.vector.tensor_tensor(lo, src.rearrange("p (q n) -> p q n", n=D), f(hi), ALU.subtract)\
                        .then_inc(sem("weights_lo"), 1)
                dve.wait_ge(loaded, 16 * n_loads[0])
                n = [0]

                def step(ins):
                    ins.then_inc(made, 1)
                    n[0] += 1
                    dve.wait_ge(made, n[0])

                bqv = wqT_b[:, :, D:D + 1].rearrange("d h o -> d (h o)")
                step(nc.vector.tensor_tensor(bqv, bqv, vb16, ALU.add))
                step(nc.vector.tensor_scalar(wqT_b[:], wqT_b[:], 0.125, None, ALU.mult))
                step(nc.vector.tensor_tensor(qk_raw[D:D + 1, 0, :], qk_raw[D:D + 1, 0, :], u_row[D:D + 1, :], ALU.add))
                step(nc.vector.tensor_scalar(qk_raw[:, 0, :], qk_raw[:, 0, :], 0.125, None, ALU.mult))
                for i in range(2):
                    nc.vector.tensor_copy(
                        qkw[:, :, i, :].rearrange("m h (k d) -> m h k d", k=DUP),
                        qk_raw[:, i, :].rearrange("m (h o d) -> m h o d", h=H, o=1).to_broadcast([D + 1, H, DUP, DH]))\
                        .then_inc(made, 1)
                    n[0] += 1
                dve.wait_ge(made, n[0])
                step(nc.vector.tensor_scalar(wqk_raw[:, 0:D], wqk_raw[:, 0:D], 0.25, None, ALU.mult))
                for k in range(3):
                    if k < 2:
                        src = wqk_raw[:, 0:D].rearrange("m (g t d) -> m t g d", g=2, t=2)[:, k]
                    else:
                        src = wqk_raw[:, D:D + 2 * DH].rearrange("m (g d) -> m g d", g=2)
                    src = src.rearrange("m g (o d) -> m g o d", o=1)
                    out_ = qk_c[:, k].rearrange("m x (g k d) -> m x g k d", g=2, k=DUP)
                    for x, d0, s0, w in ((0, 0, 0, DH), (1, 0, DH // 2, DH // 2), (1, DH // 2, 0, DH // 2)):
                        step(nc.vector.tensor_copy(out_[:, x, :, :, d0:d0 + w],
                                                   src[:, :, :, s0:s0 + w].to_broadcast([D, 2, DUP, w])))
                step(nc.vector.tensor_copy(ident_bf[:], ident[:]))
                step(nc.vector.tensor_copy(region[D:P, 0:NQ * P], big[D:P, 0:NQ * P]))
                for i, (hi, low) in enumerate(((k1, k2), (k1_late, k2_late))):
                    step(nc.vector.tensor_copy(hi[:], pe_raw[:, i, :]))
                    for b in range(2):
                        step(nc.vector.tensor_tensor(low[0:D, b, :], pe_raw[0:D, i, :], f(hi[0:D, :]), ALU.subtract))
                for hh in range(H):
                    dve.wait_ge(sem("posw_ready"), hh + 1)
                    nc.vector.tensor_copy(posw[:, hh, :], R[hh % 2][0:D + 1, 0:4 * D]).then_inc(sem("posw_copied"), 1)

            @block.tensor
            def _(pe):
                pe.wait_ge(made, 2)
                for hh in range(H):
                    if hh >= 2:
                        pe.wait_ge(sem("posw_copied"), hh - 1)
                    nc.tensor.matmul(R[hh % 2][0:D + 1, 0:4 * D], wqT_b[:, hh, :], wpos[:, hh, :],
                                     start=True, stop=True).then_inc(sem("posw_ready"), 1)

        class Attend:

            def __init__(self, name, groups, causal=False, prep=False):
                self.name, self.groups, self.causal = name, groups, causal
                self.scores_read = "scores_used" if name == "D" else "probs"
                self.steps = attend_steps(groups, lambda g: 4 * (g % 2) + 3 if causal else NC - 1, name == "B", prep)
                if name == "D":
                    self.steps.sort(key=lambda s: s[0] != "S")
                self.t_at = {s[1:]: i for i, s in enumerate(x for x in self.steps if x[0] == "T")}
                self.ring = [s for s in self.steps if s[0] in "TF"]
                self.slot = {s: k for k, s in enumerate(self.ring)}
                self.wide = [s for s in self.steps if s[0] in "SP"]
                self.turn = {s: k for k, s in enumerate(self.wide)}

            def s(self, what):
                return sem(f"{self.name}_{what}")

            def t_until(self, g):
                return sum(1 for (gg, j) in self.t_at if gg <= g)

            def wait_slot(self, eng, k):
                if k < 2:
                    return
                kind, x, j = self.ring[k - 2]
                if kind == "T":
                    eng.wait_ge(self.s("lo"), self.t_at[(x, j)] + 1)
                else:
                    eng.wait_ge(self.s("fixed"), 2 * x + 2)

            def wait_wide(self, eng, k):
                if k >= 2:
                    kind, x, j = self.wide[k - 2]
                    if kind == "S":
                        eng.wait_ge(self.s(self.scores_read), x + 1)
                    else:
                        eng.wait_ge(self.s("prep_dve"), 4 * x + (1, 2, 4)[j])

            def bank(self, *step):
                return S[self.turn[step] % 2]

            def width(self, x, j):
                return max(0, j - 4 * (x % 2)) * P if self.causal else 0

            def tensor(self, pe, scores, values, fix=None, prepare=None, after_scores=None):
                for kind, x, j in self.steps:
                    if after_scores and (kind, x, j) == ("T", 0, 0):
                        after_scores()
                    if kind == "P":
                        self.wait_wide(pe, self.turn[(kind, x, j)])
                        prepare(x, j, self.bank(kind, x, j)).then_inc(self.s("prep"), 1)
                    elif kind == "S":
                        self.wait_wide(pe, self.turn[(kind, x, j)])
                        ins = scores(x)
                        if fix is None:
                            ins.then_inc(self.s("scores"), 1)
                    elif kind == "F":
                        self.wait_slot(pe, self.slot[(kind, x, j)])
                        fix(x, R[self.slot[(kind, x, j)] % 2]).then_inc(self.s("scores"), 1)
                    elif kind == "T":
                        k, w = self.slot[(kind, x, j)], self.width(x, j)
                        if j == 0:
                            pe.wait_ge(self.s("probs"), 4 * x + 4)
                        self.wait_slot(pe, k)
                        for a in range(w // P, 4):
                            ins = nc.tensor.transpose(R[k % 2][:, chunk(a)], probs[:, x % 2, a, chunk(j)], ident[:])
                        ins.then_inc(self.s("turned"), 1)
                    else:
                        m, w = self.t_at[(x, j)], self.width(x, j)
                        last = 4 * (x % 2) + 3 if self.causal else NC - 1
                        pe.wait_ge(self.s("hi"), m + 1)
                        nc.tensor.matmul(C[x % 2][:, w:HALF], values(x, j), probsT[:, 0, m % SPLIT, w:HALF],
                                         start=(x < 2 and j == 0), stop=False, skip_group_check=True)
                        pe.wait_ge(self.s("lo"), m + 1)
                        nc.tensor.matmul(C[x % 2][:, w:HALF], values(x, j), probsT[:, 1, m % SPLIT, w:HALF], start=False,
                                         stop=(x >= self.groups - 2 and j == last),
                                         skip_group_check=True).then_inc(self.s("products"), 1)

            def take_hi(self, act, x, j):
                m, k, w = self.t_at[(x, j)], self.slot[("T", x, j)], self.width(x, j)
                act.wait_ge(self.s("turned"), m + 1)
                if m >= SPLIT:
                    act.wait_ge(self.s("products"), m - SPLIT + 1)
                nc.scalar.activation(probsT[:, 0, m % SPLIT, w:HALF], R[k % 2][:, w:HALF], ACT.Copy)\
                    .then_inc(self.s("hi"), 1)

            def take_lo(self, dve, x, j):
                m, k, w = self.t_at[(x, j)], self.slot[("T", x, j)], self.width(x, j)
                dve.wait_ge(self.s("hi"), m + 1)
                nc.vector.tensor_tensor(probsT[:, 1, m % SPLIT, w:HALF], R[k % 2][:, w:HALF],
                                        f(probsT[:, 0, m % SPLIT, w:HALF]), ALU.subtract).then_inc(self.s("lo"), 1)

            def n_products(self):
                return len(self.t_at)

        AB = Attend("B", 2 * H, prep=True)
        AC = Attend("C", 2 * H, causal=True)
        AD = Attend("D", 2)

        lasting = set(sems) | {"stored"}
        with nc.Fori(0, B) as seq:
            with nc.Block() as block:

                @block.sync
                def _(sp):
                    for dst, src in ((turn_cos, "rot_cos"), (turn_sin, "rot_sin")):
                        sp.dma_start(dst[:], t[src]).then_inc(sem("rot_loaded"), 16)
                    for dst, src in ((region[0:D, LO], "m_lo"), (region[:, HI], "m_hi")):
                        sp.dma_start(f(dst), kept[src]).then_inc(sem("M_loaded"), 16)
                    for hh in range(H):
                        b = hh % 2
                        copy = lambda dst, src: sp.dma_start(f(dst), f(src)).then_inc(sem("B_copied"), 16)
                        sp.wait_ge(sem("B_prep_act"), 3 * hh + 1)
                        copy(q2[0:D, b, :], q1[0:D, b, 0:T])
                        copy(q2_late[0:D, b, 0:T - 1], q1[0:D, b, 1:T])
                        sp.wait_ge(sem("B_prep_dve"), 4 * hh + 3)
                        copy(q2_late[D:P, b, :], q2[D:P, b, :])
                        sp.wait_ge(sem("B_prep_dve"), 4 * hh + 4)
                        copy(k2_late[D:P, b, :], k2[D:P, b, :])
                    for dst, src in ((turn_cos, "rope_cos"), (turn_sin, "rope_sin")):
                        sp.dma_start(dst[:], t[src]).then_inc(sem("rope_loaded"), 16)
                    sp.wait_ge(sem("M_down"), 2 * NQ)
                    for dst, src in ((region[0:D, 0:NG * P], "e_lo"), (region[:, HI][:, 0:2 * NG * P], "e_hi")):
                        sp.dma_start(f(dst), kept[src]).then_inc(sem("E_loaded"), 16)
                    sp.wait_ge(sem("E_logits"), 1)
                    sp.wait_ge(sem("E_x_lo"), 1)
                    sp.dma_start(fm[0:D, :], t["xT"][bass.ds(seq + 1, 1)].rearrange("o d t -> (o d) t"))\
                      .then_inc(sem("x_loaded"), 16)
                    sp.wait_ge(sem("D_products"), AD.n_products())
                    load_gate(lambda dst, src: sp.dma_start(dst, src).then_inc(sem("gate_loaded"), 16))
                    sp.wait_ge(sem("rot_loaded"), 32)
                    sp.wait_ge(sem("M_loaded"), 32)
                    sp.wait_ge(sem("rope_loaded"), 32)
                    sp.wait_ge(sem("E_loaded"), 32)
                    sp.wait_ge(sem("gate_loaded"), 32)
                    sp.wait_ge(sem("x_loaded"), 16)
                    sp.wait_ge(sem("result"), 1)
                    sp.dma_start(out[bass.ds(seq, 1)].rearrange("o (c p) d -> p (o c) d", p=P), h[:])\
                      .then_inc(sem("stored"), 16)

                @block.gpsimd
                def _(pool):
                    def hidden_lo(name, rounds):
                        for n in range(rounds):
                            pool.wait_ge(sem(f"{name}_hi"), n + 1)
                            if n:
                                pool.wait_ge(sem(f"{name}_lo"), n)
                            if n >= SPLIT:
                                pool.wait_ge(sem(f"{name}_down"), n - SPLIT + 1)
                            nc.gpsimd.tensor_tensor(probsT[:, 1, n % SPLIT, :], hidden[:, n % 3, :],
                                                    f(probsT[:, 0, n % SPLIT, :]), ALU.subtract)\
                                .then_inc(sem(f"{name}_lo"), 1)

                    for n, (k, p) in enumerate(POWERS):
                        if n == 1:
                            for i, pad in enumerate((f(q1[:, :, T:T + 1]), f(q2_late[0:D, :, T - 1:T]))):
                                if i:
                                    pool.wait_ge(sem("padded"), i)
                                nc.gpsimd.memset(pad, 0.0).then_inc(sem("padded"), 1)
                        pool.wait_ge(sem("power_base"), n + 1)
                        nc.gpsimd.tensor_tensor(st[:, k], st[:, 4], exponents[:, p], ALU.pow)\
                            .then_inc(sem("powered"), 1)
                        if n == 1:
                            turned = sem("B_prep_pool")
                            for hh in range(H):
                                pool.wait_ge(sem("B_prep_dve"), 4 * hh + 2)
                                if hh:
                                    pool.wait_ge(turned, 2 * hh)
                                    pool.wait_ge(sem("B_prep_act"), 3 * hh - 1)
                                nc.gpsimd.tensor_tensor(work[:], cosb[:, 0, :], cosb[:, 1, :], ALU.add).then_inc(turned, 1)
                                pool.wait_ge(turned, 2 * hh + 1)
                                pool.wait_ge(sem("B_prep_act"), 3 * hh + 2)
                                nc.gpsimd.tensor_tensor(q1[D:P, hh % 2, 0:T], work[D:P, :], f(rounded_wide[D:P, :]), ALU.subtract)\
                                    .then_inc(turned, 1)
                        if n == SEARCH_POWER:
                            for m in range(BY_VECTOR, NC):
                                pool.wait_ge(sem("D_signs"), (NC - BY_VECTOR) * (COUNTS - 1) + m - BY_VECTOR + 1)
                                if m > BY_VECTOR:
                                    pool.wait_ge(sem("D_top"), TOP_ORDER.index(m - 1) + 1)
                                nc.gpsimd.tensor_tensor(spare[:], unread[:, 3 + m - BY_VECTOR, :], probs[:, m // 4, m % 4, :],
                                                        ALU.mult).then_inc(sem("D_below"), 1)
                        for name, power, rounds in (("M", SWIGLU_POWER, 2 * NQ), ("E", len(POWERS) - 1, 2 * NG)):
                            if n == power:
                                if name == "E":
                                    pool.wait_ge(sem("D_products"), AD.n_products())
                                pool.wait_ge(sem("powered"), n + 1)
                                nc.gpsimd.memset(f(gate_stack), 0.0).then_inc(sem(f"{name}_cleared"), 1)
                                pool.wait_ge(sem(f"{name}_cleared"), 1)
                                hidden_lo(name, rounds)

                @block.tensor
                def _(pe):
                    mm = nc.tensor.matmul

                    def project(dst, w, src, k, done):
                        for j in range(2):
                            ins = mm(dst(j), w, src[0:k, half(j)], start=True, stop=True)
                        ins.then_inc(done, 1)

                    def by_token(dst, src, w, k, n, done):
                        for c in range(NC):
                            ins = mm(dst[:, c * n:(c + 1) * n], src[0:k, chunk(c)], w, start=True, stop=True)
                        ins.then_inc(done, 1)

                    def turn(src, done):
                        for c in range(NC):
                            ins = nc.tensor.transpose(S[0][0:D, chunk(c)], src[:, c, :], ident[:])
                        ins.then_inc(done, 1)

                    def normalise(x):
                        pe.wait_ge(sem(f"{x}_recip"), 1)
                        for i in range(NC):
                            ins = nc.tensor.transpose(S[0][0:D, chunk(i)], work[:, i * D:(i + 1) * D], ident[:])
                        ins.then_inc(sem(f"{x}_spread"), 1)

                    project(lambda j: S[0][:, half(j)], tok_w["q"][:], fm, D + 1, sem("A_q"))
                    project(lambda j: S[1][:, half(j)], tok_w["k"][:], fm, D + 1, sem("A_k"))
                    by_token(R[0], fm, tok_w["v"][:], D + 1, D, sem("A_v"))
                    pe.wait_ge(sem("A_q_hi"), 1)
                    pe.wait_ge(sem("A_split"), 2)
                    for s in range(NC + 1):
                        if s < NC:
                            if s >= 2:
                                pe.wait_ge(sem("A_gated"), s - 1)
                            for j in range(2):
                                mm(S[s % 2][:, half(j)], a_keys[:, chunk(s)], a_q_hi[:, half(j)],
                                   start=True, stop=False)
                                ins = mm(S[s % 2][:, half(j)], a_keys[:, chunk(s)], a_q_lo[:, half(j)],
                                         start=False, stop=True)
                            ins.then_inc(sem("A_scores"), 1)
                        if s >= 1:
                            pe.wait_ge(sem("A_gated"), s)
                            if s == 1:
                                pe.wait_ge(sem("A_v_copied"), 1)
                            for j in range(2):
                                ins = mm(C[j][0:D, :], v_tok[:, s - 1, :], probs[:, 0, (s - 1) % 2, half(j)],
                                         start=(s == 1), stop=(s == NC))
                            ins.then_inc(sem("A_products"), 1)
                    pe.wait_ge(sem("A_mix_copied"), 2)
                    by_token(R[1], fm2, tok_w["o"][:], D + 1, D, sem("A_out"))

                    pe.wait_ge(sem("normalised"), 1)
                    turn(xn, sem("x_turned"))
                    pe.wait_ge(sem("B_fm"), 1)
                    by_token(C[0], fm, wv_b[:], D + 1, D, sem("B_v"))

                    def prepare_b(hh, k, bank):
                        w = posw[:, hh, k * P:(k + 1) * P] if k < 2 else qkw[:, hh].rearrange("m a n -> m (a n)")
                        for j in range(2):
                            ins = mm(bank[:, half(j)], w, fm[:, half(j)], start=True, stop=True)
                        return ins

                    def late_scores(dst, b, i, j0, j1):
                        mm(dst, q1[:, b, i * P + 1:(i + 1) * P + 1], k1_late[:, j0:j1], start=True, stop=False,
                           skip_group_check=True)
                        return mm(dst, q2_late[:, b, chunk(i)], k2_late[:, b, j0:j1], start=False, stop=True,
                                  skip_group_check=True)

                    def scores_b(n):
                        hh, i = n // NC, n % NC
                        b, bank = hh % 2, AB.bank("S", n, 0)
                        if i == 0:
                            pe.wait_ge(sem("B_prep_dve"), 4 * (hh + 1))
                            pe.wait_ge(sem("B_prep_act"), 3 * (hh + 1))
                            pe.wait_ge(sem("B_prep_pool"), 2 * (hh + 1))
                            pe.wait_ge(sem("B_copied"), 64 * (hh + 1))
                        if n == 0:
                            pe.wait_ge(sem("padded"), 2)
                        edge = (i + 1) * P
                        for j0, j1 in ((0, min(edge, HALF)), (HALF, edge)):
                            if j1 > j0:
                                mm(bank[:, j0:j1], q1[:, b, chunk(i)], k1[:, j0:j1], start=True, stop=False,
                                   skip_group_check=True)
                                mm(bank[:, j0:j1], q2[:, b, chunk(i)], k2[:, b, j0:j1], start=False, stop=True,
                                   skip_group_check=True)
                        for j0, j1 in ((edge, HALF), (max(edge, HALF), T)):
                            if j1 > j0:
                                late_scores(bank[:, j0:j1], b, i, j0, j1)

                    def fix_b(n, bank):
                        hh, i = n // NC, n % NC
                        b, j1 = hh % 2, min((i + 1) * P + 2, T)
                        late_scores(bank[:, 0:j1 - i * P], b, i, i * P, j1)
                        return mm(bank[:, 256:256 + j1 - i * P], q2[D:P, b, chunk(i)], k2[D:P, b, i * P:j1],
                                  start=True, stop=True, skip_group_check=True)

                    pe.wait_ge(sem("B_v_hi"), 4)
                    pe.wait_ge(sem("B_v_lo"), 4)
                    AB.tensor(pe, scores_b, lambda x, j: v_pad[:, j, x // 2, :], fix_b, prepare_b)
                    normalise("B")
                    pe.wait_ge(sem("B_context"), 2)
                    by_token(R[0], fm2, wout_b[:], D + 1, D, sem("B_out"))

                    pe.wait_ge(sem("normalised"), 2)
                    turn(xn, sem("x_turned"))
                    pe.wait_ge(sem("C_fm"), 1)
                    for k in range(3):
                        if k == 2:
                            pe.wait_ge(sem("C_rope"), 2)
                        project(lambda j: (R[j][:] if k == 1 else S[0][:, half(j)]), qk_c[:, k, 0, :], fm, D,
                                sem("C_proj"))
                        project(lambda j: (C[j][:] if k == 1 else S[1][:, half(j)]), qk_c[:, k, 1, :], fm, D,
                                sem("C_proj"))
                    pe.wait_ge(sem("C_rope"), 8)
                    by_token(C[0], fm, wv_c[:], D, 2 * DH, sem("C_v"))

                    def scores_c(n):
                        hh, i = n // NC, n % NC
                        rows, edge = slice(D * (hh // 2), D * (hh // 2) + D), (i + 1) * P
                        for j0, j1 in ((0, min(edge, HALF)), (HALF, edge)):
                            if j1 > j0:
                                mm(S[n % 2][:, j0:j1], c_stack[hh % 2][rows, chunk(i)], c_stack[2][rows, j0:j1],
                                   start=True, stop=False, skip_group_check=True)
                        return mm(S[n % 2][:, chunk(i)], ident_bf[:], future[:], start=False, stop=True,
                                  skip_group_check=True)

                    pe.wait_ge(sem("C_v_hi"), 4)
                    pe.wait_ge(sem("C_v_lo"), 4)
                    pe.wait_ge(sem("C_rope"), 14)
                    AC.tensor(pe, scores_c, lambda x, j: v_pad[:, j, x // 2, :])
                    normalise("C")
                    pe.wait_ge(sem("C_context"), 2)
                    by_token(R[0], fm2, wo_c[:], D, D, sem("C_out"))

                    pe.wait_ge(sem("normalised"), 3)
                    turn(xn, sem("x_turned"))
                    pe.wait_ge(sem("M_fm"), 2)
                    by_token(R[0], fm, router[:], D, E, sem("M_logits"))

                    def spread_gates(name):
                        pe.wait_ge(sem(f"{name}_gates"), 1)
                        for c in range(NC):
                            ins = nc.tensor.transpose(C[c // 4][0:E, chunk(c % 4)], gates[:, c, :], ident[:])
                        ins.then_inc(sem(f"{name}_gates_turned"), 1)

                    def spread(name, n, q, j):
                        mm(R[n % 2][:], gate_rows[:, q, :], gate_stack[:, half(j)], start=True, stop=True)\
                            .then_inc(sem(f"{name}_spread_gate"), 1)

                    def down(name, m, per_half, weights):
                        j, q = m // per_half, m % per_half
                        pe.wait_ge(sem(f"{name}_lo"), m + 1)
                        mm(C[j][:], weights[:, q, :], probsT[:, 0, m % SPLIT, :], start=(q == 0), stop=False,
                           skip_group_check=True)
                        if name == "E" and q == 0:
                            mm(C[j][0:D, :], b2e[:], fm2[0:E, half(j)], start=False, stop=False, skip_group_check=True)
                        mm(C[j][:], weights[:, q, :], probsT[:, 1, m % SPLIT, :], start=False,
                           stop=(q == per_half - 1), skip_group_check=True).then_inc(sem(f"{name}_down"), 1)

                    def up(bank, lo, hi, j):
                        mm(bank, hi, x_stack[:, half(j)], start=True, stop=False)
                        return mm(bank, lo, x_stack[0:D, half(j)], start=False, stop=True)

                    def sum_by_token(name):
                        for j in range(2):
                            pe.wait_ge(sem(f"{name}_summed"), j + 1)
                            for c in range(4 * j, 4 * j + 4):
                                ins = nc.tensor.transpose(S[0][:, c * D:(c + 1) * D], context_sum[:, chunk(c)], ident[0:D, 0:D])
                        ins.then_inc(sem(f"{name}_by_token"), 1)

                    def gate_and_up(n):
                        if n >= 2:
                            pe.wait_ge(sem("M_hidden"), n - 1)
                        for w, done in enumerate((sem("M_gate"), sem("M_up"))):
                            up(S[n % 2][:, half(w)], m_lo[:, w, n % NQ, :], m_hi[:, w, n % NQ, :], n // NQ).then_inc(done, 1)

                    pe.wait_ge(sem("M_x_lo"), 1)
                    pe.wait_ge(sem("M_loaded"), 32)
                    gate_and_up(0)
                    gate_and_up(1)
                    spread_gates("M")
                    pe.wait_ge(sem("M_gates_lo"), 2)
                    spread("M", 0, 0, 0)
                    for n in range(2 * NQ + SPLIT):
                        m = n + 1
                        if m < 2 * NQ:
                            if m >= 2:
                                pe.wait_ge(sem("M_gated"), m - 1)
                            spread("M", m, m % NQ, m // NQ)
                        if n >= SPLIT:
                            down("M", n - SPLIT, NQ, m_down)
                        if n + 2 < 2 * NQ:
                            gate_and_up(n + 2)
                    sum_by_token("M")

                    pe.wait_ge(sem("normalised"), 4)
                    turn(f_tok, sem("x_turned"))
                    pe.wait_ge(sem("D_fm"), 1)
                    by_token(R[0], fm, w_d[:], D + 1, D, sem("D_v"))
                    pe.wait_ge(sem("D_unit_x"), 2)
                    for c in range(NC):
                        ins = nc.tensor.transpose(S[0][:, chunk(c)], work[:, chunk(c)], ident[:])
                    ins.then_inc(sem("D_turned_unit"), 1)
                    pe.wait_ge(sem("D_unit_split"), 2)
                    pe.wait_ge(sem("D_unit_hi"), 1)
                    pe.wait_ge(sem("D_v_hi"), 1)
                    pe.wait_ge(sem("D_v_lo"), 1)

                    def every_row():
                        pe.wait_ge(sem("D_ok"), 1)
                        mm(S[0][0:1, 0:1], all_rows, exponents[:, 1, 0:1], start=True, stop=True)\
                            .then_inc(sem("D_all_ok"), 1)

                    def scores_d(n):
                        for j in range(2):
                            mm(S[n % 2][:, half(j)], d_stack[:, chunk(n)], d_hi[:, half(j)], start=True, stop=False)
                            ins = mm(S[n % 2][:, half(j)], d_stack[:, chunk(n)], d_lo[:, half(j)],
                                     start=False, stop=True)
                        return ins

                    AD.tensor(pe, scores_d, lambda x, j: v_d[:, j, :], after_scores=every_row)
                    pe.wait_ge(sem("D_context"), 2)
                    for c in range(NC):
                        ins = nc.tensor.transpose(S[0][:, c * D:(c + 1) * D], context_sum[:, chunk(c)], ident[0:D, 0:D])
                    ins.then_inc(sem("D_by_token"), 1)

                    pe.wait_ge(sem("normalised"), 5)
                    turn(f_tok, sem("x_turned"))
                    pe.wait_ge(sem("E_fm"), 2)
                    by_token(R[0], fm, wg_e[:], D + 1, E, sem("E_logits"))

                    def up_e(n):
                        if n >= 4:
                            pe.wait_ge(sem("E_activated"), n - 3)
                        up(S[n // 2 % 2][:, half(n % 2)], e_lo[:, n % NG, :], e_hi[:, n % NG, :], n // NG)\
                            .then_inc(sem("E_up"), 1)

                    pe.wait_ge(sem("E_x_lo"), 1)
                    pe.wait_ge(sem("E_loaded"), 32)
                    for n in range(4):
                        up_e(n)
                    spread_gates("E")
                    pe.wait_ge(sem("E_gates_lo"), 2)
                    pe.wait_ge(sem("E_gates_copied"), 2)
                    for n in range(2 * NG + SPLIT):
                        if n < 2 * NG and n % 2 == 0:
                            if n >= 4:
                                pe.wait_ge(sem("E_hidden"), n - 2)
                            spread("E", n // 2, n // 2 % E, n // NG)
                        if n >= SPLIT:
                            down("E", n - SPLIT, NG, e_down)
                        if n + 4 < 2 * NG:
                            up_e(n + 4)
                    sum_by_token("E")

                @block.scalar
                def _(act):
                    fn = nc.scalar.activation

                    def copy(dst, src):
                        return fn(dst, src, ACT.Copy)

                    def softmax_of(att, width):
                        scored = []

                        def exponential():
                            if scored:
                                x = scored.pop()
                                g, a = x // 4, x % 4
                                act.wait_ge(att.s("max"), x + 1)
                                if g >= 2:
                                    act.wait_ge(att.s("turned"), att.t_until(g - 2))
                                w = width(x)
                                fn(probs[:, g % 2, a, 0:w], att.bank("S", x, 0)[:, 0:w], ACT.Exp, bias=nmax[:, x:x + 1],
                                   accum_out=rsum[:, x:x + 1])\
                                    .then_inc(att.s("probs"), 1)

                        for kind, x, j in att.steps:
                            if kind == "S":
                                exponential()
                                if att is AB and x % NC == 4:
                                    round_turned()
                                scored.append(x)
                            elif kind == "T":
                                if x == att.groups - 1:
                                    exponential()
                                att.take_hi(act, x, j)
                            elif kind == "P":
                                exponential()
                                prepare_b(x, j)

                    act.wait_ge(sem("A_q"), 1)
                    copy(a_q_hi, S[0][:]).then_inc(sem("A_q_hi"), 1)
                    act.wait_ge(sem("A_k"), 1)
                    copy(a_k_hi, S[1][:]).then_inc(sem("A_k_hi"), 1)
                    act.wait_ge(sem("A_v"), 1)
                    copy(toks(v_tok[:]), R[0][:]).then_inc(sem("A_v_copied"), 1)
                    act.wait_ge(sem("A_products"), NC)
                    for j in range(2):
                        copy(fm2[0:D, half(j)], C[j][0:D, :]).then_inc(sem("A_mix_copied"), 1)
                    act.wait_ge(sem("x_turned"), 1)
                    fn(fm[0:D, :], S[0][0:D, :], ACT.Identity, bias=affine[:, 1:2], scale=affine[:, 0:1])\
                        .then_inc(sem("B_fm"), 1)
                    act.wait_ge(sem("B_v"), 1)

                    def values_hi(x, width, group):
                        for hh in range(H):
                            src = C[0][:, 0:NC * width].rearrange("p (c d) -> p c d", d=width)
                            g = group(hh)
                            copy(v_pad[:, :, hh, hh * DH:(hh + 1) * DH], src[:, :, g * DH:(g + 1) * DH])\
                                .then_inc(sem(f"{x}_v_hi"), 1)

                    turned_due = []

                    def round_turned():
                        if turned_due:
                            hh = turned_due.pop()
                            act.wait_ge(sem("B_prep_pool"), 2 * hh + 1)
                            copy(q1[0:D, hh % 2, 0:T], work[0:D, :]).then_inc(sem("B_prep_act"), 1)
                            if hh:
                                act.wait_ge(sem("B_prep_dve"), 4 * hh)
                            copy(rounded_wide[D:P, :], work[D:P, :]).then_inc(sem("B_prep_act"), 1)

                    def prepare_b(hh, k):
                        if k == 1:
                            turned_due.append(hh)
                            if hh == 0:
                                round_turned()
                        elif k == 2:
                            act.wait_ge(sem("B_prep"), PREP * hh + k + 1)
                            act.wait_ge(sem("B_prep_pool"), 2 * hh + 2)
                            copy(rounded_wide, AB.bank("P", hh, k)[:]).then_inc(sem("B_prep_act"), 1)

                    values_hi("B", D, lambda hh: hh)
                    softmax_of(AB, lambda n: T)
                    def context(x):
                        act.wait_ge(sem(f"{x}_products"), {"B": AB, "C": AC, "D": AD}[x].n_products())
                        for j in range(2):
                            copy(context_sum[:, half(j)], C[j][D:P, :]).then_inc(sem(f"{x}_ctx_copied"), 1)

                    context("B")
                    act.wait_ge(sem("x_turned"), 2)
                    fn(fm[0:D, :], S[0][0:D, :], ACT.Identity, scale=affine[:, 2:3]).then_inc(sem("C_fm"), 1)
                    for k in range(3):
                        act.wait_ge(sem("C_rope"), (3, 9, 13)[k])
                        copy(stack_a[:, k * T:(k + 1) * T], work[:]).then_inc(sem("C_rounded"), 1)
                        if k == 1:
                            act.wait_ge(sem("C_v"), 1)
                            values_hi("C", 2 * DH, lambda hh: hh // 2)
                    softmax_of(AC, lambda n: (n % NC + 1) * P)
                    context("C")
                    act.wait_ge(sem("x_turned"), 3)
                    fn(fm[0:D, :], S[0][0:D, :], ACT.Identity, scale=affine[:, 3:4]).then_inc(sem("M_fm"), 1)
                    fn(x_stack[0:D, :], S[0][0:D, :], ACT.Identity, scale=affine[:, 3:4]).then_inc(sem("M_fm"), 1)
                    act.wait_ge(sem("M_shifted"), 1)
                    fn(gl[:, 1], gl[:, 1], ACT.Exp).then_inc(sem("M_exp"), 1)

                    def gates_hi(name):
                        act.wait_ge(sem(f"{name}_gates_turned"), 1)
                        act.wait_ge(sem(f"{name}_cleared"), 1)
                        for j in range(2):
                            copy(gate_stack[0:E, half(j)], C[j][0:E, :]).then_inc(sem(f"{name}_gates_hi"), 1)

                    def hidden_hi(name, n):
                        act.wait_ge(sem(f"{name}_hidden"), n + 1)
                        if n >= SPLIT:
                            act.wait_ge(sem(f"{name}_down"), n - SPLIT + 1)
                        copy(probsT[:, 0, n % SPLIT, :], hidden[:, n % 3, :]).then_inc(sem(f"{name}_hi"), 1)

                    def experts_sum(name, per_half):
                        for j in range(2):
                            act.wait_ge(sem(f"{name}_down"), per_half * (j + 1))
                            copy(context_sum[:, half(j)], C[j][D:P, :]).then_inc(sem(f"{name}_sum_copied"), 1)

                    for n in range(2 * NQ + 1):
                        if n < 2 * NQ:
                            act.wait_ge(sem("M_gate"), n + 1)
                            if n >= 3:
                                act.wait_ge(sem("M_gated"), n - 2)
                            fn(activated[:, n % 3, :], S[n % 2][:, half(0)], ACT.Silu).then_inc(sem("M_silu"), 1)
                        if n == 0:
                            gates_hi("M")
                        else:
                            hidden_hi("M", n - 1)
                    experts_sum("M", NQ)
                    act.wait_ge(sem("x_turned"), 4)
                    copy(fm[0:D, :], S[0][0:D, :]).then_inc(sem("D_fm"), 1)
                    act.wait_ge(sem("D_v"), 1)
                    copy(v_d[:, :, 0:D], R[0][:].rearrange("p (c d) -> p c d", d=D)).then_inc(sem("D_v_hi"), 1)
                    act.wait_ge(sem("D_turned_unit"), 1)
                    copy(d_hi, S[0][:]).then_inc(sem("D_unit_hi"), 1)

                    for x in range(NC):
                        act.wait_ge(AD.s("scores"), x + 1)
                        fn(probs[:, x // 4, x % 4, :], S[x % 2][:], ACT.Copy, accum_out=sums[:, x:x + 1])\
                            .then_inc(AD.s("scores_used"), 1)
                    for x in range(BY_VECTOR, NC):
                        if x == BY_VECTOR:
                            act.wait_ge(AD.s("scores_used"), NC)
                        copy(halved[x], probs[:, x // 4, x % 4, :]).then_inc(sem("D_halved"), 1)
                    for k in range(COUNTS):
                        act.wait_ge(sem("D_threshold"), k + 1)
                        for x in range(BY_VECTOR, NC):
                            if k == 0 and x == BY_VECTOR:
                                act.wait_ge(sem("D_halved"), NC - BY_VECTOR)
                            fn(unread[:, 3 + x - BY_VECTOR, :], halved[x], ACT.Sign, bias=threshold[k % 2][:, x:x + 1],
                               scale=-1.0, accum_out=count[:, x:x + 1]).then_inc(sem("D_signs"), 1)

                    def sparse_exp(x):
                        act.wait_ge(AD.s("sparse"), x + 1)
                        row = probs[:, x // 4, x % 4, :]
                        fn(row, row, ACT.Exp, accum_out=rsum[:, x:x + 1]).then_inc(AD.s("probs"), 1)

                    for x in range(4):
                        sparse_exp(x)
                    for kind, x, j in AD.steps:
                        if kind == "T":
                            AD.take_hi(act, x, j)
                            if x == 0 and j % 2 == 1:
                                sparse_exp(4 + j // 2)
                    context("D")
                    act.wait_ge(sem("x_turned"), 5)
                    copy(fm[0:D, :], S[0][0:D, :]).then_inc(sem("E_fm"), 1)
                    copy(x_stack[0:D, :], S[0][0:D, :]).then_inc(sem("E_fm"), 1)
                    act.wait_ge(sem("E_shifted"), 1)
                    fn(gl[:, 1], gl[:, 1], ACT.Exp).then_inc(sem("E_exp"), 1)
                    for n in range(2 * NG + 1):
                        if n < 2 * NG:
                            act.wait_ge(sem("E_up"), n + 1)
                            if n >= 3:
                                act.wait_ge(sem("E_hidden"), n - 2)
                            fn(activated[:, n % 3, :], S[n // 2 % 2][:, half(n % 2)], ACT.Gelu, bias=b1e[:, n % NG:n % NG + 1])\
                                .then_inc(sem("E_activated"), 1)
                        if n == 0:
                            act.wait_ge(sem("E_gates_turned"), 1)
                            for j in range(2):
                                copy(fm2[0:E, half(j)], C[j][0:E, :]).then_inc(sem("E_gates_copied"), 1)
                            gates_hi("E")
                        else:
                            hidden_hi("E", n - 1)
                    experts_sum("E", NG)

                @block.vector
                def _(dve):
                    v = nc.vector
                    own, n_own = sem("dve_own"), [0]

                    def step(ins):
                        ins.then_inc(own, 1)
                        n_own[0] += 1
                        dve.wait_ge(own, n_own[0])

                    def before_step(ins):
                        ins.then_inc(own, 1)
                        n_own[0] += 1

                    n_powers = [0]

                    def power(k, base):
                        assert POWERS[n_powers[0]][0] == k
                        base.then_inc(sem("power_base"), 1)
                        n_powers[0] += 1
                        dve.wait_ge(sem("powered"), n_powers[0])

                    def center(x):
                        step(v.tensor_reduce(st[:, 2], x, X, ALU.add))
                        step(v.tensor_scalar(st[:, 2], st[:, 2], -1.0 / D, None, ALU.mult))
                        step(v.tensor_tensor(xc[:], x, over_features(st[:, 2]), ALU.add))
                        mean_square(xc)
                        power(1, v.tensor_scalar(st[:, 4], st[:, 0], 1e-5, None, ALU.add))
                        step(v.tensor_tensor(st[:, 3], st[:, 1], st[:, 1], ALU.mult))
                        step(v.tensor_tensor(st[:, 3], st[:, 3], st[:, 0], ALU.mult))

                    def mean_square(x):
                        step(v.tensor_tensor(sq[:], x[:], x[:], ALU.mult))
                        step(v.tensor_reduce(st[:, 0], sq[:], X, ALU.add))
                        step(v.tensor_scalar(st[:, 0], st[:, 0], 1.0 / D, None, ALU.mult))

                    def scaled(dst, src, k):
                        return v.tensor_tensor(dst, src, over_features(st[:, k]), ALU.mult)

                    def row_max(att, n, width):
                        v.tensor_reduce(nmax[:, n:n + 1], att.bank("S", n, 0)[:, 0:width], X, ALU.max, negate=True)\
                            .then_inc(att.s("max"), 1)

                    def normalise(x):
                        att = {"B": AB, "C": AC, "D": AD}[x]
                        dve.wait_ge(att.s("probs"), 4 * att.groups)
                        n = 4 * att.groups
                        step(v.reciprocal(rsum[:, 0:n], rsum[:, 0:n]))
                        if x != "D":
                            by_chunk = rsum[:].rearrange("p (h i o) -> p i h o", h=H, o=1)
                            v.tensor_copy(work[:, 0:HALF].rearrange("p (i h d) -> p i h d", i=NC, h=H),
                                          by_chunk.to_broadcast([P, NC, H, DH])).then_inc(sem(f"{x}_recip"), 1)
                        for j in range(2):
                            dve.wait_ge(sem(f"{x}_ctx_copied"), j + 1)
                            both = v.tensor_tensor(context_sum[:, half(j)], C[j][0:D, :], context_sum[:, half(j)],
                                                   ALU.add)
                            if x == "D":
                                both.then_inc(sem("D_context"), 1)
                            else:
                                step(both)
                                dve.wait_ge(sem(f"{x}_spread"), 1)
                                v.tensor_tensor(fm2[0:D, half(j)], context_sum[:, half(j)], S[0][0:D, half(j)],
                                                ALU.mult)\
                                    .then_inc(sem(f"{x}_context"), 1)

                    def values_lo(x, width, group):
                        dve.wait_ge(sem(f"{x}_v_hi"), 4)
                        for hh in range(H):
                            src = C[0][:, 0:NC * width].rearrange("p (c d) -> p c d", d=width)
                            g = group(hh)
                            v.tensor_tensor(v_pad[:, :, hh, D + hh * DH:D + (hh + 1) * DH],
                                            src[:, :, g * DH:(g + 1) * DH],
                                            f(v_pad[:, :, hh, hh * DH:(hh + 1) * DH]), ALU.subtract)\
                                .then_inc(sem(f"{x}_v_lo"), 1)

                    def e_bcast(ap):
                        return ap.rearrange("p (c o) -> p c o", o=1).to_broadcast([P, NC, E])

                    def top_two(score, one, other, mask):
                        rank = first_key[:].rearrange("p (o e) -> p o e", o=1).to_broadcast([P, NC, E])
                        for dst, src in ((mask, score), (one, other)):
                            step(v.tensor_reduce(gs[:, 1], src, X, ALU.max))
                            step(v.tensor_tensor(dst, src, e_bcast(gs[:, 1]), ALU.is_equal))
                            step(v.tensor_tensor(dst, dst, rank, ALU.mult))
                            step(v.tensor_reduce(gs[:, 1], dst, X, ALU.max))
                            step(v.tensor_tensor(dst, dst, e_bcast(gs[:, 1]), ALU.is_equal))
                            if src is score:
                                step(v.tensor_copy(other, score))
                                step(v.copy_predicated(other, mask.bitcast(U32), lowest[:]))
                        step(v.tensor_tensor(mask, mask, one, ALU.add))

                    def x_lo(name):
                        dve.wait_ge(sem(f"{name}_fm"), 2)
                        v.tensor_tensor(x_stack[D:P, :], fm[0:D, :], f(x_stack[0:D, :]), ALU.subtract)\
                            .then_inc(sem(f"{name}_x_lo"), 1)

                    def gates_lo(name):
                        for j in range(2):
                            dve.wait_ge(sem(f"{name}_gates_hi"), j + 1)
                            v.tensor_tensor(gate_stack[D // 2:D // 2 + E, half(j)], C[j][0:E, :],
                                            f(gate_stack[0:E, half(j)]), ALU.subtract).then_inc(sem(f"{name}_gates_lo"), 1)

                    def hidden_free(name, n):
                        if n >= 3:
                            dve.wait_ge(sem(f"{name}_lo"), n - 2)

                    def experts_sum(name):
                        for j in range(2):
                            dve.wait_ge(sem(f"{name}_sum_copied"), j + 1)
                            v.tensor_tensor(context_sum[:, half(j)], C[j][0:D, :], context_sum[:, half(j)], ALU.add)\
                                .then_inc(sem(f"{name}_summed"), 1)
                        dve.wait_ge(sem(f"{name}_by_token"), 1)
                        return v.tensor_tensor(toks(h[:]), toks(h[:]), S[0][:, 0:HALF], ALU.add)

                    dve.wait_ge(sem("A_q_hi"), 1)
                    v.tensor_tensor(a_q_lo, S[0][:], f(a_q_hi), ALU.subtract).then_inc(sem("A_split"), 1)
                    dve.wait_ge(sem("A_k_hi"), 1)
                    v.scalar_tensor_tensor(a_keys, f(a_k_hi), parts[:, 0:1], S[1][:], ALU.mult, ALU.add)\
                        .then_inc(sem("A_split"), 1)
                    for s in range(NC):
                        dve.wait_ge(sem("A_scores"), s + 1)
                        if s >= 2:
                            dve.wait_ge(sem("A_products"), s - 1)
                        v.tensor_tensor(probs[:, 0, s % 2, :], S[s % 2][:], gate[s], ALU.mult)\
                            .then_inc(sem("A_gated"), 1)
                    dve.wait_ge(sem("A_out"), 1)
                    y = R[1][:]
                    step(v.tensor_scalar(toks(sq[:]), y, 0.0, prelu[:, 0:1], ALU.min, ALU.mult))
                    dve.wait_ge(sem("stored"), 16 * seq + 16)
                    step(v.scalar_tensor_tensor(toks(h[:]), y, 0.0, toks(sq[:]), ALU.max, ALU.add))
                    center(h[:])
                    power(3, v.tensor_scalar(st[:, 4], st[:, 3], 1e-5, None, ALU.add))
                    step(v.tensor_tensor(st[:, 3], st[:, 3], st[:, 1], ALU.mult))
                    scaled(xn[:], xc[:], 3).then_inc(sem("normalised"), 1)

                    values_lo("B", D, lambda hh: hh)

                    def prepare_b(hh, k):
                        b, bank, done = hh % 2, AB.bank("P", hh, k), sem("B_prep_dve")
                        dve.wait_ge(sem("B_prep"), PREP * hh + k + 1)
                        if k < 2:
                            if hh + k == 0:
                                dve.wait_ge(sem("rot_loaded"), 32)
                            if hh and k == 0:
                                dve.wait_ge(sem("B_prep_pool"), 2 * hh - 1)
                            v.tensor_tensor(cosb[:, k, :], bank[:], (turn_cos, turn_sin)[k][:], ALU.mult).then_inc(done, 1)
                        else:
                            dve.wait_ge(sem("B_prep_act"), 3 * hh + 3)
                            v.scalar_tensor_tensor(q2[D:P, b, :], f(rounded_wide[0:D, :]), parts[0:D, 1:2], bank[0:D, :],
                                                   ALU.mult, ALU.add).then_inc(done, 1)
                            v.scalar_tensor_tensor(k2[D:P, b, :], f(rounded_wide[D:P, :]), parts[D:P, 2:3], bank[D:P, :],
                                                   ALU.mult, ALU.add).then_inc(done, 1)

                    content_due = []
                    for kind, x, j in AB.steps:
                        if kind == "P":
                            if x and j == 2:
                                content_due.append(x)
                            else:
                                prepare_b(x, j)
                        elif kind == "F":
                            i, k, bank = x % NC, AB.slot[("F", x, 0)], AB.bank("S", x, 0)
                            w = min(P + 1, T - i * P)
                            dve.wait_ge(AB.s("scores"), x + 1)
                            v.copy_predicated(bank[:, i * P:i * P + w], late_mask[:, 0:w], R[k % 2][:, 0:w])\
                                .then_inc(AB.s("fixed"), 1)
                            dve.wait_ge(AB.s("fixed"), 2 * x + 1)
                            v.copy_predicated(bank[:, i * P:i * P + w], next_mask[:, 0:w],
                                              R[k % 2][:, 256:256 + w]).then_inc(AB.s("fixed"), 1)
                            dve.wait_ge(AB.s("fixed"), 2 * x + 2)
                            row_max(AB, x, T)
                            if content_due:
                                prepare_b(content_due.pop(), 2)
                        elif kind == "T":
                            AB.take_lo(dve, x, j)
                    normalise("B")
                    dve.wait_ge(sem("B_out"), 1)
                    step(v.tensor_tensor(toks(h[:]), R[0][:], toks(h[:]), ALU.add))
                    center(h[:])
                    step(scaled(f_tok[:], xc[:], 1))
                    power(3, v.tensor_scalar(st[:, 4], st[:, 3], 1e-6, None, ALU.add))
                    scaled(xn[:], f_tok[:], 3).then_inc(sem("normalised"), 1)
                    a, b = cosb[:, 0, :], cosb[:, 1, :]
                    rope, n_rope = sem("C_rope"), 0
                    dve.wait_ge(sem("rope_loaded"), 32)
                    for k in range(3):
                        for dst, table, banks in ((a, turn_cos, R if k == 1 else S[0]), (b, turn_sin, C if k == 1 else S[1])):
                            dve.wait_ge(sem("C_proj"), 2 * k + (1 if dst is a else 2))
                            if dst is a and k:
                                dve.wait_ge(rope, n_rope)
                            if k == 1:
                                for j in range(2):
                                    v.tensor_tensor(dst[:, half(j)], banks[j][:], table[:, half(j)], ALU.mult)\
                                        .then_inc(rope, 1)
                            else:
                                v.tensor_tensor(dst, banks[:], table[:], ALU.mult).then_inc(rope, 1)
                            n_rope += 2 if k == 1 else 1
                        dve.wait_ge(rope, n_rope)
                        v.tensor_tensor(work[:], a, b, ALU.add).then_inc(rope, 1)
                        dve.wait_ge(sem("C_rounded"), k + 1)
                        v.scalar_tensor_tensor(c_stack[k], f(stack_a[:, k * T:(k + 1) * T]), parts[:, 2 if k == 2 else 1:3 if k == 2 else 2],
                                               work[:], ALU.mult, ALU.add).then_inc(rope, 1)
                        n_rope += 2
                    values_lo("C", 2 * DH, lambda hh: hh // 2)
                    for kind, x, j in AC.steps:
                        if kind == "S":
                            dve.wait_ge(AC.s("scores"), x + 1)
                            row_max(AC, x, (x % NC + 1) * P)
                        elif kind == "T":
                            AC.take_lo(dve, x, j)
                    normalise("C")
                    dve.wait_ge(sem("C_out"), 1)
                    step(v.tensor_tensor(toks(f_tok[:]), R[0][:], toks(f_tok[:]), ALU.add))
                    mean_square(f_tok)
                    power(3, v.tensor_scalar(st[:, 4], st[:, 0], 1e-6, None, ALU.add))
                    scaled(xn[:], f_tok[:], 3).then_inc(sem("normalised"), 1)
                    x_lo("M")
                    dve.wait_ge(sem("M_logits"), 1)
                    v.tensor_copy(gl[:, 0], R[0][:, 0:NC * E].rearrange("p (c e) -> p c e", e=E))\
                        .then_inc(sem("M_logits_read"), 1)
                    dve.wait_ge(sem("M_logits_read"), 1)
                    step(v.tensor_reduce(gs[:, 0], gl[:, 0], X, ALU.max))
                    v.tensor_tensor(gl[:, 1], gl[:, 0], e_bcast(gs[:, 0]), ALU.subtract).then_inc(sem("M_shifted"), 1)
                    dve.wait_ge(sem("M_exp"), 1)
                    step(v.tensor_reduce(gs[:, 0], gl[:, 1], X, ALU.add))
                    step(v.reciprocal(gs[:, 0], gs[:, 0]))
                    step(v.tensor_tensor(gl[:, 0], gl[:, 1], e_bcast(gs[:, 0]), ALU.mult))
                    top_two(gl[:, 0], gl[:, 2], gl[:, 3], gl[:, 4])
                    step(v.tensor_tensor(gates[:], gl[:, 0], gl[:, 4], ALU.mult))
                    step(v.tensor_reduce(gs[:, 0], gates[:], X, ALU.add))
                    step(v.tensor_scalar(gs[:, 0], gs[:, 0], 1e-9, None, ALU.add))
                    step(v.reciprocal(gs[:, 0], gs[:, 0]))
                    v.tensor_tensor(gates[:], gates[:], e_bcast(gs[:, 0]), ALU.mult).then_inc(sem("M_gates"), 1)
                    gates_lo("M")
                    for n in range(2 * NQ):
                        dve.wait_ge(sem("M_silu"), n + 1)
                        dve.wait_ge(sem("M_spread_gate"), n + 1)
                        if n >= 3:
                            dve.wait_ge(sem("M_hidden"), n - 2)
                        v.tensor_tensor(gated[:, n % 3, :], activated[:, n % 3, :], R[n % 2][:], ALU.mult)\
                            .then_inc(sem("M_gated"), 1)
                        dve.wait_ge(sem("M_gated"), n + 1)
                        dve.wait_ge(sem("M_up"), n + 1)
                        hidden_free("M", n)
                        v.tensor_tensor(hidden[:, n % 3, :], gated[:, n % 3, :], S[n % 2][:, half(1)], ALU.mult)\
                            .then_inc(sem("M_hidden"), 1)
                    step(v.tensor_tensor(h[:], h[:], f_tok[:], ALU.add))
                    step(experts_sum("M"))
                    center(h[:])
                    scaled(f_tok[:], xc[:], 1).then_inc(sem("normalised"), 1)
                    dve.wait_ge(sem("normalised"), 4)
                    power(3, v.tensor_scalar(st[:, 4], st[:, 3], float(D), None, ALU.mult))
                    step(v.tensor_scalar(st[:, 3], st[:, 3], 1e-12, None, ALU.max))
                    step(v.reciprocal(st[:, 3], st[:, 3]))
                    twice = work[:].rearrange("p (c r d) -> p c r d", c=NC, r=2)
                    for r in range(2):
                        scaled(twice[:, :, r, :], f_tok[:], 3).then_inc(sem("D_unit_x"), 1)
                    dve.wait_ge(sem("D_v_hi"), 1)
                    v.tensor_tensor(v_d[:, :, D:P], R[0][:].rearrange("p (c d) -> p c d", d=D), f(v_d[:, :, 0:D]),
                                    ALU.subtract).then_inc(sem("D_v_lo"), 1)
                    dve.wait_ge(sem("D_unit_hi"), 1)
                    v.tensor_tensor(d_lo, S[0][:], f(d_hi), ALU.subtract).then_inc(sem("D_unit_split"), 1)
                    v.scalar_tensor_tensor(d_stack, f(d_hi), parts[:, 0:1], S[0][:], ALU.mult, ALU.add)\
                        .then_inc(sem("D_unit_split"), 1)
                    for n in range(NC):
                        dve.wait_ge(AD.s("scores_used"), n + 1)
                        row = probs[:, n // 4, n % 4, :]
                        if n >= 2 * SPLIT:
                            dve.wait_ge(sem("D_squared"), n - 2 * SPLIT + 1)
                        v.scalar_tensor_tensor(unread[:, n % (2 * SPLIT), :], row, 1.0, row, ALU.mult, ALU.mult,
                                               accum_out=squares[:, n:n + 1]).then_inc(sem("D_squared"), 1)
                        if n < BY_VECTOR:
                            before_step(v.tensor_copy(halved[n], row))
                    dve.wait_ge(sem("D_squared"), NC)
                    step(v.tensor_scalar(low, sums, 1.0 / T, None, ALU.mult))
                    step(v.tensor_tensor(above, low, low, ALU.mult))
                    step(v.scalar_tensor_tensor(above, squares, 1.0 / T, above, ALU.mult, ALU.subtract))
                    power(5, v.tensor_scalar(st[:, 4], above, 1e-12, None, ALU.max))
                    deviation = st[:, 5]
                    v.tensor_scalar(most, deviation, 3.0 * SLOPE, None, ALU.mult)
                    v.tensor_scalar(least, deviation, 0.3 * SLOPE, None, ALU.mult)
                    v.scalar_tensor_tensor(high, deviation, 4.0, low, ALU.mult, ALU.add)
                    step(v.scalar_tensor_tensor(threshold[0], deviation, FIRST_CUT, low, ALU.mult, ALU.add))
                    for k in range(COUNTS):
                        now, before, of_now, of_before = (x[i] for x in (threshold, inverse) for i in (k % 2, (k + 1) % 2))
                        step(v.tensor_scalar(now, now, 1e-3, None, ALU.max))
                        v.tensor_scalar(now.bitcast(I32), now.bitcast(I32), 1, None, ALU.bitwise_or)\
                            .then_inc(sem("D_threshold"), 1)
                        dve.wait_ge(sem("D_threshold"), k + 1)
                        for n in range(BY_VECTOR):
                            if n >= 3:
                                dve.wait_ge(sem("D_counted"), BY_VECTOR * k + n - 2)
                            v.tensor_scalar(unread[:, n % 3, :], halved[n], now[:, n:n + 1], None, ALU.is_ge, ALU.add,
                                            accum_out=count[:, n:n + 1]).then_inc(sem("D_counted"), 1)
                        dve.wait_ge(sem("D_counted"), BY_VECTOR * (k + 1))
                        dve.wait_ge(sem("D_signs"), (NC - BY_VECTOR) * (k + 1))
                        v.tensor_scalar(seen[:, 0:BY_VECTOR], count[:, 0:BY_VECTOR], float(WANTED), None, ALU.add)
                        step(v.tensor_scalar(seen[:, BY_VECTOR:NC], count[:, BY_VECTOR:NC], -0.5, T / 2.0 + WANTED, ALU.mult, ALU.add))
                        step(v.tensor_scalar(above, seen, 2.0 * WANTED + SLACK + 0.5, None, ALU.is_gt))
                        step(v.scalar_tensor_tensor(missed, seen, 2.0 * WANTED - SLACK - 0.5, above, ALU.is_lt, ALU.add))
                        if k == COUNTS - 1:
                            break
                        v.scalar_tensor_tensor(above, seen, 2.0 * WANTED, missed, ALU.is_gt, ALU.mult)
                        v.scalar_tensor_tensor(edge_high, seen, 2.0 * WANTED, missed, ALU.is_le, ALU.mult)
                        step(v.reciprocal(of_now, seen))
                        v.copy_predicated(low, above.bitcast(U32), now)
                        step(v.copy_predicated(high, edge_high.bitcast(U32), now))
                        if k == 0:
                            step(v.tensor_scalar(slope, deviation, SLOPE, None, ALU.mult))
                        else:
                            v.tensor_tensor(slope, now, before, ALU.subtract)
                            step(v.scalar_tensor_tensor(above, of_now, 1e-7, of_before, ALU.add, ALU.subtract))
                            step(v.reciprocal(above, above))
                            step(v.tensor_tensor(slope, slope, above, ALU.mult))
                            step(v.tensor_tensor(slope, slope, most, ALU.min))
                            step(v.tensor_tensor(slope, slope, least, ALU.max))
                        step(v.scalar_tensor_tensor(slope, of_now, -1.0 / (2 * WANTED), slope, ALU.add, ALU.mult))
                        step(v.tensor_tensor(slope, now, slope, ALU.subtract))
                        if k >= 2:
                            step(v.tensor_tensor(above, high, low, ALU.subtract))
                            v.scalar_tensor_tensor(edge_low, above, 0.25, low, ALU.mult, ALU.add)
                            step(v.scalar_tensor_tensor(edge_high, above, 0.75, low, ALU.mult, ALU.add))
                            step(v.tensor_tensor(slope, slope, edge_low, ALU.max))
                            step(v.tensor_tensor(slope, slope, edge_high, ALU.min))
                        step(v.tensor_copy(before, now))
                        step(v.copy_predicated(before, missed.bitcast(U32), slope))
                    for i, n in enumerate(TOP_ORDER):
                        if n < BY_VECTOR:
                            where = below[n % 2]
                            if n >= 2:
                                dve.wait_ge(sem("D_top"), TOP_ORDER.index(n - 2) + 1)
                            v.scalar_tensor_tensor(where, halved[n], now[:, n:n + 1], probs[:, n // 4, n % 4, :],
                                                   ALU.is_lt, ALU.mult).then_inc(sem("D_masked"), 1)
                            dve.wait_ge(sem("D_masked"), n + 1)
                        else:
                            where = spare[:]
                            dve.wait_ge(sem("D_below"), n - BY_VECTOR + 1)
                        v.max(top8[:, n, :], where).then_inc(sem("D_top"), 1)
                    step(v.tensor_scalar(missed, missed, 0.0, None, ALU.is_equal))
                    v.tensor_scalar(edge_low, seen, 9.0 - TOPK - WANTED, None, ALU.add)
                    step(v.tensor_scalar(edge_high, seen, 8.0 - TOPK - WANTED, None, ALU.add))
                    dve.wait_ge(sem("D_top"), NC)
                    rank = first_key[:].rearrange("p (o e) -> p o e", o=1).to_broadcast([P, NC, E])
                    for dst, key, spot in ((chosen, edge_low, gl[:, 0]), (beyond, edge_high, gl[:, 1])):
                        step(v.tensor_tensor(spot, rank, e_bcast(key), ALU.is_equal))
                        step(v.tensor_tensor(spot, spot, top8[:], ALU.mult))
                        step(v.tensor_reduce(dst, spot, X, ALU.add))
                    step(v.tensor_scalar(beyond, beyond, 0.0, None, ALU.max))
                    step(v.tensor_tensor(beyond, chosen, beyond, ALU.is_gt))
                    step(v.tensor_tensor(beyond, beyond, missed, ALU.mult))
                    v.tensor_reduce(all_rows, beyond, X, ALU.min).then_inc(sem("D_ok"), 1)
                    dve.wait_ge(sem("D_all_ok"), 1)
                    step(v.tensor_scalar(repeat[:], S[0][0:1, 0:1], P / 2 - 0.5, None, ALU.is_lt))
                    with dve.If(dve.value_load(repeat[0:1, 0:1]) != 0):
                        taken = sem("D_taken")
                        for n in range(NC):
                            src = probs[:, n // 4, n % 4, :]
                            for k in range(TOPK // 8):
                                at = 2 * (TOPK // 8 * n + k)
                                v.max(top8[:, 0, :], src if k == 0 else work[:]).then_inc(taken, 1)
                                dve.wait_ge(taken, at + 1)
                                v.match_replace(work[:], top8[:, 0, :], src if k == 0 else work[:], TAKEN)\
                                    .then_inc(taken, 1)
                                dve.wait_ge(taken, at + 2)
                            v.scalar_tensor_tensor(src, work[:], TAKEN, src, ALU.is_equal, ALU.mult)\
                                .then_inc(AD.s("sparse"), 1)
                            dve.wait_ge(AD.s("sparse"), n + 1)
                    with dve.Else():
                        for n in range(NC):
                            src = probs[:, n // 4, n % 4, :]
                            v.scalar_tensor_tensor(src, src, chosen[:, n:n + 1], src, ALU.is_ge, ALU.mult)\
                                .then_inc(AD.s("sparse"), 1)
                    for kind, x, j in AD.steps:
                        if kind == "T":
                            AD.take_lo(dve, x, j)
                    normalise("D")
                    dve.wait_ge(sem("D_by_token"), 1)
                    step(v.tensor_tensor(sq[:], S[0][:, 0:HALF].rearrange("p (c d) -> p c d", d=D),
                                         over_features(rsum[:, 0:NC]), ALU.mult))
                    step(v.tensor_tensor(h[:], h[:], sq[:], ALU.add))
                    center(h[:])
                    scaled(f_tok[:], xc[:], 1).then_inc(sem("normalised"), 1)
                    x_lo("E")
                    dve.wait_ge(sem("E_logits"), 1)
                    v.tensor_copy(gl[:, 0], R[0][:, 0:NC * E].rearrange("p (c e) -> p c e", e=E))\
                        .then_inc(sem("E_logits_read"), 1)
                    dve.wait_ge(sem("E_logits_read"), 1)
                    step(v.tensor_reduce(gs[:, 0], gl[:, 0], X, ALU.max))
                    v.tensor_tensor(gl[:, 1], gl[:, 0], e_bcast(gs[:, 0]), ALU.subtract).then_inc(sem("E_shifted"), 1)
                    top_two(gl[:, 0], gl[:, 2], gl[:, 3], gl[:, 4])
                    dve.wait_ge(sem("E_exp"), 1)
                    step(v.tensor_tensor(gates[:], gl[:, 1], gl[:, 4], ALU.mult))
                    step(v.tensor_reduce(gs[:, 0], gates[:], X, ALU.add))
                    step(v.reciprocal(gs[:, 0], gs[:, 0]))
                    v.tensor_tensor(gates[:], gates[:], e_bcast(gs[:, 0]), ALU.mult).then_inc(sem("E_gates"), 1)
                    gates_lo("E")
                    for n in range(2 * NG):
                        dve.wait_ge(sem("E_activated"), n + 1)
                        dve.wait_ge(sem("E_spread_gate"), n // 2 + 1)
                        hidden_free("E", n)
                        v.tensor_tensor(hidden[:, n % 3, :], activated[:, n % 3, :], R[n // 2 % 2][:], ALU.mult)\
                            .then_inc(sem("E_hidden"), 1)
                    experts_sum("E").then_inc(sem("result"), 1)

            numbers = sorted(sems[name].num for name in sems if name not in lasting)
            first = 0
            for i in range(1, len(numbers) + 1):
                if i == len(numbers) or numbers[i] != numbers[i - 1] + 1:
                    nc.gpsimd.sem_clear(range(numbers[first], numbers[i - 1] + 1))
                    first = i
            nc.all_engine_barrier()

        with nc.Block() as block:
            @block.sync
            def _(sp):
                sp.wait_ge(sem("stored"), 16 * (B + 1))


def tables():
    div = np.exp(np.arange(0, D, 2, dtype=np.float32) * np.float32(-np.log(10000.0) / D)).astype(np.float64)
    pos = np.arange(T, dtype=np.float64)
    angle = div[:, None] * pos
    pe_early, pe_late = (np.concatenate([np.sin(a), np.cos(a)]) for a in (angle, div[:, None] * (pos - T)))
    turn = div[:, None] * (T - 1 - pos)
    rot_cos = np.concatenate([np.cos(turn)] * 4)
    rot_sin = np.concatenate([-np.sin(turn), np.sin(turn)] * 2)
    inv = 1.0 / 10000.0 ** (np.arange(0, DH, 2, dtype=np.float32) / DH)
    freqs = np.outer(np.arange(T, dtype=np.float32), inv)
    c, s = np.cos(freqs).T, np.sin(freqs).T
    rope_cos, rope_sin = np.concatenate([c, c] * 2 * DUP), np.concatenate([-s, s] * 2 * DUP)
    i, j = np.arange(P)[:, None], np.arange(P + 1)
    bf16 = mybir.dt.np(BF16)
    rows, of = np.arange(D)[:, None, None], np.arange(NQ)[None, :, None]
    expert = np.where(of < E, of, 2 * (of - E) + np.arange(P)[None, None, :] // D)
    gate_rows = (rows % (D // 2) == expert).reshape(D, NQ * P)
    copy = np.arange(P) % D // DH
    parts = -np.stack([np.arange(P) >= D, copy % 2 == 1, copy >= 2], axis=1).astype(np.float32)
    f32 = lambda a: np.ascontiguousarray(a, dtype=np.float32)
    return {"pe_early": f32(pe_early), "pe_late": f32(pe_late), "rot_cos": f32(rot_cos), "rot_sin": f32(rot_sin), "rope_cos": f32(rope_cos),
            "rope_sin": f32(rope_sin), "identity": np.eye(P, dtype=np.float32),
            "late_mask": (j >= i + 2).astype(np.int32), "next_mask": (j == i + 1).astype(np.int32),
            "future": np.where(j[:P] > i, -1e30, 0.0).astype(bf16), "parts": f32(parts), "gate_rows": f32(gate_rows)}


def laid_out(inp):
    a = {k: np.asarray(v) for k, v in inp.items()}
    L = "L0_attn_"
    pos_t = a[L + "Wpos"].T
    sin_rows, cos_rows = pos_t[:, 0::2], pos_t[:, 1::2]
    x = a["x"].reshape(B, T, D).transpose(0, 2, 1)
    r = {"xT": np.concatenate([x, x[-1:]]), "gateT": a["L0_tok_d_gamma_batched"].T,
         "prelu_a": a["L0_tok_prelu_a"].reshape(1, 1),
         "WqT": a[L + "Wq"].T, "WposT": np.stack([np.concatenate([sin_rows, cos_rows], 1),
                                                 np.concatenate([cos_rows, sin_rows], 1)]),
         "v_bias": a[L + "v_bias"].T,
         "W_D": a["L1_attn_W"].T, "b_D": a["L1_attn_b"]}
    for n in ("Wq", "bq", "Wk", "bk", "Wv", "bv", "Wo", "bo"):
        r["tok_" + n] = a["L0_tok_" + n]
    for n in ("ln_gamma", "ln_beta", "Wq", "bq", "Wk", "bk", "Wv", "bv", "u_bias", "Wout", "bout"):
        r[n] = a[L + n]
    for n in ("wq", "wk", "wv", "wo"):
        r[n + "T"] = a["L0_ffn_" + n].T
    r["routerT"] = a["L0_ffn_router_w"].T
    for n in ("w1", "w2", "w3"):
        r[n + "T"] = a["L0_ffn_" + n].transpose(0, 2, 1)
    for n in ("ln1_w", "ln2_w"):
        r[n] = a["L0_ffn_" + n]
    for n in ("Wg", "bg", "W1", "b1", "W2", "b2"):
        r[n] = a["L1_ffn_" + n]
    r.update(tables())
    return {n: np.ascontiguousarray(r[n]) for n in INPUTS}


def kernel(**inputs):
    from concourse import bacc, bass_utils

    nc = bacc.Bacc("TRN2", target_bir_lowering=False, num_devices=1)
    arrays, aps = {}, {}
    for name, a in laid_out(inputs).items():
        arrays[f"in_{name}"] = a
        aps[name] = nc.dram_tensor(f"in_{name}", a.shape, mybir.dt.from_np(a.dtype), kind="ExternalInput").ap()
    out = nc.dram_tensor("out", (B, T, D), F32, kind="ExternalOutput").ap()
    build(nc, aps, out)
    r = bass_utils.run_bass_kernel_spmd(nc, [arrays], core_ids=[0])
    return r.results[0]["out"]
```

```python
from contextlib import ExitStack

import numpy as np

import concourse.bass as bass
from concourse import mybir
from concourse.alu_op_type import AluOpType as ALU

F32 = mybir.dt.float32
F32R = mybir.dt.float32r
BF16 = mybir.dt.bfloat16
F16 = mybir.dt.float16
I32 = mybir.dt.int32
U32 = mybir.dt.uint32
ACT = mybir.ActivationFunctionType
X = mybir.AxisListType.X

P = 128
B, T, D = 4, 1024, 64
NC = T // P
HALF = 512
H, DH = 4, 16
E = 8
HID = int(8 / 3 * D)
REST = HID - P
NQ = E + E // 2
GH = 256
NG = E * GH // P
TOPK = 64
DUP = D // DH
PREP = 3
PREP_AFTER = [0, 1, 5]
SPLIT = 3
COUNTS = 6
WANTED, SLACK = 60, 3
FIRST_CUT = 1.55
SLOPE = 130.0
BY_VECTOR = 5
TOP_ORDER = [0, 1, 5, 2, 6, 3, 7, 4]
SPARSE_FIRST = 5
TAKEN = -3.0

EXPONENTS = [-0.5, -0.5, 0.5]
POWERS = [(1, 0), (2, 0), (1, 0), (2, 1), (1, 2), (1, 0)]
SWIGLU_POWER, SEARCH_POWER = 2, 4

INPUTS = ["xT", "gateT", "projections", "columns", "attention_64", "attention_16", "positions", "experts_up",
          "experts_down", "b2", "rot_cos", "rot_sin", "rope_cos", "rope_sin", "masks", "future", "gate_rows"]

POSW = 5 * D // 2

PROJECTIONS = [("tok_q", 2 * D), ("tok_k", 2 * D), ("tok_v", D), ("tok_o", D), ("v", D), ("out", D), ("cosine_v", D),
               ("gelu_gate", E), ("causal_o", D), ("causal_v", 2 * DH), ("router", E), ("affine", 4)]
COLUMNS = [("identity", P), ("parts", 4), ("prelu", 1), ("b1", NG)]


def parts_of(tensor, packing):
    at, views = 0, {}
    for name, width in packing:
        views[name] = tensor[:, at:at + width]
        at += width
    return views


def attend_steps(groups, last_chunk, fix=False, prep=False):
    steps = [("P", 0, k) for k in range(PREP)] + [("V", 0, 0)] if prep else []
    waiting = []

    def product():
        if len(waiting) == SPLIT:
            steps.append(("AV",) + waiting.pop(0))

    late = []

    def transpose(t):
        product()
        steps.append(("T",) + t)
        waiting.append(t)

    for g in range(groups + 1):
        todo = [(g - 1, j) for j in range(last_chunk(g - 1) + 1)] if g else []
        for a in range(4):
            if g < groups:
                steps.append(("S", 4 * g + a, 0))
                if fix:
                    steps.append(("F", 4 * g + a, 0))
                product()
            while late:
                transpose(late.pop(0))
            due = todo[len(todo) * a // 4:len(todo) * (a + 1) // 4]
            if fix and len(due) > 1:
                late.append(due.pop())
            for t in due:
                transpose(t)
            if prep and g // 2 + 1 < groups // 2 and 4 * (g % 2) + a in PREP_AFTER:
                steps.append(("P", g // 2 + 1, PREP_AFTER.index(4 * (g % 2) + a)))
    for t in late:
        transpose(t)
    return steps + [("AV",) + t for t in waiting]


def build(nc, t, out):
    with ExitStack() as ctx:
        def sb(name, shape, dt=F32):
            return ctx.enter_context(nc.sbuf_tensor(name, shape, dt))

        sems = {}

        def sem(name):
            if name not in sems:
                sems[name] = ctx.enter_context(nc.semaphore(name))
            return sems[name]

        turn_cos, turn_sin = sb("turn_cos", [P, T]), sb("turn_sin", [P, T])
        columns = sb("columns_sb", [P, sum(w for _, w in COLUMNS)])
        view = parts_of(columns, COLUMNS)
        ident, parts, prelu, b1e = (view[n] for n in ("identity", "parts", "prelu", "b1"))
        ident_bf = sb("ident_bf", [P, P], BF16)
        future = sb("future_sb", [P, P], BF16)
        masks = sb("masks_sb", [P, 2, P + 1], I32)
        late_mask, next_mask = masks[:, 0, :], masks[:, 1, :]
        projections = sb("projections_sb", [D + 1, sum(w for _, w in PROJECTIONS)])
        view = parts_of(projections, PROJECTIONS)
        tok_w = {n: view["tok_" + n] for n in "qkvo"}
        wv_b, wout_b, w_d, wg_e = (view[n] for n in ("v", "out", "cosine_v", "gelu_gate"))
        wo_c, wv_c, router, affine = (view[n][0:D] for n in ("causal_o", "causal_v", "router", "affine"))
        posw_hi, posw_lo = sb("posw_hi", [P, H, POSW], F32R), sb("posw_lo", [D + 2, H, POSW], F32R)
        qkw_hi, qkw_lo = sb("qkw_hi", [P, H, 2 * D], F32R), sb("qkw_lo", [D + 2, H, 2 * D], F32R)
        qk_hi = sb("qk_hi", [P, 3, 2, P], F32R)
        b2e = sb("b2e", [E, D])
        region = sb("region", [P, 2 * NQ * P + 3 * NQ * P], F32R)
        LO, HI = slice(0, 2 * NQ * P), slice(2 * NQ * P, 5 * NQ * P)
        m_lo = region[0:D, LO].rearrange("p (w q n) -> p w q n", w=2, q=NQ)
        m_hi = region[:, HI][:, 0:2 * NQ * P].rearrange("p (w q n) -> p w q n", w=2, q=NQ)
        m_down = region[:, HI][:, 2 * NQ * P:3 * NQ * P].rearrange("p (q n) -> p q n", q=NQ)
        e_lo = region[0:D, 0:NG * P].rearrange("p (q n) -> p q n", q=NG)
        e_hi = region[:, HI][:, 0:NG * P].rearrange("p (q n) -> p q n", q=NG)
        e_down = region[:, HI][:, NG * P:2 * NG * P].rearrange("p (q n) -> p q n", q=NG)
        gate_rows = region[D:P, 0:NQ * P].rearrange("p (q n) -> p q n", q=NQ)
        kept = {n: nc.dram_tensor(f"kept_{n}", shape, F32, kind="Internal").ap() for n, shape in
                (("m_lo", (D, 2 * NQ * P)), ("m_hi", (P, 3 * NQ * P)), ("e_lo", (D, NG * P)), ("e_hi", (P, 2 * NG * P)))}
        exponents = sb("exponents", [P, len(EXPONENTS), NC])
        lowest = sb("lowest", [P, NC, E])
        first_key = sb("first_key", [P, E])

        fm = sb("fm", [D + 1, T])
        fm2_at = -(-nc.sbuf_base // 32) * 32
        fm2 = sb("fm2", [D + 2, T])
        ones_stack = nc.alloc_sbuf_tensor_at("ones_stack", [D + 2, T], F32R, offset=fm2_at)
        halves_at = -(-nc.sbuf_base // 32) * 32
        halves = sb("halves", [P, T])
        context_sum = halves[0:D, :]
        qk_lo = nc.alloc_sbuf_tensor_at("qk_lo", [P, 3, 2, P], F32R, offset=halves_at)[D:P]
        v_d = sb("v_d", [P, NC, P], F32R)
        v_pad = sb("v_pad", [P, NC, H, P], F32R)
        base = -(-nc.sbuf_base // 32) * 32
        area = sb("area", [P, 6 * T + 8])
        assert nc.sbuf_base == base + 4 * (6 * T + 8)

        def at(name, offset, shape, dt=F32R):
            return nc.alloc_sbuf_tensor_at(name, shape, dt, offset=base + 4 * offset)

        q1 = at("q1", 0, [P, 2, T + 1])
        q2 = at("q2", 2 * T + 8, [P, 2, T])
        q2_late = at("q2_late", 4 * T + 8, [P, 2, T])
        k1, k1_late = sb("k1", [P, T], F32R), sb("k1_late", [P, T], F32R)
        k2, k2_late = sb("k2", [P, 2, T], F32R), sb("k2_late", [P, 2, T], F32R)
        rounded_at = -(-nc.sbuf_base // 32) * 32
        rounded = sb("rounded", [P, 2, HALF], F32R)
        assert nc.sbuf_base == rounded_at + 8 * HALF
        probs = sb("probs", [P, 2, 4, T])
        probsT_at = -(-nc.sbuf_base // 32) * 32
        probsT = sb("probsT", [P, 2, SPLIT, HALF], F32R)
        assert nc.sbuf_base == probsT_at + 8 * SPLIT * HALF
        stack_a = probsT[:].rearrange("p a b t -> p (a b t)")
        big = probs[:].rearrange("p a b t -> p (a b t)")
        at16 = H * (D + 2)
        wqT_b = big[0:DH, 0:at16].rearrange("d (h m) -> d h m", h=H)
        vb16 = big[0:DH, at16:at16 + H]
        wpos = big[0:DH, at16 + H:at16 + H + H * POSW].rearrange("d (h m) -> d h m", h=H)
        pe_raw = big[:, 3072:3072 + 2 * T].rearrange("p (a t) -> p a t", a=2)
        at64 = 3072 + 2 * T
        u_row = big[0:D + 2, at64:at64 + D]
        qk_raw = big[0:D + 2, at64 + D:at64 + 3 * D].rearrange("m (a n) -> m a n", a=2)
        wqk_raw = big[0:D, at64 + 3 * D:at64 + 4 * D + 2 * DH]
        at_copies = at64 + 4 * D + 2 * DH
        qk_copies = big[0:D + 2, at_copies:at_copies + 2 * H * D].rearrange("m (h a n) -> m h a n", h=H, a=2)
        qk_c = context_sum[:, 0:6 * P].rearrange("m (k x n) -> m k x n", k=3, x=2)
        activated, gated, hidden = (big[:, 3 * i * HALF:3 * (i + 1) * HALF].rearrange("p (b t) -> p b t", b=3)
                                    for i in range(3))
        cosb = sb("cosb", [P, 2, T])
        work = sb("work", [P, T])
        top8 = sb("top8", [P, NC, 8])
        cut = sb("cut", [P, 21, NC])
        repeat = sb("repeat", [1, 1], I32)
        nmax = sb("nmax", [P, 32])
        rsum = sb("rsum", [P, 32])
        h = sb("h", [P, NC, D])
        xc_at = -(-nc.sbuf_base // 32) * 32
        xc = sb("xc", [P, NC, D])
        sq = sb("sq", [P, NC, D])
        assert nc.sbuf_base == xc_at + 4 * 2 * NC * D
        f_tok = sb("f_tok", [P, NC, D])
        v_tok = f_tok
        xn = sq
        st = sb("st", [P, 8, NC])
        shift, total, unit = st[:, 0], st[:, 1], st[:, 2]
        bases, roots = st[:, 4:6], st[:, 6:8]
        gl = sb("gl", [P, 5, NC, E])
        gates = sb("gates", [P, NC, E])
        gs = sb("gs", [P, 3, NC])

        S = [ctx.enter_context(nc.psum_tensor(f"scores{i}", [P, T], F32)) for i in range(2)]
        R = [ctx.enter_context(nc.psum_tensor(f"ring{i}", [P, HALF], F32)) for i in range(2)]
        C = [ctx.enter_context(nc.psum_tensor(f"context{i}", [P, HALF], F32)) for i in range(2)]

        def f(ap):
            return ap.bitcast(F32)

        gate_a = nc.alloc_sbuf_tensor_at("gate_a", [P, 6, T], F32, offset=base)
        gate_raw = nc.alloc_sbuf_tensor_at("gate_raw", [P, 6 * T], F32, offset=base)
        gate = [gate_a[:, c, :] for c in range(6)] + [cosb[:, c, :] for c in range(2)]

        def load_gate(load):
            by_tile = t["gateT"].rearrange("(c p) t -> p c t", p=P)
            load(gate_a[:], by_tile[:, 0:6, :])
            load(cosb[:], by_tile[:, 6:8, :])

        a_q_hi, a_q_lo, a_keys = (stack_a[:, k * T:(k + 1) * T] for k in range(3))
        rounded_wide = rounded[:].rearrange("p a t -> p (a t)")
        a_k_hi = rounded_wide
        c_stack = q2[:, 0, :], q2[:, 1, :], q2_late[:, 0, :]
        d_hi, d_lo, d_stack = q1[:, 0, 0:T], q1[:, 1, 0:T], q2_late[:, 1, :]

        x_hi_below = v_d[D:P].rearrange("p c d -> p (c d)")
        x_stack = rounded[:].rearrange("p a t -> p (a t)")
        def content_hi(head):
            return rounded_wide if head else stack_a[:, 0:T]

        b_stack = v_d[:].rearrange("p c d -> p (c d)")
        gate_stack = v_d[D:P].rearrange("p c d -> p (c d)")
        raw = gate_raw[:]
        raw_up = raw[:, 0:2 * NQ * P]
        raw_down = raw[:, 2 * NQ * P:2 * NQ * P + NQ * D]
        raw_e = raw[:, 2 * NQ * P + NQ * D:2 * NQ * P + NQ * D + NG * P]
        raw_e_down = work[:]
        e_hi_made = big[:, 6 * T:6 * T + NG * P].bitcast(F32R)
        e_lo_made = stack_a[0:D, 0:NG * P]
        e_down_made = cosb[:].rearrange("p a t -> p (a t)").bitcast(F32R)

        halved_a = nc.alloc_sbuf_tensor_at("halved_a", [P, 4, T], F16, offset=base + 4 * (2 * T + 8))
        halved = [halved_a[:, n, :] for n in range(4)]
        halved += [cosb[:, n // 2, :].bitcast(F16)[:, n % 2 * T:(n % 2 + 1) * T] for n in range(4)]
        unread = nc.alloc_sbuf_tensor_at("unread", [P, 2 * SPLIT, T], F16, offset=probsT_at)
        below = [work[:], nc.alloc_sbuf_tensor_at("below", [P, T], F32, offset=rounded_at)[:]]
        spare = nc.alloc_sbuf_tensor_at("spare", [P, T], F32, offset=xc_at)
        sums, squares, count, seen, low, high, above, missed, edge_low, edge_high, slope, most, least = (
            cut[:, k, :] for k in range(13))
        threshold, inverse = ([cut[:, k + i, :] for i in range(2)] for k in (14, 16))
        chosen, beyond = cut[:, 18, :], cut[:, 19, :]
        all_rows = cut[:, 20, 0:1]

        def half(j):
            return slice(j * HALF, (j + 1) * HALF)

        def chunk(c):
            return slice(c * P, (c + 1) * P)

        def toks(ap):
            return ap.rearrange("p c d -> p (c d)")

        def over_features(ap):
            return ap.rearrange("p (c o) -> p c o", o=1).to_broadcast([P, NC, D])

        with nc.Block() as block:
            zeroed, loaded, made = sem("zeroed"), sem("loaded"), sem("made")
            fills = [(f(v_pad[:]), 0.0)]
            fills += [(fm[D:D + 1, :], 1.0), (fm2[D:D + 1, :], 1.0)]
            fills += [(exponents[:, i], value) for i, value in enumerate(EXPONENTS)] + [(lowest[:], -3.0e38)]
            fills += [(first_key[:, e:e + 1], float(E - e)) for e in range(E)]

            @block.gpsimd
            def _(pool):
                for n, (where, value) in enumerate(fills):
                    if n:
                        pool.wait_ge(zeroed, n)
                    nc.gpsimd.memset(where, value).then_inc(zeroed, 1)
                for i, (hi, low) in enumerate(((k1, k2), (k1_late, k2_late))):
                    pool.wait_ge(sem("tables_hi"), i + 1)
                    for b in range(2):
                        pool.wait_ge(zeroed, len(fills) + 2 * i + b)
                        nc.gpsimd.tensor_tensor(low[0:D, b, :], pe_raw[0:D, i, :], f(hi[0:D, :]), ALU.subtract)\
                            .then_inc(zeroed, 1)

            up_parts = ((region[:, HI][:, 0:2 * NQ * P], raw_up, region[0:D, LO]), (e_hi_made, raw_e, e_lo_made))
            down_parts = ((region[:, HI][:, 2 * NQ * P:3 * NQ * P], raw_down), (e_down_made, raw_e_down))

            def both_halves(dst):
                b = dst.rearrange("p (q n) -> p q n", n=2 * D)
                return b[:, :, 0:D], b[:, :, D:2 * D]

            n_loads, n_weights = [0], [0]

            def loader(engine, signal, count):
                def load(dst, src):
                    count[0] += 1
                    engine.dma_start(dst, src).then_inc(signal, 16)
                return load

            @block.sync
            def _(sp):
                load = loader(sp, sem("weights_loaded"), n_weights)
                load(raw[:, 0:2 * NQ * P + NQ * D + NG * P], t["experts_up"])
                load(raw_e_down, t["experts_down"])
                load = loader(sp, loaded, n_loads)
                load(pe_raw.rearrange("p a t -> p (a t)"), t["positions"])
                load(big[D:P, 0:NQ * P], t["gate_rows"])
                load(masks[:].rearrange("p a t -> p (a t)"), t["masks"])
                load(future[:], t["future"])
                load(b2e[:], t["b2"])
                load(fm[0:D, :], t["xT"][0])
                sp.wait_ge(sem("weights_hi"), 4)
                sp.wait_ge(sem("weights_lo"), 4)
                for dst, src in ((kept["e_hi"][:, NG * P:2 * NG * P], e_down_made), (kept["e_lo"], e_lo_made),
                                 (kept["e_hi"][:, 0:NG * P], e_hi_made)):
                    sp.dma_start(dst, f(src)).then_inc(sem("kept_gelu"), 16)
                by_tile = t["gateT"].rearrange("(c p) t -> p c t", p=P)
                sp.dma_start(gate_a[:], by_tile[:, 0:6, :]).then_inc(sem("first_gate"), 16)
                sp.wait_ge(sem("kept_gelu"), 48)
                sp.dma_start(cosb[:], by_tile[:, 6:8, :]).then_inc(sem("first_gate"), 16)
                for dst, src in ((kept["m_lo"], region[0:D, LO]), (kept["m_hi"], region[:, HI])):
                    sp.dma_start(dst, f(src)).then_inc(sem("kept"), 16)

            @block.scalar
            def _(act):
                load = loader(act, loaded, n_loads)
                load(big[0:DH, 0:at16 + H + H * POSW], t["attention_16"])
                load(big[0:D + 2, at64:at_copies], t["attention_64"])
                load(projections[:], t["projections"])
                load(columns[:], t["columns"])
                act.wait_ge(sem("weights_loaded"), 16 * n_weights[0])
                for dst, src, _ in up_parts:
                    nc.scalar.activation(dst, src, ACT.Copy).then_inc(sem("weights_hi"), 1)
                for dst, src in down_parts:
                    nc.scalar.activation(both_halves(dst)[0], src.rearrange("p (q n) -> p q n", n=D), ACT.Copy)\
                        .then_inc(sem("weights_hi"), 1)
                act.dma_start(h[0:1, 0, 0:1], t["xT"][0, 0:1, 0:1]).then_inc(sem("stored"), 16)
                act.wait_ge(loaded, 16 * n_loads[0])
                for i, hi in enumerate((k1, k1_late)):
                    nc.scalar.activation(hi[:], pe_raw[:, i, :], ACT.Copy).then_inc(sem("tables_hi"), 1)
                nc.scalar.activation(region[D:P, 0:NQ * P], big[D:P, 0:NQ * P], ACT.Copy).then_inc(sem("tables_hi"), 1)

            @block.vector
            def _(dve):
                for i, (hi, src, lo) in enumerate(up_parts):
                    dve.wait_ge(sem("weights_hi"), i + 1)
                    nc.vector.tensor_tensor(lo, src[0:D, :], f(hi[0:D, :]), ALU.subtract).then_inc(sem("weights_lo"), 1)
                for i, (dst, src) in enumerate(down_parts):
                    hi, lo = both_halves(dst)
                    dve.wait_ge(sem("weights_hi"), i + 3)
                    nc.vector.tensor_tensor(lo, src.rearrange("p (q n) -> p q n", n=D), f(hi), ALU.subtract)\
                        .then_inc(sem("weights_lo"), 1)
                dve.wait_ge(loaded, 16 * n_loads[0])
                n = [0]

                def step(ins):
                    ins.then_inc(made, 1)
                    n[0] += 1
                    dve.wait_ge(made, n[0])

                def in_parts(hi, lo, src):
                    step(nc.vector.tensor_copy(hi[0:D + 2], src))
                    step(nc.vector.scalar_tensor_tensor(lo, f(hi[0:D + 2]), parts[0:D + 2, 3:4], src, ALU.mult, ALU.add))
                    step(nc.vector.tensor_copy(hi[D:P], src[0:D]))

                for i in range(2):
                    bqv = wqT_b[:, :, D + i:D + i + 1].rearrange("d h o -> d (h o)")
                    step(nc.vector.tensor_tensor(bqv, bqv, vb16, ALU.add))
                step(nc.vector.tensor_scalar(wqT_b[:], wqT_b[:], 0.125, None, ALU.mult))
                step(nc.vector.tensor_tensor(qk_raw[D:D + 2, 0, :], qk_raw[D:D + 2, 0, :], u_row[D:D + 2, :], ALU.add))
                step(nc.vector.tensor_scalar(qk_raw[:, 0, :], qk_raw[:, 0, :], 0.125, None, ALU.mult))
                for i in range(2):
                    nc.vector.tensor_copy(
                        qk_copies[:, :, i, :].rearrange("m h (k d) -> m h k d", k=DUP),
                        qk_raw[:, i, :].rearrange("m (h o d) -> m h o d", h=H, o=1).to_broadcast([D + 2, H, DUP, DH]))\
                        .then_inc(made, 1)
                    n[0] += 1
                dve.wait_ge(made, n[0])
                in_parts(qkw_hi[:], qkw_lo[:], qk_copies.rearrange("m h a n -> m h (a n)"))
                dve.wait_ge(made, n[0])
                step(nc.vector.tensor_scalar(wqk_raw[:, 0:D], wqk_raw[:, 0:D], 0.25, None, ALU.mult))
                for k in range(3):
                    if k < 2:
                        src = wqk_raw[:, 0:D].rearrange("m (g t d) -> m t g d", g=2, t=2)[:, k]
                    else:
                        src = wqk_raw[:, D:D + 2 * DH].rearrange("m (g d) -> m g d", g=2)
                    src = src.rearrange("m g (o d) -> m g o d", o=1)
                    out_ = qk_c[:, k].rearrange("m x (g k d) -> m x g k d", g=2, k=DUP)
                    for x, d0, s0, w in ((0, 0, 0, DH), (1, 0, DH // 2, DH // 2), (1, DH // 2, 0, DH // 2)):
                        step(nc.vector.tensor_copy(out_[:, x, :, :, d0:d0 + w],
                                                   src[:, :, :, s0:s0 + w].to_broadcast([D, 2, DUP, w])))
                step(nc.vector.tensor_copy(qk_hi[0:D], qk_c))
                step(nc.vector.tensor_copy(qk_hi[D:P], f(qk_hi[0:D])))
                step(nc.vector.tensor_tensor(qk_lo, qk_c, f(qk_hi[0:D]), ALU.subtract))
                step(nc.vector.tensor_copy(ident_bf[:], ident[:]))
                for hh in range(H):
                    dve.wait_ge(sem("posw_ready"), hh + 1)
                    in_parts(posw_hi[:, hh, :], posw_lo[:, hh, :], R[hh % 2][0:D + 2, 0:POSW])
                    nc.vector.drain().then_inc(sem("posw_copied"), 1)

            @block.tensor
            def _(pe):
                pe.wait_ge(made, 3)
                for hh in range(H):
                    if hh >= 2:
                        pe.wait_ge(sem("posw_copied"), hh - 1)
                    nc.tensor.matmul(R[hh % 2][0:D + 2, 0:POSW], wqT_b[:, hh, :], wpos[:, hh, :],
                                     start=True, stop=True).then_inc(sem("posw_ready"), 1)

        class Attend:

            def __init__(self, name, groups, causal=False, prep=False):
                self.name, self.groups, self.causal = name, groups, causal
                self.scores_read = "scores_used" if name == "D" else "probs"
                self.steps = attend_steps(groups, lambda g: 4 * (g % 2) + 3 if causal else NC - 1, name == "B", prep)
                if name == "D":
                    self.steps.sort(key=lambda s: s[0] != "S")
                self.t_at = {s[1:]: i for i, s in enumerate(x for x in self.steps if x[0] == "T")}
                self.ring = [s for s in self.steps if s[0] in "TF"]
                self.slot = {s: k for k, s in enumerate(self.ring)}
                self.wide = [s for s in self.steps if s[0] in "SP"]
                self.turn = {s: k for k, s in enumerate(self.wide)}

            def s(self, what):
                return sem(f"{self.name}_{what}")

            def t_until(self, g):
                return sum(1 for (gg, j) in self.t_at if gg <= g)

            def wait_slot(self, eng, k):
                if k < 2:
                    return
                kind, x, j = self.ring[k - 2]
                if kind == "T":
                    eng.wait_ge(self.s("lo"), self.t_at[(x, j)] + 1)
                else:
                    eng.wait_ge(self.s("fixed"), 2 * x + 2)

            def wait_wide(self, eng, k):
                if k >= 2:
                    kind, x, j = self.wide[k - 2]
                    if kind == "S":
                        eng.wait_ge(self.s(self.scores_read), x + 1)
                    else:
                        eng.wait_ge(self.s("prep_dve"), 4 * x + (1, 2, 4)[j])

            def bank(self, *step):
                return S[self.turn[step] % 2]

            def width(self, x, j):
                return max(0, j - 4 * (x % 2)) * P if self.causal else 0

            def tensor(self, pe, scores, values, fix=None, prepare=None, make_values=None, after_scores=None):
                for kind, x, j in self.steps:
                    if after_scores and (kind, x, j) == ("T", 0, 0):
                        after_scores()
                    if kind == "P":
                        self.wait_wide(pe, self.turn[(kind, x, j)])
                        prepare(x, j, self.bank(kind, x, j)).then_inc(self.s("prep"), 1)
                    elif kind == "S":
                        self.wait_wide(pe, self.turn[(kind, x, j)])
                        ins = scores(x)
                        if fix is None:
                            ins.then_inc(self.s("scores"), 1)
                    elif kind == "V":
                        make_values()
                    elif kind == "F":
                        self.wait_slot(pe, self.slot[(kind, x, j)])
                        fix(x, R[self.slot[(kind, x, j)] % 2]).then_inc(self.s("scores"), 1)
                    elif kind == "T":
                        k, w = self.slot[(kind, x, j)], self.width(x, j)
                        if j == 0:
                            pe.wait_ge(self.s("probs"), 4 * x + 4)
                        self.wait_slot(pe, k)
                        for a in range(w // P, 4):
                            ins = nc.tensor.transpose(R[k % 2][:, chunk(a)], probs[:, x % 2, a, chunk(j)], ident[:])
                        ins.then_inc(self.s("turned"), 1)
                    else:
                        m, w = self.t_at[(x, j)], self.width(x, j)
                        last = 4 * (x % 2) + 3 if self.causal else NC - 1
                        if m == 0:
                            pe.wait_ge(self.s("v_hi"), 1 if self.name == "D" else H)
                            pe.wait_ge(self.s("v_lo"), 1 if self.name == "D" else H)
                        pe.wait_ge(self.s("hi"), m + 1)
                        nc.tensor.matmul(C[x % 2][:, w:HALF], values(x, j), probsT[:, 0, m % SPLIT, w:HALF],
                                         start=(x < 2 and j == 0), stop=False, skip_group_check=True)
                        pe.wait_ge(self.s("lo"), m + 1)
                        nc.tensor.matmul(C[x % 2][:, w:HALF], values(x, j), probsT[:, 1, m % SPLIT, w:HALF], start=False,
                                         stop=(x >= self.groups - 2 and j == last),
                                         skip_group_check=True).then_inc(self.s("products"), 1)

            def take_hi(self, act, x, j):
                m, k, w = self.t_at[(x, j)], self.slot[("T", x, j)], self.width(x, j)
                act.wait_ge(self.s("turned"), m + 1)
                if m >= SPLIT:
                    act.wait_ge(self.s("products"), m - SPLIT + 1)
                nc.scalar.activation(probsT[:, 0, m % SPLIT, w:HALF], R[k % 2][:, w:HALF], ACT.Copy)\
                    .then_inc(self.s("hi"), 1)

            def take_lo(self, dve, x, j):
                m, k, w = self.t_at[(x, j)], self.slot[("T", x, j)], self.width(x, j)
                dve.wait_ge(self.s("hi"), m + 1)
                nc.vector.tensor_tensor(probsT[:, 1, m % SPLIT, w:HALF], R[k % 2][:, w:HALF],
                                        f(probsT[:, 0, m % SPLIT, w:HALF]), ALU.subtract).then_inc(self.s("lo"), 1)

            def n_products(self):
                return len(self.t_at)

        AB = Attend("B", 2 * H, prep=True)
        AC = Attend("C", 2 * H, causal=True)
        AD = Attend("D", 2)

        lasting = set(sems) | {"stored"}
        with nc.Fori(0, B) as seq:
            with nc.Block() as block:

                @block.sync
                def _(sp):
                    for dst, src in ((turn_cos, "rot_cos"), (turn_sin, "rot_sin")):
                        sp.dma_start(dst[:], t[src]).then_inc(sem("rot_loaded"), 16)
                    sp.wait_ge(sem("kept"), 32)
                    for dst, src in ((region[0:D, LO], "m_lo"), (region[:, HI], "m_hi")):
                        sp.dma_start(f(dst), kept[src]).then_inc(sem("M_loaded"), 16)
                    for hh in range(H):
                        b = hh % 2
                        copy = lambda dst, src: sp.dma_start(f(dst), f(src)).then_inc(sem("B_copied"), 16)
                        sp.wait_ge(sem("B_prep_act"), 3 * hh + (1 if hh else 2))
                        copy(q2[0:D, b, :], q1[0:D, b, 0:T])
                        copy(q2_late[0:D, b, 0:T - 1], q1[0:D, b, 1:T])
                        sp.wait_ge(sem("B_prep_dve"), 4 * hh + 3)
                        copy(q2_late[D:P, b, :], q2[D:P, b, :])
                        sp.wait_ge(sem("B_prep_dve"), 4 * hh + 4)
                        copy(k2_late[D:P, b, :], k2[D:P, b, :])
                    for dst, src in ((turn_cos, "rope_cos"), (turn_sin, "rope_sin")):
                        sp.dma_start(dst[:], t[src]).then_inc(sem("rope_loaded"), 16)
                    sp.wait_ge(sem("M_down"), 2 * NQ)
                    for dst, src in ((region[0:D, 0:NG * P], "e_lo"), (region[:, HI][:, 0:2 * NG * P], "e_hi")):
                        sp.dma_start(f(dst), kept[src]).then_inc(sem("E_loaded"), 16)
                    sp.wait_ge(sem("E_logits"), 1)
                    sp.wait_ge(sem("E_x_lo"), 1)
                    sp.dma_start(fm[0:D, :], t["xT"][bass.ds(seq + 1, 1)].rearrange("o d t -> (o d) t"))\
                      .then_inc(sem("x_loaded"), 16)
                    sp.wait_ge(sem("D_products"), AD.n_products())
                    load_gate(lambda dst, src: sp.dma_start(dst, src).then_inc(sem("gate_loaded"), 16))
                    sp.wait_ge(sem("rot_loaded"), 32)
                    sp.wait_ge(sem("M_loaded"), 32)
                    sp.wait_ge(sem("rope_loaded"), 32)
                    sp.wait_ge(sem("E_loaded"), 32)
                    sp.wait_ge(sem("gate_loaded"), 32)
                    sp.wait_ge(sem("x_loaded"), 16)
                    sp.wait_ge(sem("result"), 1)
                    sp.dma_start(out[bass.ds(seq, 1)].rearrange("o (c p) d -> p (o c) d", p=P), h[:])\
                      .then_inc(sem("stored"), 16)

                @block.gpsimd
                def _(pool):
                    def hidden_lo(name, rounds):
                        for n in range(rounds):
                            pool.wait_ge(sem(f"{name}_hi"), n + 1)
                            if n:
                                pool.wait_ge(sem(f"{name}_lo"), n)
                            if n >= SPLIT:
                                pool.wait_ge(sem(f"{name}_down"), n - SPLIT + 1)
                            nc.gpsimd.tensor_tensor(probsT[:, 1, n % SPLIT, :], hidden[:, n % 3, :],
                                                    f(probsT[:, 0, n % SPLIT, :]), ALU.subtract)\
                                .then_inc(sem(f"{name}_lo"), 1)

                    for n, (k, p) in enumerate(POWERS):
                        pool.wait_ge(sem("power_base"), n + 1)
                        nc.gpsimd.tensor_tensor(roots[:, 0:k], bases[:, 0:k], exponents[:, p:p + k], ALU.pow)\
                            .then_inc(sem("powered"), 1)
                        if n == 0:
                            for i, (pad, value) in enumerate(((f(ones_stack[D:D + 2, :]), 1.0), (f(q1[:, :, T:T + 1]), 0.0),
                                                              (f(q2_late[0:D, :, T - 1:T]), 0.0))):
                                if i:
                                    pool.wait_ge(sem("padded"), i)
                                else:
                                    pool.wait_ge(sem("powered"), 1)
                                nc.gpsimd.memset(pad, value).then_inc(sem("padded"), 1)
                        if n == 0:
                            turned = sem("B_prep_turn")
                            for hh in range(1, H):
                                pool.wait_ge(sem("B_prep_dve"), 4 * hh + 2)
                                pool.wait_ge(turned, 2 * hh)
                                pool.wait_ge(sem("B_prep_act"), 3 * hh if hh == 1 else 3 * hh - 1)
                                nc.gpsimd.tensor_tensor(work[:], cosb[:, 0, :], cosb[:, 1, :], ALU.add).then_inc(turned, 1)
                                pool.wait_ge(turned, 2 * hh + 1)
                                pool.wait_ge(sem("B_prep_act"), 3 * hh + 2)
                                nc.gpsimd.tensor_tensor(q1[D:P, hh % 2, 0:T], work[D:P, :], f(rounded_wide[D:P, :]), ALU.subtract)\
                                    .then_inc(turned, 1)
                            pool.wait_ge(sem("B_prep"), PREP * H)
                            pool.wait_ge(sem("padded"), 3)
                            nc.gpsimd.memset(fm2[D:D + 1, :], 1.0).then_inc(sem("padded"), 1)
                        if n == SEARCH_POWER:
                            for m in range(BY_VECTOR, NC):
                                pool.wait_ge(sem("D_signs"), (NC - BY_VECTOR) * (COUNTS - 1) + m - BY_VECTOR + 1)
                                if m > BY_VECTOR:
                                    pool.wait_ge(sem("D_top"), TOP_ORDER.index(m - 1) + 1)
                                nc.gpsimd.tensor_tensor(spare[:], unread[:, 3 + m - BY_VECTOR, :], probs[:, m // 4, m % 4, :],
                                                        ALU.mult).then_inc(sem("D_below"), 1)
                        for name, power, rounds in (("M", SWIGLU_POWER, 2 * NQ), ("E", len(POWERS) - 1, 2 * NG)):
                            if n == power:
                                if name == "E":
                                    pool.wait_ge(sem("D_products"), AD.n_products())
                                pool.wait_ge(sem("powered"), n + 1)
                                nc.gpsimd.memset(f(gate_stack), 0.0).then_inc(sem(f"{name}_cleared"), 1)
                                pool.wait_ge(sem(f"{name}_cleared"), 1)
                                hidden_lo(name, rounds)

                @block.tensor
                def _(pe):
                    mm = nc.tensor.matmul

                    def project(dst, w, src, k, done):
                        for j in range(2):
                            ins = mm(dst(j), w, src[0:k, half(j)], start=True, stop=True)
                        ins.then_inc(done, 1)

                    def by_token(dst, src, w, k, n, done):
                        for c in range(NC):
                            ins = mm(dst[:, c * n:(c + 1) * n], src[0:k, chunk(c)], w, start=True, stop=True)
                        ins.then_inc(done, 1)

                    def up(bank, lo, hi, j):
                        mm(bank, hi, x_stack[:, half(j)], start=True, stop=False)
                        return mm(bank, lo, x_stack[0:D, half(j)], start=False, stop=True)

                    def turn(src, done):
                        for c in range(NC):
                            ins = nc.tensor.transpose(S[0][0:D, chunk(c)], src[:, c, :], ident[:])
                        ins.then_inc(done, 1)

                    def normalise(x):
                        pe.wait_ge(sem(f"{x}_recip"), 1)
                        for i in range(NC):
                            ins = nc.tensor.transpose(S[0][0:D, chunk(i)], work[:, i * D:(i + 1) * D], ident[:])
                        ins.then_inc(sem(f"{x}_spread"), 1)

                    project(lambda j: S[0][:, half(j)], tok_w["q"][:], fm, D + 1, sem("A_q"))
                    project(lambda j: S[1][:, half(j)], tok_w["k"][:], fm, D + 1, sem("A_k"))
                    by_token(R[0], fm, tok_w["v"][:], D + 1, D, sem("A_v"))
                    pe.wait_ge(sem("A_q_hi"), 1)
                    pe.wait_ge(sem("A_split"), 2)
                    for s in range(NC + 1):
                        if s < NC:
                            if s >= 2:
                                pe.wait_ge(sem("A_gated"), s - 1)
                            for j in range(2):
                                mm(S[s % 2][:, half(j)], a_keys[:, chunk(s)], a_q_hi[:, half(j)],
                                   start=True, stop=False)
                                ins = mm(S[s % 2][:, half(j)], a_keys[:, chunk(s)], a_q_lo[:, half(j)],
                                         start=False, stop=True)
                            ins.then_inc(sem("A_scores"), 1)
                        if s >= 1:
                            pe.wait_ge(sem("A_gated"), s)
                            if s == 1:
                                pe.wait_ge(sem("A_v_copied"), 1)
                            for j in range(2):
                                ins = mm(C[j][0:D, :], v_tok[:, s - 1, :], probs[:, 0, (s - 1) % 2, half(j)],
                                         start=(s == 1), stop=(s == NC))
                            ins.then_inc(sem("A_products"), 1)
                    pe.wait_ge(sem("A_mix_copied"), 2)
                    by_token(R[1], fm2, tok_w["o"][:], D + 1, D, sem("A_out"))

                    pe.wait_ge(sem("normalised"), 1)
                    turn(xn, sem("x_turned"))
                    pe.wait_ge(sem("B_fm"), 4)
                    pe.wait_ge(sem("padded"), 1)
                    def prepare_b(hh, k, bank):
                        hi, lo = (qkw_hi, qkw_lo) if k == 2 else (posw_hi, posw_lo)
                        w = slice(0, P) if k == 2 else slice(k * D // 2, k * D // 2 + P)
                        for j in range(2):
                            mm(bank[:, half(j)], lo[:, hh, w], ones_stack[:, half(j)], start=True, stop=False)
                            ins = mm(bank[:, half(j)], hi[:, hh, w], b_stack[:, half(j)], start=False, stop=True)
                        return ins

                    def late_scores(dst, b, i, j0, j1):
                        mm(dst, q1[:, b, i * P + 1:(i + 1) * P + 1], k1_late[:, j0:j1], start=True, stop=False,
                           skip_group_check=True)
                        return mm(dst, q2_late[:, b, chunk(i)], k2_late[:, b, j0:j1], start=False, stop=True,
                                  skip_group_check=True)

                    def scores_b(n):
                        hh, i = n // NC, n % NC
                        b, bank = hh % 2, AB.bank("S", n, 0)
                        if i == 0:
                            pe.wait_ge(sem("B_prep_dve"), 4 * (hh + 1))
                            pe.wait_ge(sem("B_prep_act"), 3 * (hh + 1))
                            pe.wait_ge(sem("B_prep_turn"), 2 * (hh + 1))
                            pe.wait_ge(sem("B_copied"), 64 * (hh + 1))
                        if n == 0:
                            pe.wait_ge(sem("padded"), 3)
                        edge = (i + 1) * P
                        for j0, j1 in ((0, min(edge, HALF)), (HALF, edge)):
                            if j1 > j0:
                                mm(bank[:, j0:j1], q1[:, b, chunk(i)], k1[:, j0:j1], start=True, stop=False,
                                   skip_group_check=True)
                                mm(bank[:, j0:j1], q2[:, b, chunk(i)], k2[:, b, j0:j1], start=False, stop=True,
                                   skip_group_check=True)
                        for j0, j1 in ((edge, HALF), (max(edge, HALF), T)):
                            if j1 > j0:
                                late_scores(bank[:, j0:j1], b, i, j0, j1)

                    def fix_b(n, bank):
                        hh, i = n // NC, n % NC
                        b, j1 = hh % 2, min((i + 1) * P + 2, T)
                        late_scores(bank[:, 0:j1 - i * P], b, i, i * P, j1)
                        return mm(bank[:, 256:256 + j1 - i * P], q2[D:P, b, chunk(i)], k2[D:P, b, i * P:j1],
                                  start=True, stop=True, skip_group_check=True)

                    AB.tensor(pe, scores_b, lambda x, j: v_pad[:, j, x // 2, :], fix_b, prepare_b,
                              lambda: by_token(C[0], fm, wv_b[:], D + 1, D, sem("B_v")))
                    normalise("B")
                    pe.wait_ge(sem("B_context"), 2)
                    pe.wait_ge(sem("padded"), 4)
                    by_token(R[0], fm2, wout_b[:], D + 1, D, sem("B_out"))

                    pe.wait_ge(sem("normalised"), 2)
                    turn(xn, sem("x_turned"))
                    def project_c(k, x, banks):
                        for j in range(2):
                            mm(banks[j], qk_lo[:, k, x, :], x_hi_below[:, half(j)], start=True, stop=False)
                            ins = mm(banks[j], qk_hi[:, k, x, :], x_stack[:, half(j)], start=False, stop=True)
                        ins.then_inc(sem("C_proj"), 1)

                    pe.wait_ge(sem("C_fm"), 2)
                    pe.wait_ge(sem("C_rope"), 1)
                    project_c(1, 0, [R[j][:] for j in range(2)])
                    project_c(1, 1, [C[j][:] for j in range(2)])
                    pe.wait_ge(sem("C_fm"), 3)
                    project_c(0, 0, [S[0][:, half(j)] for j in range(2)])
                    project_c(0, 1, [S[1][:, half(j)] for j in range(2)])
                    pe.wait_ge(sem("C_rope"), 5)
                    by_token(C[0], fm, wv_c[:], D, 2 * DH, sem("C_v"))
                    for x in range(2):
                        pe.wait_ge(sem("C_rope"), 7 + x)
                        project_c(2, x, [S[x][:, half(j)] for j in range(2)])

                    def scores_c(n):
                        hh, i = n // NC, n % NC
                        rows, edge = slice(D * (hh // 2), D * (hh // 2) + D), (i + 1) * P
                        for j0, j1 in ((0, min(edge, HALF)), (HALF, edge)):
                            if j1 > j0:
                                mm(S[n % 2][:, j0:j1], c_stack[hh % 2][rows, chunk(i)], c_stack[2][rows, j0:j1],
                                   start=True, stop=False, skip_group_check=True)
                        return mm(S[n % 2][:, chunk(i)], ident_bf[:], future[:], start=False, stop=True,
                                  skip_group_check=True)

                    pe.wait_ge(sem("C_rope"), 15)
                    AC.tensor(pe, scores_c, lambda x, j: v_pad[:, j, x // 2, :])
                    normalise("C")
                    pe.wait_ge(sem("C_context"), 2)
                    by_token(R[0], fm2, wo_c[:], D, D, sem("C_out"))

                    pe.wait_ge(sem("normalised"), 3)
                    turn(xn, sem("x_turned"))
                    pe.wait_ge(sem("M_fm"), 2)
                    by_token(R[0], fm, router[:], D, E, sem("M_logits"))

                    def spread_gates(name):
                        pe.wait_ge(sem(f"{name}_gates"), 1)
                        for c in range(NC):
                            ins = nc.tensor.transpose(C[c // 4][0:E, chunk(c % 4)], gates[:, c, :], ident[:])
                        ins.then_inc(sem(f"{name}_gates_turned"), 1)

                    def spread(name, n, q, j):
                        mm(R[n % 2][:], gate_rows[:, q, :], gate_stack[:, half(j)], start=True, stop=True)\
                            .then_inc(sem(f"{name}_spread_gate"), 1)

                    def down(name, m, per_half, weights):
                        j, q = m // per_half, m % per_half
                        pe.wait_ge(sem(f"{name}_lo"), m + 1)
                        mm(C[j][:], weights[:, q, :], probsT[:, 0, m % SPLIT, :], start=(q == 0), stop=False,
                           skip_group_check=True)
                        if name == "E" and q == 0:
                            mm(C[j][0:D, :], b2e[:], fm2[0:E, half(j)], start=False, stop=False, skip_group_check=True)
                        mm(C[j][:], weights[:, q, :], probsT[:, 1, m % SPLIT, :], start=False,
                           stop=(q == per_half - 1), skip_group_check=True).then_inc(sem(f"{name}_down"), 1)

                    def sum_by_token(name):
                        for j in range(2):
                            pe.wait_ge(sem(f"{name}_summed"), j + 1)
                            for c in range(4 * j, 4 * j + 4):
                                ins = nc.tensor.transpose(S[0][:, c * D:(c + 1) * D], context_sum[:, chunk(c)], ident[0:D, 0:D])
                        ins.then_inc(sem(f"{name}_by_token"), 1)

                    def gate_and_up(n):
                        if n >= 2:
                            pe.wait_ge(sem("M_hidden"), n - 1)
                        for w, done in enumerate((sem("M_gate"), sem("M_up"))):
                            up(S[n % 2][:, half(w)], m_lo[:, w, n % NQ, :], m_hi[:, w, n % NQ, :], n // NQ).then_inc(done, 1)

                    pe.wait_ge(sem("M_x_lo"), 1)
                    pe.wait_ge(sem("M_loaded"), 32)
                    gate_and_up(0)
                    gate_and_up(1)
                    spread_gates("M")
                    pe.wait_ge(sem("M_gates_lo"), 2)
                    spread("M", 0, 0, 0)
                    for n in range(2 * NQ + SPLIT):
                        m = n + 1
                        if m < 2 * NQ:
                            if m >= 2:
                                pe.wait_ge(sem("M_gated"), m - 1)
                            spread("M", m, m % NQ, m // NQ)
                        if n >= SPLIT:
                            down("M", n - SPLIT, NQ, m_down)
                        if n + 2 < 2 * NQ:
                            gate_and_up(n + 2)
                    sum_by_token("M")

                    pe.wait_ge(sem("normalised"), 4)
                    turn(f_tok, sem("x_turned"))
                    pe.wait_ge(sem("D_fm"), 1)
                    by_token(R[0], fm, w_d[:], D + 1, D, sem("D_v"))
                    pe.wait_ge(sem("D_unit_x"), 2)
                    for c in range(NC):
                        ins = nc.tensor.transpose(S[0][:, chunk(c)], work[:, chunk(c)], ident[:])
                    ins.then_inc(sem("D_turned_unit"), 1)
                    pe.wait_ge(sem("D_unit_split"), 2)
                    pe.wait_ge(sem("D_unit_hi"), 1)

                    def every_row():
                        pe.wait_ge(sem("D_ok"), 1)
                        mm(S[0][0:1, 0:1], all_rows, exponents[:, 2, 0:1], start=True, stop=True)\
                            .then_inc(sem("D_all_ok"), 1)

                    def scores_d(n):
                        for j in range(2):
                            mm(S[n % 2][:, half(j)], d_stack[:, chunk(n)], d_hi[:, half(j)], start=True, stop=False)
                            ins = mm(S[n % 2][:, half(j)], d_stack[:, chunk(n)], d_lo[:, half(j)],
                                     start=False, stop=True)
                        return ins

                    AD.tensor(pe, scores_d, lambda x, j: v_d[:, j, :], after_scores=every_row)
                    pe.wait_ge(sem("D_context"), 2)
                    for c in range(NC):
                        ins = nc.tensor.transpose(S[0][:, c * D:(c + 1) * D], context_sum[:, chunk(c)], ident[0:D, 0:D])
                    ins.then_inc(sem("D_by_token"), 1)

                    pe.wait_ge(sem("normalised"), 5)
                    turn(f_tok, sem("x_turned"))
                    pe.wait_ge(sem("E_fm"), 2)
                    by_token(R[0], fm, wg_e[:], D + 1, E, sem("E_logits"))

                    def up_e(n):
                        if n >= 4:
                            pe.wait_ge(sem("E_activated"), n - 3)
                        up(S[n // 2 % 2][:, half(n % 2)], e_lo[:, n % NG, :], e_hi[:, n % NG, :], n // NG)\
                            .then_inc(sem("E_up"), 1)

                    pe.wait_ge(sem("E_x_lo"), 1)
                    pe.wait_ge(sem("E_loaded"), 32)
                    for n in range(4):
                        up_e(n)
                    spread_gates("E")
                    pe.wait_ge(sem("E_gates_lo"), 2)
                    pe.wait_ge(sem("E_gates_copied"), 2)
                    for n in range(2 * NG + SPLIT):
                        if n < 2 * NG and n % 2 == 0:
                            if n >= 4:
                                pe.wait_ge(sem("E_hidden"), n - 2)
                            spread("E", n // 2, n // 2 % E, n // NG)
                        if n >= SPLIT:
                            down("E", n - SPLIT, NG, e_down)
                        if n + 4 < 2 * NG:
                            up_e(n + 4)
                    sum_by_token("E")

                @block.scalar
                def _(act):
                    fn = nc.scalar.activation

                    def copy(dst, src):
                        return fn(dst, src, ACT.Copy)

                    def softmax_of(att, width):
                        scored = []

                        def exponential():
                            if scored:
                                x = scored.pop()
                                g, a = x // 4, x % 4
                                act.wait_ge(att.s("max"), x + 1)
                                if g >= 2:
                                    act.wait_ge(att.s("turned"), att.t_until(g - 2))
                                w = width(x)
                                fn(probs[:, g % 2, a, 0:w], att.bank("S", x, 0)[:, 0:w], ACT.Exp, bias=nmax[:, x:x + 1],
                                   accum_out=rsum[:, x:x + 1])\
                                    .then_inc(att.s("probs"), 1)

                        for kind, x, j in att.steps:
                            if kind == "S":
                                exponential()
                                if att is AB and x % NC == 4:
                                    round_turned()
                                scored.append(x)
                            elif kind == "T":
                                if x == att.groups - 1:
                                    exponential()
                                att.take_hi(act, x, j)
                            elif kind == "P":
                                exponential()
                                prepare_b(x, j)
                            elif kind == "V":
                                act.wait_ge(sem("B_v"), 1)
                                values_hi("B", D, lambda hh: hh)

                    act.wait_ge(sem("A_q"), 1)
                    copy(a_q_hi, S[0][:]).then_inc(sem("A_q_hi"), 1)
                    act.wait_ge(sem("A_k"), 1)
                    copy(a_k_hi, S[1][:]).then_inc(sem("A_k_hi"), 1)
                    act.wait_ge(sem("A_v"), 1)
                    copy(toks(v_tok[:]), R[0][:]).then_inc(sem("A_v_copied"), 1)
                    act.wait_ge(sem("A_products"), NC)
                    for j in range(2):
                        copy(fm2[0:D, half(j)], C[j][0:D, :]).then_inc(sem("A_mix_copied"), 1)
                    act.wait_ge(sem("x_turned"), 1)
                    fn(fm[0:D, :], S[0][0:D, :], ACT.Identity, bias=affine[:, 1:2], scale=affine[:, 0:1])\
                        .then_inc(sem("B_fm"), 1)
                    fn(ones_stack[0:D, :], S[0][0:D, :], ACT.Identity, bias=affine[:, 1:2], scale=affine[:, 0:1])\
                        .then_inc(sem("B_fm"), 1)

                    def values_hi(x, width, group):
                        for hh in range(H):
                            src = C[0][:, 0:NC * width].rearrange("p (c d) -> p c d", d=width)
                            g = group(hh)
                            copy(v_pad[:, :, hh, hh * DH:(hh + 1) * DH], src[:, :, g * DH:(g + 1) * DH])\
                                .then_inc(sem(f"{x}_v_hi"), 1)

                    turned_due = []

                    def round_turned():
                        if turned_due:
                            hh = turned_due.pop()
                            act.wait_ge(sem("B_prep_turn"), 2 * hh + 1)
                            copy(q1[0:D, hh % 2, 0:T], work[0:D, :]).then_inc(sem("B_prep_act"), 1)
                            if hh:
                                act.wait_ge(sem("B_prep_dve"), 4 * hh)
                            copy(rounded_wide[D:P, :], work[D:P, :]).then_inc(sem("B_prep_act"), 1)

                    def prepare_b(hh, k):
                        if k == 1:
                            turned_due.append(hh)
                        elif k == 2:
                            act.wait_ge(sem("B_prep"), PREP * hh + k + 1)
                            if hh:
                                act.wait_ge(sem("B_prep_turn"), 2 * hh + 2)
                            copy(content_hi(hh), AB.bank("P", hh, k)[:]).then_inc(sem("B_prep_act"), 1)
                            if hh == 0:
                                round_turned()

                    softmax_of(AB, lambda n: T)
                    def context(x):
                        act.wait_ge(sem(f"{x}_products"), {"B": AB, "C": AC, "D": AD}[x].n_products())
                        for j in range(2):
                            copy(context_sum[:, half(j)], C[j][D:P, :]).then_inc(sem(f"{x}_ctx_copied"), 1)

                    context("B")
                    act.wait_ge(sem("x_turned"), 2)
                    for dst in (x_stack, fm):
                        if dst is fm:
                            act.wait_ge(sem("C_fm"), 1)
                            copy(x_hi_below, f(x_stack[0:D, :])).then_inc(sem("C_fm"), 1)
                            act.wait_ge(sem("C_rope"), 1)
                        fn(dst[0:D, :], S[0][0:D, :], ACT.Identity, scale=affine[:, 2:3]).then_inc(sem("C_fm"), 1)
                    for n, k in enumerate((1, 0, 2)):
                        act.wait_ge(sem("C_rope"), (6, 10, 14)[n])
                        copy(stack_a[:, k * T:(k + 1) * T], work[:]).then_inc(sem("C_rounded"), 1)
                        if k == 0:
                            act.wait_ge(sem("C_v"), 1)
                            values_hi("C", 2 * DH, lambda hh: hh // 2)
                    softmax_of(AC, lambda n: (n % NC + 1) * P)
                    context("C")
                    act.wait_ge(sem("x_turned"), 3)
                    fn(fm[0:D, :], S[0][0:D, :], ACT.Identity, scale=affine[:, 3:4]).then_inc(sem("M_fm"), 1)
                    fn(x_stack[0:D, :], S[0][0:D, :], ACT.Identity, scale=affine[:, 3:4]).then_inc(sem("M_fm"), 1)
                    act.wait_ge(sem("M_shifted"), 1)
                    fn(gl[:, 1], gl[:, 1], ACT.Exp).then_inc(sem("M_exp"), 1)

                    def gates_hi(name):
                        act.wait_ge(sem(f"{name}_gates_turned"), 1)
                        act.wait_ge(sem(f"{name}_cleared"), 1)
                        for j in range(2):
                            copy(gate_stack[0:E, half(j)], C[j][0:E, :]).then_inc(sem(f"{name}_gates_hi"), 1)

                    def hidden_hi(name, n):
                        act.wait_ge(sem(f"{name}_hidden"), n + 1)
                        if n >= SPLIT:
                            act.wait_ge(sem(f"{name}_down"), n - SPLIT + 1)
                        copy(probsT[:, 0, n % SPLIT, :], hidden[:, n % 3, :]).then_inc(sem(f"{name}_hi"), 1)

                    def experts_sum(name, per_half):
                        for j in range(2):
                            act.wait_ge(sem(f"{name}_down"), per_half * (j + 1))
                            copy(context_sum[:, half(j)], C[j][D:P, :]).then_inc(sem(f"{name}_sum_copied"), 1)

                    for n in range(2 * NQ + 1):
                        if n < 2 * NQ:
                            act.wait_ge(sem("M_gate"), n + 1)
                            if n >= 3:
                                act.wait_ge(sem("M_gated"), n - 2)
                            fn(activated[:, n % 3, :], S[n % 2][:, half(0)], ACT.Silu).then_inc(sem("M_silu"), 1)
                        if n == 0:
                            gates_hi("M")
                        else:
                            hidden_hi("M", n - 1)
                    experts_sum("M", NQ)
                    act.wait_ge(sem("x_turned"), 4)
                    copy(fm[0:D, :], S[0][0:D, :]).then_inc(sem("D_fm"), 1)
                    act.wait_ge(sem("D_v"), 1)
                    copy(v_d[:, :, 0:D], R[0][:].rearrange("p (c d) -> p c d", d=D)).then_inc(sem("D_v_hi"), 1)
                    act.wait_ge(sem("D_turned_unit"), 1)
                    copy(d_hi, S[0][:]).then_inc(sem("D_unit_hi"), 1)

                    for x in range(NC):
                        act.wait_ge(AD.s("scores"), x + 1)
                        fn(probs[:, x // 4, x % 4, :], S[x % 2][:], ACT.Copy, accum_out=sums[:, x:x + 1])\
                            .then_inc(AD.s("scores_used"), 1)
                    for x in range(BY_VECTOR, NC):
                        if x == BY_VECTOR:
                            act.wait_ge(AD.s("scores_used"), NC)
                        copy(halved[x], probs[:, x // 4, x % 4, :]).then_inc(sem("D_halved"), 1)
                    for k in range(COUNTS):
                        act.wait_ge(sem("D_threshold"), k + 1)
                        for x in range(BY_VECTOR, NC):
                            if k == 0 and x == BY_VECTOR:
                                act.wait_ge(sem("D_halved"), NC - BY_VECTOR)
                            fn(unread[:, 3 + x - BY_VECTOR, :], halved[x], ACT.Sign, bias=threshold[k % 2][:, x:x + 1],
                               scale=-1.0, accum_out=count[:, x:x + 1]).then_inc(sem("D_signs"), 1)

                    def sparse_exp(x):
                        act.wait_ge(AD.s("sparse"), x + 1)
                        row = probs[:, x // 4, x % 4, :]
                        fn(row, row, ACT.Exp, accum_out=rsum[:, x:x + 1]).then_inc(AD.s("probs"), 1)

                    for x in range(4):
                        sparse_exp(x)
                    for kind, x, j in AD.steps:
                        if kind == "T":
                            AD.take_hi(act, x, j)
                            if x == 0 and j % 2 == 1:
                                sparse_exp(4 + j // 2)
                    context("D")
                    act.wait_ge(sem("x_turned"), 5)
                    copy(fm[0:D, :], S[0][0:D, :]).then_inc(sem("E_fm"), 1)
                    copy(x_stack[0:D, :], S[0][0:D, :]).then_inc(sem("E_fm"), 1)
                    act.wait_ge(sem("E_shifted"), 1)
                    fn(gl[:, 1], gl[:, 1], ACT.Exp).then_inc(sem("E_exp"), 1)
                    for n in range(2 * NG + 1):
                        if n < 2 * NG:
                            act.wait_ge(sem("E_up"), n + 1)
                            if n >= 3:
                                act.wait_ge(sem("E_hidden"), n - 2)
                            fn(activated[:, n % 3, :], S[n // 2 % 2][:, half(n % 2)], ACT.Gelu, bias=b1e[:, n % NG:n % NG + 1])\
                                .then_inc(sem("E_activated"), 1)
                        if n == 0:
                            act.wait_ge(sem("E_gates_turned"), 1)
                            for j in range(2):
                                copy(fm2[0:E, half(j)], C[j][0:E, :]).then_inc(sem("E_gates_copied"), 1)
                            gates_hi("E")
                        else:
                            hidden_hi("E", n - 1)
                    experts_sum("E", NG)

                @block.vector
                def _(dve):
                    v = nc.vector
                    own, n_own = sem("dve_own"), [0]

                    def step(ins):
                        ins.then_inc(own, 1)
                        n_own[0] += 1
                        dve.wait_ge(own, n_own[0])

                    def before_step(ins):
                        ins.then_inc(own, 1)
                        n_own[0] += 1

                    n_powers = [0]

                    def power(base):
                        base.then_inc(sem("power_base"), 1)
                        n_powers[0] += 1
                        dve.wait_ge(sem("powered"), n_powers[0])

                    def squares_of(x):
                        step(v.tensor_tensor(sq[:], x, x, ALU.mult))
                        step(v.tensor_reduce(total, sq[:], X, ALU.add))

                    def center(x):
                        step(v.tensor_reduce(shift, x, X, ALU.add))
                        step(v.tensor_scalar(shift, shift, -1.0 / D, None, ALU.mult))
                        step(v.tensor_tensor(xc[:], x, over_features(shift), ALU.add))
                        squares_of(xc[:])

                    def root_base(k, epsilon, scale=1.0):
                        return v.tensor_scalar(bases[:, k], total, scale / D, epsilon, ALU.mult, ALU.add)

                    def scaled(dst, src, by):
                        return v.tensor_tensor(dst, src, over_features(by), ALU.mult)

                    def row_max(att, n, width):
                        v.tensor_reduce(nmax[:, n:n + 1], att.bank("S", n, 0)[:, 0:width], X, ALU.max, negate=True)\
                            .then_inc(att.s("max"), 1)

                    def normalise(x):
                        att = {"B": AB, "C": AC, "D": AD}[x]
                        dve.wait_ge(att.s("probs"), 4 * att.groups)
                        n = 4 * att.groups
                        step(v.reciprocal(rsum[:, 0:n], rsum[:, 0:n]))
                        if x != "D":
                            by_chunk = rsum[:].rearrange("p (h i o) -> p i h o", h=H, o=1)
                            v.tensor_copy(work[:, 0:HALF].rearrange("p (i h d) -> p i h d", i=NC, h=H),
                                          by_chunk.to_broadcast([P, NC, H, DH])).then_inc(sem(f"{x}_recip"), 1)
                        for j in range(2):
                            dve.wait_ge(sem(f"{x}_ctx_copied"), j + 1)
                            both = v.tensor_tensor(context_sum[:, half(j)], C[j][0:D, :], context_sum[:, half(j)],
                                                   ALU.add)
                            if x == "D":
                                both.then_inc(sem("D_context"), 1)
                            else:
                                step(both)
                                dve.wait_ge(sem(f"{x}_spread"), 1)
                                v.tensor_tensor(fm2[0:D, half(j)], context_sum[:, half(j)], S[0][0:D, half(j)],
                                                ALU.mult)\
                                    .then_inc(sem(f"{x}_context"), 1)

                    def values_lo(x, width, group):
                        dve.wait_ge(sem(f"{x}_v_hi"), 4)
                        for hh in range(H):
                            src = C[0][:, 0:NC * width].rearrange("p (c d) -> p c d", d=width)
                            g = group(hh)
                            v.tensor_tensor(v_pad[:, :, hh, D + hh * DH:D + (hh + 1) * DH],
                                            src[:, :, g * DH:(g + 1) * DH],
                                            f(v_pad[:, :, hh, hh * DH:(hh + 1) * DH]), ALU.subtract)\
                                .then_inc(sem(f"{x}_v_lo"), 1)

                    def e_bcast(ap):
                        return ap.rearrange("p (c o) -> p c o", o=1).to_broadcast([P, NC, E])

                    def top_two(score, one, other, mask):
                        rank = first_key[:].rearrange("p (o e) -> p o e", o=1).to_broadcast([P, NC, E])
                        for dst, src in ((mask, score), (one, other)):
                            step(v.tensor_reduce(gs[:, 1], src, X, ALU.max))
                            step(v.tensor_tensor(dst, src, e_bcast(gs[:, 1]), ALU.is_equal))
                            step(v.tensor_tensor(dst, dst, rank, ALU.mult))
                            step(v.tensor_reduce(gs[:, 1], dst, X, ALU.max))
                            step(v.tensor_tensor(dst, dst, e_bcast(gs[:, 1]), ALU.is_equal))
                            if src is score:
                                step(v.tensor_copy(other, score))
                                step(v.copy_predicated(other, mask.bitcast(U32), lowest[:]))
                        step(v.tensor_tensor(mask, mask, one, ALU.add))

                    def x_lo(name):
                        dve.wait_ge(sem(f"{name}_fm"), 2)
                        v.tensor_tensor(x_stack[D:P, :], fm[0:D, :], f(x_stack[0:D, :]), ALU.subtract)\
                            .then_inc(sem(f"{name}_x_lo"), 1)

                    def gates_lo(name):
                        for j in range(2):
                            dve.wait_ge(sem(f"{name}_gates_hi"), j + 1)
                            v.tensor_tensor(gate_stack[D // 2:D // 2 + E, half(j)], C[j][0:E, :],
                                            f(gate_stack[0:E, half(j)]), ALU.subtract).then_inc(sem(f"{name}_gates_lo"), 1)

                    def hidden_free(name, n):
                        if n >= 3:
                            dve.wait_ge(sem(f"{name}_lo"), n - 2)

                    def experts_sum(name):
                        for j in range(2):
                            dve.wait_ge(sem(f"{name}_sum_copied"), j + 1)
                            v.tensor_tensor(context_sum[:, half(j)], C[j][0:D, :], context_sum[:, half(j)], ALU.add)\
                                .then_inc(sem(f"{name}_summed"), 1)
                        dve.wait_ge(sem(f"{name}_by_token"), 1)
                        return v.tensor_tensor(toks(h[:]), toks(h[:]), S[0][:, 0:HALF], ALU.add)

                    dve.wait_ge(sem("A_q_hi"), 1)
                    v.tensor_tensor(a_q_lo, S[0][:], f(a_q_hi), ALU.subtract).then_inc(sem("A_split"), 1)
                    dve.wait_ge(sem("A_k_hi"), 1)
                    v.scalar_tensor_tensor(a_keys, f(a_k_hi), parts[:, 0:1], S[1][:], ALU.mult, ALU.add)\
                        .then_inc(sem("A_split"), 1)
                    dve.wait_ge(sem("first_gate"), 32)
                    for s in range(NC):
                        dve.wait_ge(sem("A_scores"), s + 1)
                        if s >= 2:
                            dve.wait_ge(sem("A_products"), s - 1)
                        v.tensor_tensor(probs[:, 0, s % 2, :], S[s % 2][:], gate[s], ALU.mult)\
                            .then_inc(sem("A_gated"), 1)
                    dve.wait_ge(sem("A_out"), 1)
                    y = R[1][:]
                    step(v.tensor_scalar(toks(sq[:]), y, 0.0, prelu[:, 0:1], ALU.min, ALU.mult))
                    dve.wait_ge(sem("stored"), 16 * seq + 16)
                    step(v.scalar_tensor_tensor(toks(h[:]), y, 0.0, toks(sq[:]), ALU.max, ALU.add))
                    center(h[:])
                    power(root_base(0, 1e-5 * 1e-5, 1.0 + 1e-5))
                    scaled(xn[:], xc[:], roots[:, 0]).then_inc(sem("normalised"), 1)

                    dve.wait_ge(sem("B_fm"), 1)
                    x_hi = v.tensor_copy(b_stack[0:D, :], fm[0:D, :])
                    x_hi.then_inc(sem("B_fm"), 1)
                    dve.wait_ge(sem("B_fm"), 3)
                    v.tensor_tensor(b_stack[D:P, :], fm[0:D, :], f(b_stack[0:D, :]), ALU.subtract)\
                        .then_inc(sem("B_fm"), 1)

                    def prepare_b(hh, k):
                        b, bank, done = hh % 2, AB.bank("P", hh, k), sem("B_prep_dve")
                        dve.wait_ge(sem("B_prep"), PREP * hh + k + 1)
                        if k < 2:
                            if hh + k == 0:
                                dve.wait_ge(sem("rot_loaded"), 32)
                            if hh and k == 0:
                                dve.wait_ge(sem("B_prep_turn"), 2 * hh - 1)
                            v.tensor_tensor(cosb[:, k, :], bank[:], (turn_cos, turn_sin)[k][:], ALU.mult).then_inc(done, 1)
                            if hh == 0 and k == 1:
                                dve.wait_ge(done, 2)
                                v.tensor_tensor(work[:], cosb[:, 0, :], cosb[:, 1, :], ALU.add)\
                                    .then_inc(sem("B_prep_turn"), 1)
                        else:
                            dve.wait_ge(sem("B_prep_act"), 3 * hh + 3 if hh else 1)
                            v.scalar_tensor_tensor(q2[D:P, b, :], f(content_hi(hh)[0:D, :]), parts[0:D, 1:2], bank[0:D, :],
                                                   ALU.mult, ALU.add).then_inc(done, 1)
                            v.scalar_tensor_tensor(k2[D:P, b, :], f(content_hi(hh)[D:P, :]), parts[D:P, 2:3], bank[D:P, :],
                                                   ALU.mult, ALU.add).then_inc(done, 1)

                            if hh == 0:
                                dve.wait_ge(sem("B_prep_act"), 3)
                                v.tensor_tensor(q1[D:P, 0, 0:T], work[D:P, :], f(rounded_wide[D:P, :]), ALU.subtract)\
                                    .then_inc(sem("B_prep_turn"), 1)

                    content_due = []
                    for kind, x, j in AB.steps:
                        if kind == "P":
                            if x and j == 2:
                                content_due.append(x)
                            else:
                                prepare_b(x, j)
                        elif kind == "V":
                            values_lo("B", D, lambda hh: hh)
                        elif kind == "F":
                            i, k, bank = x % NC, AB.slot[("F", x, 0)], AB.bank("S", x, 0)
                            w = min(P + 1, T - i * P)
                            dve.wait_ge(AB.s("scores"), x + 1)
                            v.copy_predicated(bank[:, i * P:i * P + w], late_mask[:, 0:w], R[k % 2][:, 0:w])\
                                .then_inc(AB.s("fixed"), 1)
                            dve.wait_ge(AB.s("fixed"), 2 * x + 1)
                            v.copy_predicated(bank[:, i * P:i * P + w], next_mask[:, 0:w],
                                              R[k % 2][:, 256:256 + w]).then_inc(AB.s("fixed"), 1)
                            dve.wait_ge(AB.s("fixed"), 2 * x + 2)
                            row_max(AB, x, T)
                            if content_due:
                                prepare_b(content_due.pop(), 2)
                        elif kind == "T":
                            AB.take_lo(dve, x, j)
                    normalise("B")
                    dve.wait_ge(sem("B_out"), 1)
                    step(v.tensor_tensor(toks(h[:]), R[0][:], toks(h[:]), ALU.add))
                    center(h[:])
                    step(root_base(0, 1e-5))
                    power(root_base(1, 1e-6 * 1e-5, 1.0 + 1e-6))
                    scaled(xn[:], xc[:], roots[:, 1]).then_inc(sem("normalised"), 1)
                    step(scaled(f_tok[:], xc[:], roots[:, 0]))
                    a, b = cosb[:, 0, :], cosb[:, 1, :]
                    rope, n_rope = sem("C_rope"), [0]

                    def rope_step(ins):
                        ins.then_inc(rope, 1)
                        n_rope[0] += 1

                    dve.wait_ge(sem("C_fm"), 1)
                    rope_step(v.scalar_tensor_tensor(x_stack[D:P, :], S[0][0:D, :], affine[:, 2:3], f(x_stack[0:D, :]),
                                                     ALU.mult, ALU.subtract))
                    dve.wait_ge(sem("rope_loaded"), 32)

                    def split_c(n, k):
                        dve.wait_ge(sem("C_rounded"), n + 1)
                        rope_step(v.scalar_tensor_tensor(c_stack[k], f(stack_a[:, k * T:(k + 1) * T]),
                                                         parts[:, 2:3] if k == 2 else parts[:, 1:2], work[:], ALU.mult, ALU.add))

                    order = (1, 0, 2)
                    for n, k in enumerate(order):
                        for x, (dst, table) in enumerate(((a, turn_cos), (b, turn_sin))):
                            dve.wait_ge(sem("C_proj"), 2 * n + x + 1)
                            if n and x == 0:
                                dve.wait_ge(rope, n_rope[0])
                            if k == 1:
                                for j in range(2):
                                    rope_step(v.tensor_tensor(dst[:, half(j)], (R, C)[x][j][:], table[:, half(j)], ALU.mult))
                            else:
                                rope_step(v.tensor_tensor(dst, S[x][:], table[:], ALU.mult))
                        if n:
                            split_c(n - 1, order[n - 1])
                        dve.wait_ge(rope, n_rope[0])
                        rope_step(v.tensor_tensor(work[:], a, b, ALU.add))
                    split_c(2, 2)
                    values_lo("C", 2 * DH, lambda hh: hh // 2)
                    for kind, x, j in AC.steps:
                        if kind == "S":
                            dve.wait_ge(AC.s("scores"), x + 1)
                            row_max(AC, x, (x % NC + 1) * P)
                        elif kind == "T":
                            AC.take_lo(dve, x, j)
                    normalise("C")
                    dve.wait_ge(sem("C_out"), 1)
                    step(v.tensor_tensor(toks(f_tok[:]), R[0][:], toks(f_tok[:]), ALU.add))
                    squares_of(f_tok[:])
                    power(root_base(0, 1e-6))
                    scaled(xn[:], f_tok[:], roots[:, 0]).then_inc(sem("normalised"), 1)
                    x_lo("M")
                    dve.wait_ge(sem("M_logits"), 1)
                    v.tensor_copy(gl[:, 0], R[0][:, 0:NC * E].rearrange("p (c e) -> p c e", e=E))\
                        .then_inc(sem("M_logits_read"), 1)
                    dve.wait_ge(sem("M_logits_read"), 1)
                    step(v.tensor_reduce(gs[:, 0], gl[:, 0], X, ALU.max))
                    v.tensor_tensor(gl[:, 1], gl[:, 0], e_bcast(gs[:, 0]), ALU.subtract).then_inc(sem("M_shifted"), 1)
                    dve.wait_ge(sem("M_exp"), 1)
                    step(v.tensor_reduce(gs[:, 0], gl[:, 1], X, ALU.add))
                    step(v.reciprocal(gs[:, 0], gs[:, 0]))
                    step(v.tensor_tensor(gl[:, 0], gl[:, 1], e_bcast(gs[:, 0]), ALU.mult))
                    top_two(gl[:, 0], gl[:, 2], gl[:, 3], gl[:, 4])
                    step(v.tensor_tensor(gates[:], gl[:, 0], gl[:, 4], ALU.mult))
                    step(v.tensor_reduce(gs[:, 0], gates[:], X, ALU.add))
                    step(v.tensor_scalar(gs[:, 0], gs[:, 0], 1e-9, None, ALU.add))
                    step(v.reciprocal(gs[:, 0], gs[:, 0]))
                    v.tensor_tensor(gates[:], gates[:], e_bcast(gs[:, 0]), ALU.mult).then_inc(sem("M_gates"), 1)
                    gates_lo("M")
                    for n in range(2 * NQ):
                        dve.wait_ge(sem("M_silu"), n + 1)
                        dve.wait_ge(sem("M_spread_gate"), n + 1)
                        if n >= 3:
                            dve.wait_ge(sem("M_hidden"), n - 2)
                        v.tensor_tensor(gated[:, n % 3, :], activated[:, n % 3, :], R[n % 2][:], ALU.mult)\
                            .then_inc(sem("M_gated"), 1)
                        dve.wait_ge(sem("M_gated"), n + 1)
                        dve.wait_ge(sem("M_up"), n + 1)
                        hidden_free("M", n)
                        v.tensor_tensor(hidden[:, n % 3, :], gated[:, n % 3, :], S[n % 2][:, half(1)], ALU.mult)\
                            .then_inc(sem("M_hidden"), 1)
                    step(v.tensor_tensor(h[:], h[:], f_tok[:], ALU.add))
                    step(experts_sum("M"))
                    center(h[:])
                    step(root_base(0, 1e-5))
                    step(v.reciprocal(bases[:, 1], bases[:, 0]))
                    power(v.tensor_tensor(bases[:, 1], bases[:, 1], total, ALU.mult))
                    scaled(f_tok[:], xc[:], roots[:, 0]).then_inc(sem("normalised"), 1)
                    step(v.tensor_scalar(unit, roots[:, 1], 1e-12, None, ALU.max))
                    step(v.reciprocal(unit, unit))
                    step(v.tensor_tensor(unit, unit, roots[:, 0], ALU.mult))
                    twice = work[:].rearrange("p (c r d) -> p c r d", c=NC, r=2)
                    for r in range(2):
                        scaled(twice[:, :, r, :], xc[:], unit).then_inc(sem("D_unit_x"), 1)
                    dve.wait_ge(sem("D_v_hi"), 1)
                    v.tensor_tensor(v_d[:, :, D:P], R[0][:].rearrange("p (c d) -> p c d", d=D), f(v_d[:, :, 0:D]),
                                    ALU.subtract).then_inc(sem("D_v_lo"), 1)
                    dve.wait_ge(sem("D_unit_hi"), 1)
                    v.tensor_tensor(d_lo, S[0][:], f(d_hi), ALU.subtract).then_inc(sem("D_unit_split"), 1)
                    v.scalar_tensor_tensor(d_stack, f(d_hi), parts[:, 0:1], S[0][:], ALU.mult, ALU.add)\
                        .then_inc(sem("D_unit_split"), 1)
                    for n in range(NC):
                        dve.wait_ge(AD.s("scores_used"), n + 1)
                        row = probs[:, n // 4, n % 4, :]
                        if n >= 2 * SPLIT:
                            dve.wait_ge(sem("D_squared"), n - 2 * SPLIT + 1)
                        v.scalar_tensor_tensor(unread[:, n % (2 * SPLIT), :], row, 1.0, row, ALU.mult, ALU.mult,
                                               accum_out=squares[:, n:n + 1]).then_inc(sem("D_squared"), 1)
                        if n < BY_VECTOR:
                            before_step(v.tensor_copy(halved[n], row))
                    dve.wait_ge(sem("D_squared"), NC)
                    step(v.tensor_scalar(low, sums, 1.0 / T, None, ALU.mult))
                    step(v.tensor_tensor(above, low, low, ALU.mult))
                    step(v.scalar_tensor_tensor(above, squares, 1.0 / T, above, ALU.mult, ALU.subtract))
                    power(v.tensor_scalar(bases[:, 0], above, 1e-12, None, ALU.max))
                    deviation = roots[:, 0]
                    v.tensor_scalar(most, deviation, 3.0 * SLOPE, None, ALU.mult)
                    v.tensor_scalar(least, deviation, 0.3 * SLOPE, None, ALU.mult)
                    v.scalar_tensor_tensor(high, deviation, 4.0, low, ALU.mult, ALU.add)
                    step(v.scalar_tensor_tensor(threshold[0], deviation, FIRST_CUT, low, ALU.mult, ALU.add))
                    for k in range(COUNTS):
                        now, before, of_now, of_before = (x[i] for x in (threshold, inverse) for i in (k % 2, (k + 1) % 2))
                        step(v.tensor_scalar(now, now, 1e-3, None, ALU.max))
                        v.tensor_scalar(now.bitcast(I32), now.bitcast(I32), 1, None, ALU.bitwise_or)\
                            .then_inc(sem("D_threshold"), 1)
                        dve.wait_ge(sem("D_threshold"), k + 1)
                        for n in range(BY_VECTOR):
                            if n >= 3:
                                dve.wait_ge(sem("D_counted"), BY_VECTOR * k + n - 2)
                            v.tensor_scalar(unread[:, n % 3, :], halved[n], now[:, n:n + 1], None, ALU.is_ge, ALU.add,
                                            accum_out=count[:, n:n + 1]).then_inc(sem("D_counted"), 1)
                        dve.wait_ge(sem("D_counted"), BY_VECTOR * (k + 1))
                        dve.wait_ge(sem("D_signs"), (NC - BY_VECTOR) * (k + 1))
                        v.tensor_scalar(seen[:, 0:BY_VECTOR], count[:, 0:BY_VECTOR], float(WANTED), None, ALU.add)
                        step(v.tensor_scalar(seen[:, BY_VECTOR:NC], count[:, BY_VECTOR:NC], -0.5, T / 2.0 + WANTED, ALU.mult, ALU.add))
                        step(v.tensor_scalar(above, seen, 2.0 * WANTED + SLACK + 0.5, None, ALU.is_gt))
                        step(v.scalar_tensor_tensor(missed, seen, 2.0 * WANTED - SLACK - 0.5, above, ALU.is_lt, ALU.add))
                        if k == COUNTS - 1:
                            break
                        v.scalar_tensor_tensor(above, seen, 2.0 * WANTED, missed, ALU.is_gt, ALU.mult)
                        v.scalar_tensor_tensor(edge_high, seen, 2.0 * WANTED, missed, ALU.is_le, ALU.mult)
                        step(v.reciprocal(of_now, seen))
                        v.copy_predicated(low, above.bitcast(U32), now)
                        step(v.copy_predicated(high, edge_high.bitcast(U32), now))
                        if k == 0:
                            step(v.tensor_scalar(slope, deviation, SLOPE, None, ALU.mult))
                        else:
                            v.tensor_tensor(slope, now, before, ALU.subtract)
                            step(v.scalar_tensor_tensor(above, of_now, 1e-7, of_before, ALU.add, ALU.subtract))
                            step(v.reciprocal(above, above))
                            step(v.tensor_tensor(slope, slope, above, ALU.mult))
                            step(v.tensor_tensor(slope, slope, most, ALU.min))
                            step(v.tensor_tensor(slope, slope, least, ALU.max))
                        step(v.scalar_tensor_tensor(slope, of_now, -1.0 / (2 * WANTED), slope, ALU.add, ALU.mult))
                        step(v.tensor_tensor(slope, now, slope, ALU.subtract))
                        if k >= 2:
                            step(v.tensor_tensor(above, high, low, ALU.subtract))
                            v.scalar_tensor_tensor(edge_low, above, 0.25, low, ALU.mult, ALU.add)
                            step(v.scalar_tensor_tensor(edge_high, above, 0.75, low, ALU.mult, ALU.add))
                            step(v.tensor_tensor(slope, slope, edge_low, ALU.max))
                            step(v.tensor_tensor(slope, slope, edge_high, ALU.min))
                        step(v.tensor_copy(before, now))
                        step(v.copy_predicated(before, missed.bitcast(U32), slope))
                    for i, n in enumerate(TOP_ORDER):
                        if n < BY_VECTOR:
                            where = below[n % 2]
                            if n >= 2:
                                dve.wait_ge(sem("D_top"), TOP_ORDER.index(n - 2) + 1)
                            v.scalar_tensor_tensor(where, halved[n], now[:, n:n + 1], probs[:, n // 4, n % 4, :],
                                                   ALU.is_lt, ALU.mult).then_inc(sem("D_masked"), 1)
                            dve.wait_ge(sem("D_masked"), n + 1)
                        else:
                            where = spare[:]
                            dve.wait_ge(sem("D_below"), n - BY_VECTOR + 1)
                        v.max(top8[:, n, :], where).then_inc(sem("D_top"), 1)
                    step(v.tensor_scalar(missed, missed, 0.0, None, ALU.is_equal))
                    v.tensor_scalar(edge_low, seen, 9.0 - TOPK - WANTED, None, ALU.add)
                    step(v.tensor_scalar(edge_high, seen, 8.0 - TOPK - WANTED, None, ALU.add))
                    dve.wait_ge(sem("D_top"), NC)
                    rank = first_key[:].rearrange("p (o e) -> p o e", o=1).to_broadcast([P, NC, E])
                    for dst, key, spot in ((chosen, edge_low, gl[:, 0]), (beyond, edge_high, gl[:, 1])):
                        step(v.tensor_tensor(spot, rank, e_bcast(key), ALU.is_equal))
                        step(v.tensor_tensor(spot, spot, top8[:], ALU.mult))
                        step(v.tensor_reduce(dst, spot, X, ALU.add))
                    step(v.tensor_scalar(beyond, beyond, 0.0, None, ALU.max))
                    step(v.tensor_tensor(beyond, chosen, beyond, ALU.is_gt))
                    step(v.tensor_tensor(beyond, beyond, missed, ALU.mult))
                    v.tensor_reduce(all_rows, beyond, X, ALU.min).then_inc(sem("D_ok"), 1)
                    dve.wait_ge(sem("D_all_ok"), 1)
                    step(v.tensor_scalar(repeat[:], S[0][0:1, 0:1], P / 2 - 0.5, None, ALU.is_lt))
                    def only_chosen(n):
                        src = probs[:, n // 4, n % 4, :]
                        v.scalar_tensor_tensor(src, src, chosen[:, n:n + 1], src, ALU.is_ge, ALU.mult)\
                            .then_inc(AD.s("sparse"), 1)

                    with dve.If(dve.value_load(repeat[0:1, 0:1]) != 0):
                        taken = sem("D_taken")
                        for n in range(NC):
                            src = probs[:, n // 4, n % 4, :]
                            for k in range(TOPK // 8):
                                at = 2 * (TOPK // 8 * n + k) + max(0, n - SPARSE_FIRST)
                                v.max(top8[:, 0, :], src if k == 0 else work[:]).then_inc(taken, 1)
                                dve.wait_ge(taken, at + 1)
                                v.match_replace(work[:], top8[:, 0, :], src if k == 0 else work[:], TAKEN)\
                                    .then_inc(taken, 1)
                                dve.wait_ge(taken, at + 2)
                            v.scalar_tensor_tensor(src, work[:], TAKEN, src, ALU.is_equal, ALU.mult)\
                                .then_inc(AD.s("sparse") if n < SPARSE_FIRST else taken, 1)
                            if n < SPARSE_FIRST:
                                dve.wait_ge(AD.s("sparse"), n + 1)
                            else:
                                dve.wait_ge(taken, at + 3)
                        v.memset(chosen, 2 * TAKEN).then_inc(taken, 1)
                        dve.wait_ge(taken, at + 4)
                    with dve.Else():
                        for n in range(SPARSE_FIRST):
                            only_chosen(n)
                    for kind, x, j in AD.steps:
                        if kind == "T":
                            if x == 0 and j % 2 == 0 and j // 2 + SPARSE_FIRST - 1 in range(SPARSE_FIRST, NC):
                                only_chosen(j // 2 + SPARSE_FIRST - 1)
                            AD.take_lo(dve, x, j)
                    normalise("D")
                    dve.wait_ge(sem("D_by_token"), 1)
                    step(v.tensor_tensor(sq[:], S[0][:, 0:HALF].rearrange("p (c d) -> p c d", d=D),
                                         over_features(rsum[:, 0:NC]), ALU.mult))
                    step(v.tensor_tensor(h[:], h[:], sq[:], ALU.add))
                    center(h[:])
                    power(root_base(0, 1e-5))
                    scaled(f_tok[:], xc[:], roots[:, 0]).then_inc(sem("normalised"), 1)
                    x_lo("E")
                    dve.wait_ge(sem("E_logits"), 1)
                    v.tensor_copy(gl[:, 0], R[0][:, 0:NC * E].rearrange("p (c e) -> p c e", e=E))\
                        .then_inc(sem("E_logits_read"), 1)
                    dve.wait_ge(sem("E_logits_read"), 1)
                    step(v.tensor_reduce(gs[:, 0], gl[:, 0], X, ALU.max))
                    v.tensor_tensor(gl[:, 1], gl[:, 0], e_bcast(gs[:, 0]), ALU.subtract).then_inc(sem("E_shifted"), 1)
                    top_two(gl[:, 0], gl[:, 2], gl[:, 3], gl[:, 4])
                    dve.wait_ge(sem("E_exp"), 1)
                    step(v.tensor_tensor(gates[:], gl[:, 1], gl[:, 4], ALU.mult))
                    step(v.tensor_reduce(gs[:, 0], gates[:], X, ALU.add))
                    step(v.reciprocal(gs[:, 0], gs[:, 0]))
                    v.tensor_tensor(gates[:], gates[:], e_bcast(gs[:, 0]), ALU.mult).then_inc(sem("E_gates"), 1)
                    gates_lo("E")
                    for n in range(2 * NG):
                        dve.wait_ge(sem("E_activated"), n + 1)
                        dve.wait_ge(sem("E_spread_gate"), n // 2 + 1)
                        hidden_free("E", n)
                        v.tensor_tensor(hidden[:, n % 3, :], activated[:, n % 3, :], R[n // 2 % 2][:], ALU.mult)\
                            .then_inc(sem("E_hidden"), 1)
                    experts_sum("E").then_inc(sem("result"), 1)

            numbers = sorted(sems[name].num for name in sems if name not in lasting)
            first = 0
            for i in range(1, len(numbers) + 1):
                if i == len(numbers) or numbers[i] != numbers[i - 1] + 1:
                    nc.gpsimd.sem_clear(range(numbers[first], numbers[i - 1] + 1))
                    first = i
            nc.all_engine_barrier()

        with nc.Block() as block:
            @block.sync
            def _(sp):
                sp.wait_ge(sem("stored"), 16 * (B + 1))


def tables():
    div = np.exp(np.arange(0, D, 2, dtype=np.float32) * np.float32(-np.log(10000.0) / D)).astype(np.float64)
    pos = np.arange(T, dtype=np.float64)
    angle = div[:, None] * pos
    pe_early, pe_late = (np.concatenate([np.sin(a), np.cos(a)]) for a in (angle, div[:, None] * (pos - T)))
    turn = div[:, None] * (T - 1 - pos)
    rot_cos = np.concatenate([np.cos(turn)] * 4)
    rot_sin = np.concatenate([-np.sin(turn), np.sin(turn)] * 2)
    inv = 1.0 / 10000.0 ** (np.arange(0, DH, 2, dtype=np.float32) / DH)
    freqs = np.outer(np.arange(T, dtype=np.float32), inv)
    c, s = np.cos(freqs).T, np.sin(freqs).T
    rope_cos, rope_sin = np.concatenate([c, c] * 2 * DUP), np.concatenate([-s, s] * 2 * DUP)
    i, j = np.arange(P)[:, None], np.arange(P + 1)
    bf16 = mybir.dt.np(BF16)
    rows, of = np.arange(D)[:, None, None], np.arange(NQ)[None, :, None]
    expert = np.where(of < E, of, 2 * (of - E) + np.arange(P)[None, None, :] // D)
    gate_rows = (rows % (D // 2) == expert).reshape(D, NQ * P)
    copy = np.arange(P) % D // DH
    parts = -np.stack([np.arange(P) >= D, copy % 2 == 1, copy >= 2, np.arange(P) != D], axis=1).astype(np.float32)
    f32 = lambda a: np.ascontiguousarray(a, dtype=np.float32)
    return {"positions": f32(np.tile(np.concatenate([pe_early, pe_late], 1), (2, 1))),
            "rot_cos": f32(rot_cos), "rot_sin": f32(rot_sin), "rope_cos": f32(rope_cos), "rope_sin": f32(rope_sin),
            "masks": np.concatenate([j >= i + 2, j == i + 1], 1).astype(np.int32),
            "future": np.where(j[:P] > i, -1e30, 0.0).astype(bf16), "parts": f32(parts), "gate_rows": f32(gate_rows)}


def laid_out(inp):
    a = {k: np.asarray(v) for k, v in inp.items()}
    tab = tables()
    tok = {n: a["L0_tok_" + n] for n in ("Wq", "bq", "Wk", "bk", "Wv", "bv", "Wo", "bo")}
    att = {n: a["L0_attn_" + n] for n in ("ln_gamma", "ln_beta", "Wq", "bq", "Wk", "bk", "Wv", "bv", "Wpos", "u_bias",
                                          "v_bias", "Wout", "bout")}
    ffn = {n: a["L0_ffn_" + n] for n in ("ln1_w", "ln2_w", "wq", "wk", "wv", "wo", "router_w", "w1", "w2", "w3")}
    gelu = {n: a["L1_ffn_" + n] for n in ("Wg", "bg", "W1", "b1", "W2", "b2")}
    none = lambda *shape: np.zeros(shape, np.float32)

    def below(w, b=None):
        return np.concatenate([w, none(1, w.shape[1]) if b is None else b.reshape(1, -1)])

    x = a["x"].reshape(B, T, D).transpose(0, 2, 1)
    r = {"xT": np.concatenate([x, x[-1:]]), "gateT": a["L0_tok_d_gamma_batched"].T, "b2": gelu["b2"]}
    packed = {"tok_q": np.tile(below(tok["Wq"], tok["bq"]), (1, 2)), "tok_k": np.tile(below(tok["Wk"], tok["bk"]), (1, 2)),
              "tok_v": below(tok["Wv"], tok["bv"]), "tok_o": below(tok["Wo"], tok["bo"]),
              "v": below(att["Wv"], att["bv"]), "out": below(att["Wout"], att["bout"]),
              "cosine_v": below(a["L1_attn_W"].T, a["L1_attn_b"]), "gelu_gate": below(gelu["Wg"], gelu["bg"]),
              "causal_o": below(ffn["wo"].T), "causal_v": below(ffn["wv"].T), "router": below(ffn["router_w"].T),
              "affine": below(np.stack([att["ln_gamma"], att["ln_beta"], ffn["ln1_w"], ffn["ln2_w"]], 1))}
    r["projections"] = np.concatenate([packed[n] for n, _ in PROJECTIONS], 1)
    packed = {"identity": np.eye(P, dtype=np.float32), "parts": tab.pop("parts"),
              "prelu": np.tile(a["L0_tok_prelu_a"].reshape(1, 1), (P, 1)), "b1": gelu["b1"].reshape(NG, P).T}
    r["columns"] = np.concatenate([packed[n] for n, _ in COLUMNS], 1)
    def twice(arrays, axis):
        whole = np.concatenate(arrays, axis)
        return np.concatenate([whole, whole[D:D + 1]])

    r["attention_64"] = twice([below(none(D, D), att["u_bias"]), below(att["Wq"], att["bq"]),
                       below(att["Wk"], att["bk"]), below(ffn["wq"].T), below(ffn["wk"].T)], 1)
    heads = att["Wq"].T.reshape(H, DH, D)
    with_bias = np.concatenate([heads] + 2 * [att["bq"].reshape(H, DH, 1)], 2).transpose(1, 0, 2).reshape(DH, -1)
    sine, cosine = (att["Wpos"][k::2].T.reshape(H, DH, D // 2) for k in range(2))
    pos = np.concatenate([sine, cosine] * 2 + [sine], 2).transpose(1, 0, 2).reshape(DH, -1)
    r["attention_16"] = np.concatenate([with_bias, att["v_bias"].T, pos], 1)
    ups = []
    for n in ("w1", "w3"):
        w = ffn[n].transpose(2, 0, 1)
        rests = none(D, E // 2, 2, D)
        rests[:, :, :, 0:REST] = w[:, :, P:HID].reshape(D, E // 2, 2, REST)
        ups += [w[:, :, 0:P].reshape(D, E * P), rests.reshape(D, -1)]
    w = ffn["w2"].transpose(2, 0, 1)
    rests = none(2, D, E // 2, D)
    rests[:, 0:REST] = w[P:HID].reshape(REST, E // 2, 2, D).transpose(2, 0, 1, 3)
    down = np.concatenate([w[0:P].reshape(P, -1), rests.reshape(P, -1)], 1)
    gelu_up = gelu["W1"].transpose(1, 0, 2).reshape(D, -1)
    r["experts_up"] = np.concatenate([np.tile(np.concatenate(ups, 1), (2, 1)), down, np.tile(gelu_up, (2, 1))], 1)
    r["experts_down"] = gelu["W2"].reshape(NG, P, D).transpose(1, 0, 2).reshape(P, -1)
    r.update(tab)
    return {n: np.ascontiguousarray(r[n]) for n in INPUTS}


def kernel(**inputs):
    from concourse import bacc, bass_utils

    nc = bacc.Bacc("TRN2", target_bir_lowering=False, num_devices=1)
    arrays, aps = {}, {}
    for name, a in laid_out(inputs).items():
        arrays[f"in_{name}"] = a
        aps[name] = nc.dram_tensor(f"in_{name}", a.shape, mybir.dt.from_np(a.dtype), kind="ExternalInput").ap()
    out = nc.dram_tensor("out", (B, T, D), F32, kind="ExternalOutput").ap()
    build(nc, aps, out)
    r = bass_utils.run_bass_kernel_spmd(nc, [arrays], core_ids=[0])
    return r.results[0]["out"]
```
